# Optimizing a Trainium2 kernel written in Bass

```python
import numpy as np
import jax
import jax.numpy as jnp

def _softmax(x, axis=-1):
    return jax.nn.softmax(x, axis=axis)

def _gelu(x):
    return jax.nn.gelu(x, approximate=True)

def _silu(x):
    return jax.nn.silu(x)

def _sigmoid(x):
    return jax.nn.sigmoid(x)

def _layernorm(x, axis=-1, eps=1e-05):
    m = jnp.mean(x, axis=axis, keepdims=True)
    v = jnp.var(x, axis=axis, keepdims=True)
    return (x - m) / jnp.sqrt(v + eps)

def _scatter_add(tgt, idx, src, axis=0):
    return tgt.at[idx].add(src)

def _segment_sum(src, seg, n):
    return jax.ops.segment_sum(src, seg, n)
kernel_name = 'mk_decoder_preln_d2_seqx_r4_db0a2b'

def setup_inputs(seed: int=0):
    np.random.seed(seed)
    _w = jnp.asarray

    def _rec_inputs():
        import jax
        import jax.numpy as jnp
        _rk = jax.random.key(seed)
        x = 0.0002417 + 0.9998 * jax.random.normal(jax.random.fold_in(_rk, 1), (16, 112, 256), jnp.float32)
        _lenS = 112 - jax.random.randint(jax.random.fold_in(_rk, 7), (16,), 0, max(1, 112 // 4) + 1, jnp.int32)
        _lenS2 = 375 - jax.random.randint(jax.random.fold_in(_rk, 8), (16,), 0, max(1, 375 // 4) + 1, jnp.int32)
        _ctx_1024P = jax.random.normal(jax.random.fold_in(_rk, 11), (16, 16, 256), jnp.float32)
        _ctx_1024c = jax.random.dirichlet(jax.random.fold_in(_rk, 511), 0.3 * jnp.ones((16,), jnp.float32), (16, 375))
        _ctx_1024t = jnp.einsum('bsk,bkd->bsd', _ctx_1024c, _ctx_1024P)
        _ctx_1024t = _ctx_1024t * jax.lax.rsqrt(jnp.mean(jnp.square(_ctx_1024t)) + 1e-12) * 0.953939
        ctx_1024 = 7.22013e-05 + 1.00017 * (_ctx_1024t + 0.3 * jax.random.normal(jax.random.fold_in(_rk, 611), (16, 375, 256), jnp.float32))
        _validS = jnp.arange(112)[None, :] < _lenS[:, None]
        _validS2 = jnp.arange(375)[None, :] < _lenS2[:, None]
        _causal = jnp.tril(jnp.ones((112, 112), dtype=bool))
        mask_Bx1xSxS2_if1 = jnp.where(jnp.ones((16, 1, 112, 375), dtype=bool), 1, 0).astype(jnp.int32)
        mask_Bx1xSxS2_bk0 = jnp.logical_not(jnp.broadcast_to(_validS2[:, None, None, :], (16, 1, 112, 375)))
        return (x, ctx_1024, mask_Bx1xSxS2_if1, mask_Bx1xSxS2_bk0)
    x, ctx_1024, mask_Bx1xSxS2_if1, mask_Bx1xSxS2_bk0 = _rec_inputs()

    def _L0_attn_setup():
        import jax, jax.numpy as jnp
        import numpy as np
        from jax import lax
        B, T, HID = (4, 256, 256)
        H, DK, DV = (8, 128, 128)
        KCONV = 4
        EPS = 1e-06
        KEY_DIM = H * DK
        VAL_DIM = H * DV
        CONV_DIM = 2 * KEY_DIM + VAL_DIM
        key = jax.random.key(seed)
        ks = jax.random.split(key, 11)
        s = 0.02
        return {'hidden_states': jax.random.normal(ks[0], (B, T, HID), jnp.float32), 'qkv_w': jax.random.normal(ks[1], (CONV_DIM, HID), jnp.float32) * s, 'z_w': jax.random.normal(ks[2], (VAL_DIM, HID), jnp.float32) * s, 'b_w': jax.random.normal(ks[3], (H, HID), jnp.float32) * s, 'a_w': jax.random.normal(ks[4], (H, HID), jnp.float32) * s, 'conv_w': jax.random.normal(ks[5], (CONV_DIM, 1, KCONV), jnp.float32) * 0.2, 'dt_bias': jnp.ones((H,), jnp.float32), 'A_log': jnp.log(jax.random.uniform(ks[6], (H,), jnp.float32, 0.001, 16.0)), 'norm_w': jnp.ones((DV,), jnp.float32), 'out_w': jax.random.normal(ks[7], (HID, VAL_DIM), jnp.float32) * s}
    _L0_attn_all = _L0_attn_setup()
    _L0_attn_in = {k: v for k, v in _L0_attn_all.items() if k in ('qkv_w', 'z_w', 'b_w', 'a_w', 'conv_w', 'dt_bias', 'A_log', 'norm_w', 'out_w')}
    del _L0_attn_all

    def _L0_xattn_setup():
        import jax, jax.numpy as jnp
        import numpy as np
        EMBED = 256
        HEADS = 16
        HEAD_DIM = EMBED // HEADS
        key = jax.random.key(seed)
        ks = jax.random.split(key, 9)
        N, L, E = (4, 512, EMBED)
        scale = 1.0 / np.sqrt(E)
        return {'values': jax.random.normal(ks[0], (N, L, E), dtype=jnp.float32), 'keys': jax.random.normal(ks[1], (N, L, E), dtype=jnp.float32), 'query': jax.random.normal(ks[2], (N, L, E), dtype=jnp.float32), 'mask': jnp.ones((N, 1, L, L), dtype=jnp.int32), 'Wv': jax.random.normal(ks[3], (E, E), dtype=jnp.float32) * scale, 'Wk': jax.random.normal(ks[4], (E, E), dtype=jnp.float32) * scale, 'Wq': jax.random.normal(ks[5], (E, E), dtype=jnp.float32) * scale, 'Wo': jax.random.normal(ks[6], (E, E), dtype=jnp.float32) * scale, 'bo': jax.random.normal(ks[7], (E,), dtype=jnp.float32) * scale}
    _L0_xattn_all = _L0_xattn_setup()
    _L0_xattn_in = {k: v for k, v in _L0_xattn_all.items() if k in ('Wv', 'Wk', 'Wq', 'Wo', 'bo')}
    del _L0_xattn_all

    def _L0_ffn_setup():
        import jax, jax.numpy as jnp
        import numpy as np
        B, S, D, O, E, K = (4, 512, 256, 256, 8, 2)
        key = jax.random.key(seed)
        ks = jax.random.split(key, 5)
        scale_in = 1.0 / np.sqrt(D)
        x = jax.random.normal(ks[0], (B, S, D), dtype=jnp.float32)
        gate_w = jax.random.uniform(ks[1], (E, D), jnp.float32, -scale_in, scale_in)
        gate_b = jax.random.uniform(ks[2], (E,), jnp.float32, -scale_in, scale_in)
        expert_w = jax.random.uniform(ks[3], (E, D, O), jnp.float32, -scale_in, scale_in)
        expert_b = jax.random.uniform(ks[4], (E, O), jnp.float32, -scale_in, scale_in)
        return {'x': x, 'gate_w': gate_w, 'gate_b': gate_b, 'expert_w': expert_w, 'expert_b': expert_b}
    _L0_ffn_all = _L0_ffn_setup()
    _L0_ffn_in = {k: v for k, v in _L0_ffn_all.items() if k in ('gate_w', 'gate_b', 'expert_w', 'expert_b')}
    del _L0_ffn_all

    def _L1_attn_setup():
        import jax, jax.numpy as jnp
        import numpy as np
        B, S, D, P = (4, 512, 256, 256)
        key = jax.random.key(seed)
        k1, k2, k3, k4 = jax.random.split(key, 4)
        x = jax.random.normal(k1, (B, S, D), dtype=jnp.float32)
        scale = 1.0 / np.sqrt(D)
        Wq = jax.random.normal(k2, (D, P), dtype=jnp.float32) * scale
        Wk = jax.random.normal(k3, (D, P), dtype=jnp.float32) * scale
        Wv = jax.random.normal(k4, (D, P), dtype=jnp.float32) * scale
        return {'x': x, 'Wq': Wq, 'Wk': Wk, 'Wv': Wv}
    _L1_attn_all = _L1_attn_setup()
    _L1_attn_in = {k: v for k, v in _L1_attn_all.items() if k in ('Wq', 'Wk', 'Wv')}
    del _L1_attn_all

    def _L1_xattn_setup():
        import jax, jax.numpy as jnp
        import numpy as np
        D = 256
        H = 16
        B = 4
        S = 512
        NEG = -1000000000.0
        key = jax.random.key(seed)
        ks = jax.random.split(key, 12)
        s = 0.02
        inp = {'Q': jax.random.normal(ks[0], (B, S, D), jnp.float32), 'K': jax.random.normal(ks[1], (B, S, D), jnp.float32), 'V': jax.random.normal(ks[2], (B, S, D), jnp.float32), 'mask': jnp.broadcast_to(jnp.tril(jnp.ones((S, S), bool)), (B, 1, S, S)), 'Wq': jax.random.normal(ks[3], (D, D), jnp.float32) * s, 'bq': jnp.zeros((D,), jnp.float32), 'Wk': jax.random.normal(ks[4], (D, D), jnp.float32) * s, 'bk': jnp.zeros((D,), jnp.float32), 'Wv': jax.random.normal(ks[5], (D, D), jnp.float32) * s, 'bv': jnp.zeros((D,), jnp.float32), 'Wo': jax.random.normal(ks[6], (D, D), jnp.float32) * s, 'bo': jnp.zeros((D,), jnp.float32)}
        return inp
    _L1_xattn_all = _L1_xattn_setup()
    _L1_xattn_in = {k: v for k, v in _L1_xattn_all.items() if k in ('Wq', 'bq', 'Wk', 'bk', 'Wv', 'bv', 'Wo', 'bo')}
    del _L1_xattn_all

    def _L1_ffn_setup():
        import jax, jax.numpy as jnp
        import numpy as np
        D_IN, D_HID = (256, 1024)

        def _ternary(key, shape):
            return jax.random.randint(key, shape, -1, 2).astype(jnp.float32)

        def _tlin(x, w, s):
            return jnp.einsum('bsi,oi->bso', x, w) * s
        key = jax.random.key(seed)
        ks = jax.random.split(key, 12)
        inv = lambda fan: 1.0 / np.sqrt(fan).astype(np.float32)
        return {'x': jax.random.normal(ks[0], (4, 512, D_IN), dtype=jnp.float32), 'w1_w': _ternary(ks[1], (D_HID, D_IN)), 'w1_s': jax.random.uniform(ks[2], (D_HID,), dtype=jnp.float32) * inv(D_IN), 'w2_w': _ternary(ks[3], (D_HID, D_IN)), 'w2_s': jax.random.uniform(ks[4], (D_HID,), dtype=jnp.float32) * inv(D_IN), 'h1_w': _ternary(ks[5], (D_HID, D_HID)), 'h1_s': jax.random.uniform(ks[6], (D_HID,), dtype=jnp.float32) * inv(D_HID), 'h2_w': _ternary(ks[7], (D_HID, D_HID)), 'h2_s': jax.random.uniform(ks[8], (D_HID,), dtype=jnp.float32) * inv(D_HID), 'w3_w': _ternary(ks[9], (D_IN, D_HID)), 'w3_s': jax.random.uniform(ks[10], (D_IN,), dtype=jnp.float32) * inv(D_HID)}
    _L1_ffn_all = _L1_ffn_setup()
    _L1_ffn_in = {k: v for k, v in _L1_ffn_all.items() if k in ('w1_w', 'w1_s', 'w2_w', 'w2_s', 'h1_w', 'h1_s', 'h2_w', 'h2_s', 'w3_w', 'w3_s')}
    del _L1_ffn_all
    return {'x': x, 'ctx_1024': ctx_1024, 'mask_Bx1xSxS2_if1': mask_Bx1xSxS2_if1, 'mask_Bx1xSxS2_bk0': mask_Bx1xSxS2_bk0, 'L0_attn_qkv_w': _L0_attn_in['qkv_w'], 'L0_attn_z_w': _L0_attn_in['z_w'], 'L0_attn_b_w': _L0_attn_in['b_w'], 'L0_attn_a_w': _L0_attn_in['a_w'], 'L0_attn_conv_w': _L0_attn_in['conv_w'], 'L0_attn_dt_bias': _L0_attn_in['dt_bias'], 'L0_attn_A_log': _L0_attn_in['A_log'], 'L0_attn_norm_w': _L0_attn_in['norm_w'], 'L0_attn_out_w': _L0_attn_in['out_w'], 'L0_xattn_Wv': _L0_xattn_in['Wv'], 'L0_xattn_Wk': _L0_xattn_in['Wk'], 'L0_xattn_Wq': _L0_xattn_in['Wq'], 'L0_xattn_Wo': _L0_xattn_in['Wo'], 'L0_xattn_bo': _L0_xattn_in['bo'], 'L0_ffn_gate_w': _L0_ffn_in['gate_w'], 'L0_ffn_gate_b': _L0_ffn_in['gate_b'], 'L0_ffn_expert_w': _L0_ffn_in['expert_w'], 'L0_ffn_expert_b': _L0_ffn_in['expert_b'], 'L1_attn_Wq': _L1_attn_in['Wq'], 'L1_attn_Wk': _L1_attn_in['Wk'], 'L1_attn_Wv': _L1_attn_in['Wv'], 'L1_xattn_Wq': _L1_xattn_in['Wq'], 'L1_xattn_bq': _L1_xattn_in['bq'], 'L1_xattn_Wk': _L1_xattn_in['Wk'], 'L1_xattn_bk': _L1_xattn_in['bk'], 'L1_xattn_Wv': _L1_xattn_in['Wv'], 'L1_xattn_bv': _L1_xattn_in['bv'], 'L1_xattn_Wo': _L1_xattn_in['Wo'], 'L1_xattn_bo': _L1_xattn_in['bo'], 'L1_ffn_w1_w': _L1_ffn_in['w1_w'], 'L1_ffn_w1_s': _L1_ffn_in['w1_s'], 'L1_ffn_w2_w': _L1_ffn_in['w2_w'], 'L1_ffn_w2_s': _L1_ffn_in['w2_s'], 'L1_ffn_h1_w': _L1_ffn_in['h1_w'], 'L1_ffn_h1_s': _L1_ffn_in['h1_s'], 'L1_ffn_h2_w': _L1_ffn_in['h2_w'], 'L1_ffn_h2_s': _L1_ffn_in['h2_s'], 'L1_ffn_w3_w': _L1_ffn_in['w3_w'], 'L1_ffn_w3_s': _L1_ffn_in['w3_s']}

def reference(x, ctx_1024, mask_Bx1xSxS2_if1, mask_Bx1xSxS2_bk0, L0_attn_qkv_w, L0_attn_z_w, L0_attn_b_w, L0_attn_a_w, L0_attn_conv_w, L0_attn_dt_bias, L0_attn_A_log, L0_attn_norm_w, L0_attn_out_w, L0_xattn_Wv, L0_xattn_Wk, L0_xattn_Wq, L0_xattn_Wo, L0_xattn_bo, L0_ffn_gate_w, L0_ffn_gate_b, L0_ffn_expert_w, L0_ffn_expert_b, L1_attn_Wq, L1_attn_Wk, L1_attn_Wv, L1_xattn_Wq, L1_xattn_bq, L1_xattn_Wk, L1_xattn_bk, L1_xattn_Wv, L1_xattn_bv, L1_xattn_Wo, L1_xattn_bo, L1_ffn_w1_w, L1_ffn_w1_s, L1_ffn_w2_w, L1_ffn_w2_s, L1_ffn_h1_w, L1_ffn_h1_s, L1_ffn_h2_w, L1_ffn_h2_s, L1_ffn_w3_w, L1_ffn_w3_s):
    import jax
    import jax.numpy as jnp

    def _L0_attn_ref(hidden_states, qkv_w, z_w, b_w, a_w, conv_w, dt_bias, A_log, norm_w, out_w):
        import jax, jax.numpy as jnp
        import numpy as np
        from jax import lax
        B, T, HID = (4, 256, 256)
        H, DK, DV = (8, 128, 128)
        KCONV = 4
        EPS = 1e-06
        KEY_DIM = H * DK
        VAL_DIM = H * DV
        CONV_DIM = 2 * KEY_DIM + VAL_DIM
        b_, t_, _ = hidden_states.shape
        mixed = jnp.einsum('bth,ch->btc', hidden_states, qkv_w)
        x = mixed.transpose(0, 2, 1)
        x = lax.conv_general_dilated(x, conv_w, window_strides=(1,), padding=[(KCONV - 1, 0)], feature_group_count=CONV_DIM, dimension_numbers=('NCH', 'OIH', 'NCH'))
        mixed = x.transpose(0, 2, 1)
        z = jnp.einsum('bth,vh->btv', hidden_states, z_w).reshape(b_, t_, H, DV)
        bb = jnp.einsum('bth,nh->btn', hidden_states, b_w)
        aa = jnp.einsum('bth,nh->btn', hidden_states, a_w)
        q, k, v = jnp.split(mixed, 3, axis=-1)
        q = q.reshape(b_, t_, H, DK)
        k = k.reshape(b_, t_, H, DK)
        v = v.reshape(b_, t_, H, DV)
        beta = jax.nn.sigmoid(bb)
        g = -jnp.exp(A_log) * jax.nn.softplus(aa + dt_bias)
        alpha = jnp.exp(g)

        def step(S, inp):
            q_t, k_t, v_t, beta_t, alpha_t = inp
            S = S * alpha_t[..., None, None]
            kv = jnp.einsum('bhk,bhkv->bhv', k_t, S)
            S = S + jnp.einsum('bhk,bhv->bhkv', k_t, (v_t - kv) * beta_t[..., None])
            o_t = jnp.einsum('bhk,bhkv->bhv', q_t, S)
            return (S, o_t)
        qt = q.transpose(1, 0, 2, 3)
        kt = k.transpose(1, 0, 2, 3)
        vt = v.transpose(1, 0, 2, 3)
        bt = beta.transpose(1, 0, 2)
        at = alpha.transpose(1, 0, 2)
        S0 = jnp.zeros((b_, H, DK, DV), hidden_states.dtype)
        _, o = lax.scan(step, S0, (qt, kt, vt, bt, at))
        o = o.transpose(1, 0, 2, 3)
        var = jnp.mean(jnp.square(o), axis=-1, keepdims=True)
        o = o * lax.rsqrt(var + EPS) * norm_w
        o = o * (z * jax.nn.sigmoid(z))
        out = jnp.einsum('btv,hv->bth', o.reshape(b_, t_, VAL_DIM), out_w)
        return out

    def _L0_xattn_ref(values, keys, query, mask, Wv, Wk, Wq, Wo, bo):
        import jax, jax.numpy as jnp
        import numpy as np
        EMBED = 256
        HEADS = 16
        HEAD_DIM = EMBED // HEADS
        N, Lq, E = query.shape
        Lk = keys.shape[1]
        Lv = values.shape[1]
        v = (values @ Wv.T).reshape(N, Lv, HEADS, HEAD_DIM)
        k = (keys @ Wk.T).reshape(N, Lk, HEADS, HEAD_DIM)
        q = (query @ Wq.T).reshape(N, Lq, HEADS, HEAD_DIM)
        energy = jnp.einsum('nqhd,nkhd->nhqk', q, k)
        energy = jnp.where(mask == 0, jnp.float32(-1e+20), energy)
        attention = jax.nn.softmax(energy / jnp.sqrt(jnp.float32(E)), axis=3)
        out = jnp.einsum('nhql,nlhd->nqhd', attention, v).reshape(N, Lq, E)
        return out @ Wo.T + bo

    def _L0_ffn_ref(x, gate_w, gate_b, expert_w, expert_b):
        import jax, jax.numpy as jnp
        import numpy as np
        B, S, D, O, E, K = (4, 512, 256, 256, 8, 2)
        logits = jnp.einsum('bsd,ed->bse', x, gate_w) + gate_b
        if K < E:
            topv, topi = jax.lax.top_k(logits, K)
            keep = jax.nn.one_hot(topi, E, dtype=jnp.float32).sum(axis=-2)
            logits = jnp.where(keep > 0, logits, -jnp.inf)
        gate_score = jax.nn.softmax(logits, axis=-1)
        expert_out = jnp.einsum('bsd,edo->bseo', x, expert_w) + expert_b
        out = jnp.einsum('bseo,bse->bso', expert_out, gate_score)
        return out

    def _L1_attn_ref(x, Wq, Wk, Wv):
        import jax, jax.numpy as jnp
        import numpy as np
        B, S, D, P = (4, 512, 256, 256)
        q = x @ Wq
        k = x @ Wk
        v = x @ Wv
        scores = jnp.einsum('bsd,btd->bst', q, k)
        seq = x.shape[1]
        causal = jnp.triu(jnp.ones((seq, seq), dtype=bool), k=1)
        scores = jnp.where(causal, -jnp.inf, scores)
        scores = scores / jnp.sqrt(jnp.asarray(P, dtype=scores.dtype))
        attn = jax.nn.softmax(scores, axis=-1)
        context = jnp.einsum('bst,btd->bsd', attn, v)
        return context

    def _L1_xattn_ref(Q, K, V, mask, Wq, bq, Wk, bk, Wv, bv, Wo, bo):
        import jax, jax.numpy as jnp
        import numpy as np
        D = 256
        H = 16
        B = 4
        S = 512
        NEG = -1000000000.0
        d = D // H

        def split(x):
            Bx, Sx, _ = x.shape
            return x.reshape(Bx, Sx, H, d).transpose(0, 2, 1, 3)
        q = split(Q @ Wq + bq)
        k = split(K @ Wk + bk)
        v = split(V @ Wv + bv)
        scores = jnp.einsum('bhsd,bhtd->bhst', q, k) / jnp.sqrt(jnp.float32(d))
        scores = jnp.where(mask, scores, NEG)
        attn = jax.nn.softmax(scores, axis=-1)
        out = jnp.einsum('bhst,bhtd->bhsd', attn, v)
        out = out.transpose(0, 2, 1, 3).reshape(Q.shape[0], Q.shape[1], D)
        return out @ Wo + bo

    def _L1_ffn_ref(x, w1_w, w1_s, w2_w, w2_s, h1_w, h1_s, h2_w, h2_s, w3_w, w3_s):
        import jax, jax.numpy as jnp
        import numpy as np
        D_IN, D_HID = (256, 1024)

        def _ternary(key, shape):
            return jax.random.randint(key, shape, -1, 2).astype(jnp.float32)

        def _tlin(x, w, s):
            return jnp.einsum('bsi,oi->bso', x, w) * s
        h = jax.nn.silu(_tlin(x, w1_w, w1_s)) * _tlin(x, w2_w, w2_s)
        h = jax.nn.gelu(_tlin(h, h1_w, h1_s), approximate=False)
        h = jax.nn.gelu(_tlin(h, h2_w, h2_s), approximate=False)
        return _tlin(h, w3_w, w3_s)
    x = x + _L0_attn_ref(_layernorm(x, axis=-1), L0_attn_qkv_w, L0_attn_z_w, L0_attn_b_w, L0_attn_a_w, L0_attn_conv_w, L0_attn_dt_bias, L0_attn_A_log, L0_attn_norm_w, L0_attn_out_w)
    x = x + _L0_xattn_ref(ctx_1024, ctx_1024, _layernorm(x, axis=-1), mask_Bx1xSxS2_if1, L0_xattn_Wv, L0_xattn_Wk, L0_xattn_Wq, L0_xattn_Wo, L0_xattn_bo)
    x = x + _L0_ffn_ref(_layernorm(x, axis=-1), L0_ffn_gate_w, L0_ffn_gate_b, L0_ffn_expert_w, L0_ffn_expert_b)
    x = x + _L1_attn_ref(_layernorm(x, axis=-1), L1_attn_Wq, L1_attn_Wk, L1_attn_Wv)
    x = x + _L1_xattn_ref(_layernorm(x, axis=-1), ctx_1024, ctx_1024, mask_Bx1xSxS2_bk0, L1_xattn_Wq, L1_xattn_bq, L1_xattn_Wk, L1_xattn_bk, L1_xattn_Wv, L1_xattn_bv, L1_xattn_Wo, L1_xattn_bo)
    x = x + _L1_ffn_ref(_layernorm(x, axis=-1), L1_ffn_w1_w, L1_ffn_w1_s, L1_ffn_w2_w, L1_ffn_w2_s, L1_ffn_h1_w, L1_ffn_h1_s, L1_ffn_h2_w, L1_ffn_h2_s, L1_ffn_w3_w, L1_ffn_w3_s)
    return x

_drawn_inputs = setup_inputs


def setup_inputs(seed=0):
    import zlib

    import numpy as np

    out = dict(_drawn_inputs(seed))
    spreads = {'L0_attn_dt_bias': (1.0, 0.2),
     'L0_attn_norm_w': (1.0, 0.2),
     'L1_xattn_bq': (0.0, 0.1),
     'L1_xattn_bk': (0.0, 0.1),
     'L1_xattn_bv': (0.0, 0.1),
     'L1_xattn_bo': (0.0, 0.1)}
    factors = {}
    for name, (base, spread) in spreads.items():
        noise = np.random.default_rng([zlib.crc32(name.encode()), seed]).standard_normal(out[name].shape)
        drawn = base * np.exp(spread * noise) if base else spread * noise
        out[name] = jnp.asarray(drawn.astype(out[name].dtype))
    for name, factor in factors.items():
        out[name] = (out[name] * factor).astype(out[name].dtype)
    return out
```

```python
from contextlib import ExitStack

import numpy as np

import concourse.bass as bass
from concourse import mybir

F32 = mybir.dt.float32
BF16 = mybir.dt.bfloat16
I32 = mybir.dt.int32
U8 = mybir.dt.uint8
ACT = mybir.ActivationFunctionType
ALU = mybir.AluOpType
AXX = mybir.AxisListType.X

B, T, D = 16, 112, 256
S2 = 375
KD = D // 128
G = 4
GT = G * T
NG = B // G
HEADS, DK = 8, 128
TAPS = 4
HWID = 4 * KD * 128
XH, XD = 16, 16
CK = 125
NC = S2 // CK
EXPERTS = 8
HID = 1024
HT = HID // 128
NEG = -1.0e30
BUMP = 4096
LEVELS = 7
STAGES = 6


class Steps:

    def __init__(self, who, sem, plan):
        self.who, self.sem, self.plan = who, sem, plan
        self.frames = [{"name": who, "origin": BUMP, "n": 0, "pos": 0}]

    def open(self, name, i):
        top = self.frames[-1]
        n = self.plan.get((self.who, name), 0)
        self.frames.append({"name": name, "origin": top["origin"] + top["pos"] + i * n, "n": n, "pos": 0})

    def close(self, trips):
        f = self.frames.pop()
        self.plan[(self.who, f["name"])] = f["pos"]
        self.frames[-1]["pos"] += trips * f["pos"]

    def do(self, ins, name=None):
        f = self.frames[-1]
        f["pos"] += 1
        if name:
            self.plan[(self.who, f["name"], name)] = f["pos"]
        ins.then_inc(self.sem, 1)
        return ins

    def at(self, name, ago=0):
        for f in reversed(self.frames):
            if (self.who, f["name"], name) in self.plan:
                v = f["origin"] + self.plan[(self.who, f["name"], name)] - ago * f["n"]
                return self.sem, v
        return self.sem, self.frames[0]["origin"]

    def all(self):
        f = self.frames[-1]
        return self.sem, f["origin"] + f["pos"]


def after(eng, *points):
    for sem, value in points:
        eng.wait_ge(sem, value)


def decoder(nc, a, out, plan):
    pe, act, dve, pool, sp = nc.tensor, nc.scalar, nc.vector, nc.gpsimd, nc.sync
    with ExitStack() as ctx:
        def sb(name, shape, dt=F32):
            return ctx.enter_context(nc.sbuf_tensor(name, shape, dt))

        def sem(name):
            return ctx.enter_context(nc.semaphore(name))

        x = sb("x", [T, B, D])
        ident = sb("ident", [128, 128])
        ident_bf = sb("ident_bf", [128, 128], BF16)
        before = sb("before", [T, T])
        upto = sb("upto", [T, T])
        minus_strict = sb("minus_strict", [T, T])
        causal_neg = sb("causal_neg", [T, T])
        rows = sb("rows", [128, 4])
        rank = sb("rank", [T, G * EXPERTS])
        minus_half = sb("minus_half", [T, G])

        head_w = sb("head_w", [128, HWID + 3 * TAPS])
        ba_w = sb("ba_w", [128, KD, 2 * HEADS])
        dt_bias = sb("dt_bias", [T, HEADS])
        decay = sb("decay", [T, HEADS])
        norm_w = sb("norm_w", [128, 1])
        gdn_out_w = sb("gdn_out_w", [128, HEADS, D])
        xw = [{n: sb(f"x{n}{l}", [128, KD, D]) for n in ("q", "k", "v", "o")} for l in range(2)]
        xb_row = [{n: sb(f"x{n}_bias{l}", [128, D]) for n in (("o",), ("v", "o"))[l]} for l in range(2)]
        xb_col = sb("xb_col", [128, 2, KD])
        gate_w = sb("gate_w", [128, KD, EXPERTS])
        gate_b = sb("gate_b", [T, EXPERTS])
        expert_w = sb("expert_w", [128, KD, EXPERTS * D])
        expert_b = sb("expert_b", [EXPERTS, D])
        attn_w = sb("attn_w", [128, KD, 3 * D])
        w12 = sb("w12", [128, 2, KD, HID])
        hw = [sb(f"h{n}_w", [128, HT, HID]) for n in (1, 2)]
        w3 = sb("w3", [128, HT, D])
        hid_s = sb("hid_s", [128, 4, HT])
        w3_s = sb("w3_s", [T, D])

        stats = sb("stats", [T, G, 6])
        mean_var = sb("mean_var", [T, G, 2])
        var_eps = sb("var_eps", [T, G])
        rstd = sb("rstd", [T, G])
        carrier = sb("carrier", [T, 1])
        xn = sb("xn", [T, G, D])
        xT = sb("xT", [128, KD, GT])
        big_a = sb("big_a", [128, HT, GT])
        big_b = sb("big_b", [128, HT, GT])
        silu = sb("silu", [128, 2, GT])
        small = sb("small", [T, 16, G * EXPERTS])
        soft = sb("soft", [T, G, T])
        soft_max = sb("soft_max", [T, 4, G])

        ps = ctx.enter_context(nc.psum_tensor("ps", [128, 8, 512], F32))

        PE, AC, DV, PL = (Steps(n, sem(f"s_{n}"), plan) for n in ("pe", "act", "dve", "pool"))
        for eng, st in ((pe, PE), (act, AC), (dve, DV), (pool, PL)):
            eng.sem_inc(st.sem, BUMP)
        s_x, s_const, s_headw, s_ctx, s_out = (sem(n) for n in ("s_x", "s_const", "s_headw", "s_ctx", "s_out"))
        s_mask = sem("s_mask")

        def loop(name, n):
            class L:
                def __enter__(self):
                    self.c = nc.Fori(0, n)
                    self.i = self.c.__enter__()
                    for st in (PE, AC, DV, PL):
                        st.open(name, self.i)
                    return self.i

                def __exit__(self, *e):
                    for st in (PE, AC, DV, PL):
                        st.close(n)
                    return self.c.__exit__(*e)
            return L()

        def load(dst, name, s, eng=sp):
            eng.dma_start(dst, a[name]).then_inc(s, 16)

        sp.dma_start(x[:, :, :], a["x"].rearrange("b t d -> t b d")).then_inc(s_x, 16)
        consts = [(ident[:, :], "ident"), (before[:, :], "before"), (upto[:, :], "upto"),
                  (minus_strict[:, :], "minus_strict"), (causal_neg[:, :], "causal_neg"), (rows[:, :], "rows"),
                  (rank[:, :], "rank"), (ba_w[:, :, :], "ba_w"), (dt_bias[:, :], "dt_bias"), (decay[:, :], "A_log"),
                  (norm_w[:, :], "norm_w"), (gdn_out_w[:, :, :], "gdn_out_w")]
        for dst, name in consts:
            load(dst, name, s_const)
        weights = {}
        for l in range(2):
            weights[f"x{l}"] = [(xw[l][n][:, :, :], f"x{l}_W{n}") for n in "qkvo"] + \
                               [(t[:, :], f"x{l}_b{n}") for n, t in xb_row[l].items()]
        weights["x1"].append((xb_col[:, :, :], "x1_bqk"))
        weights["moe"] = [(gate_w[:, :, :], "gate_w"), (gate_b[:, :], "gate_b"), (expert_w[:, :, :], "expert_w"),
                          (expert_b[:, :], "expert_b")]
        weights["attn"] = [(attn_w[:, :, :], "attn_w")]
        weights["ffn"] = [(w12[:, :, :, :], "w12"), (hw[0][:, :, :], "h1"), (hw[1][:, :, :], "h2"),
                          (w3[:, :, :], "w3"), (hid_s[:, :, :], "hid_s"), (w3_s[:, :], "w3_s")]
        s_w = {}
        for stage in ("x0", "moe", "attn", "x1", "ffn"):
            s_w[stage] = (sem(f"s_w_{stage}"), 16 * len(weights[stage]))
            for dst, name in weights[stage]:
                load(dst, name, s_w[stage][0], act)

        consts_in = (s_const, 16 * len(consts))
        for eng in (pe, act, dve, pool):
            after(eng, consts_in)
        after(dve, (s_x, 16))
        PL.do(pool.memset(minus_half[:, :], -0.5), "minus_half")
        DV.do(dve.tensor_copy(ident_bf[:, :], ident[:, :]))
        DV.do(dve.tensor_scalar(norm_w[:, :], norm_w[:, :], 0.5, None, ALU.mult))
        AC.do(act.activation(decay[:, :], decay[:, :], ACT.Exp), "decay")
        for eng in (pe, act, dve, pool):
            after(eng, PL.all(), DV.all(), AC.all())

        def layernorm(seqs, first, cols):
            after(dve, DV.all(), PE.all())
            for j in range(seqs):
                DV.do(dve.bn_stats(stats[:, j, :], x[:, first + j, :]))
            after(dve, DV.all())
            DV.do(dve.memset(carrier[:, :], 0.0))
            for j in range(seqs):
                DV.do(dve.bn_aggr(mean_var[:, j, :], stats[:, j, :]))
            after(dve, DV.all())
            DV.do(dve.tensor_scalar(var_eps[:, 0:seqs], mean_var[:, 0:seqs, 1], 1e-5, None, ALU.add), "ln_var")
            after(pool, DV.at("ln_var"))
            PL.do(pool.tensor_tensor(rstd[:, 0:seqs], var_eps[:, 0:seqs], minus_half[:, 0:seqs], ALU.pow), "ln_rstd")
            after(dve, PL.at("ln_rstd"))
            for j in range(seqs):
                DV.do(dve.tensor_scalar(xn[:, j, :], x[:, first + j, :], mean_var[:, j, 0:1], rstd[:, j:j + 1],
                                        ALU.subtract, ALU.mult), "ln_xn")
            after(pe, DV.at("ln_xn"), AC.all())
            for k in range(KD):
                for j in range(seqs):
                    last = pe.transpose(ps[:, k, j * T:(j + 1) * T], xn[:, j, k * 128:(k + 1) * 128], ident[0:T, 0:T])
                PE.do(last, f"ln_T{k}")
            after(act, PE.at("ln_T0"))
            AC.do(act.activation(xT[:, 0, 0:cols], ps[:, 0, 0:cols], ACT.Copy), "ln_done0")
            after(dve, PE.at("ln_T1"))
            DV.do(dve.tensor_copy(xT[:, 1, 0:cols], ps[:, 1, 0:cols]), "ln_done1")
            after(pe, AC.at("ln_done0"), DV.at("ln_done1"))

        beta_decay = small[:, 0:2, :]
        here = sb("here", [T, 2, G])
        cum_l = big_a[0:T, 0, :].rearrange("p (g t) -> p g t", g=G)
        gamma = big_a[0:T, 1, :]
        gam_s = big_a[0:T, 2, :].rearrange("p (g t) -> p g t", g=G)
        gam_i = big_a[0:T, 3, :].rearrange("p (g t) -> p g t", g=G)
        qT, kT, vT, zT = (big_b[:, n, :] for n in range(4))
        oT = big_b[:, 4, :]
        sz = big_b[:, 5, :]
        NT = [big_a[0:T, 4, :], big_a[0:T, 5, :]]
        MM = big_a[0:T, 6, :]
        QG = big_a[0:T, 7, :]
        W = silu[0:T, :, :].rearrange("p a b -> p (a b)")[:, 0:G * DK]
        On = xn[:, 0:2, :].rearrange("p a b -> p (a b)")

        def p3(ap):
            return ap.rearrange("p (g t) -> p g t", g=G)

        with loop("gdn", NG) as g:
            layernorm(G, g * G, GT)
            for j in range(G):
                for k in range(KD):
                    last = pe.matmul(ps[0:T, 2, j * 16:(j + 1) * 16], xT[:, k, j * T:(j + 1) * T], ba_w[:, k, :],
                                     start=(k == 0), stop=(k == KD - 1))
            PE.do(last, "ba")
            ba = ps[0:T, 2, 0:G * 16].rearrange("p (g c) -> p g c", g=G)
            y, t1, t2, bb = (small[:, n, :].rearrange("p (g c) -> p g c", g=G) for n in (2, 3, 4, 5))
            after(dve, PE.at("ba"))
            DV.do(dve.tensor_tensor(y, ba[:, :, HEADS:], dt_bias[:, :].unsqueeze(1).to_broadcast([T, G, HEADS]), ALU.add))
            DV.do(dve.tensor_copy(bb, ba[:, :, 0:HEADS]), "ba_in")
            after(act, DV.at("ba_in"))
            AC.do(act.activation(t1, y, ACT.Abs), "sp1")
            after(act, AC.at("sp1"))
            AC.do(act.activation(t1, t1, ACT.Exp, scale=-1.0), "sp2")
            AC.do(act.activation(bb, bb, ACT.Exp, scale=-1.0), "sig")
            after(act, AC.at("sp2"))
            AC.do(act.activation(t1, t1, ACT.Ln, bias=1.0), "sp3")
            after(dve, AC.at("sp3"))
            DV.do(dve.scalar_tensor_tensor(t2, y, 0.0, t1, ALU.max, ALU.add))
            DV.do(dve.tensor_scalar(bb, bb, 1.0, None, ALU.add))
            after(dve, DV.all())
            DV.do(dve.reciprocal(beta_decay[:, 0, :].rearrange("p (g c) -> p g c", g=G), bb))
            DV.do(dve.scalar_tensor_tensor(beta_decay[:, 1, :].rearrange("p (g c) -> p g c", g=G), t2, -1.0,
                                           decay[:, :].unsqueeze(1).to_broadcast([T, G, HEADS]), ALU.mult, ALU.mult),
                  "beta_decay")

            with loop("head", HEADS) as h:
                after(sp, PE.at("proj3", 1), DV.at("conv2", 1))
                sp.dma_start(head_w[:, :], a["head_w"][h]).then_inc(s_headw, 16)
                w4 = head_w[:, 0:HWID].rearrange("p (n k c) -> p n k c", n=4, k=KD)
                taps = head_w[:, HWID:].rearrange("p (n j) -> p n j", j=TAPS)
                head_in = (s_headw, (g * HEADS + h + 1) * 16)

                after(pe, head_in, AC.all(), DV.all())
                for n in (1, 0, 2, 3):
                    for k in range(KD):
                        last = pe.matmul(ps[:, n, 0:GT], w4[:, n, k, :], xT[:, k, :], start=(k == 0), stop=(k == KD - 1))
                    PE.do(last, f"proj{n}")
                after(dve, DV.all())
                DV.do(dve.tensor_copy(here[:, :, :],
                                       beta_decay.rearrange("p n (g c) -> p n g c", g=G)[:, :, :, h]), "here")
                after(dve, DV.at("here"))
                DV.do(dve.tensor_tensor(cum_l, before[:, :].unsqueeze(1).to_broadcast([T, G, T]),
                                        here[:, 1, :].unsqueeze(2).to_broadcast([T, G, T]), ALU.mult), "cum_l")
                after(act, head_in)
                for n, dst in ((1, kT), (0, qT), (2, vT)):
                    after(act, PE.at(f"proj{n}"))
                    AC.do(act.activation(dst, ps[:, n, 0:GT], ACT.Copy, scale=taps[:, n, TAPS - 1:TAPS]), f"tap{n}")
                after(act, PE.at("proj3"))
                AC.do(act.activation(zT, ps[:, 3, 0:GT], ACT.Tanh, scale=0.5), "tanh")
                for n, dst in ((1, kT), (0, qT), (2, vT)):
                    after(dve, AC.at(f"tap{n}"))
                    for s in range(1, TAPS):
                        DV.do(dve.scalar_tensor_tensor(p3(dst)[:, :, s:], p3(ps[:, n, 0:GT])[:, :, 0:T - s],
                                                       taps[:, n, TAPS - 1 - s:TAPS - s], p3(dst)[:, :, s:],
                                                       ALU.mult, ALU.add), f"conv{n}")
                        after(dve, DV.at(f"conv{n}"))
                after(dve, AC.at("tanh"))
                DV.do(dve.scalar_tensor_tensor(sz, zT, 1.0, ps[:, 3, 0:GT], ALU.add, ALU.mult), "sz")
                after(pe, DV.at("cum_l"))
                for j in range(G):
                    last = pe.matmul(ps[0:T, 4, j * T:(j + 1) * T], cum_l[:, j, :], upto[:, :], start=True, stop=True)
                PE.do(last, "logG")
                after(act, PE.at("logG"))
                AC.do(act.activation(gamma, ps[0:T, 4, 0:GT], ACT.Exp), "gamma")
                after(pool, AC.at("gamma"))
                PL.do(pool.tensor_tensor(gam_s, p3(gamma), minus_strict[:, :].unsqueeze(1).to_broadcast([T, G, T]), ALU.mult), "gam_s")
                PL.do(pool.tensor_tensor(gam_i, p3(gamma), upto[:, :].unsqueeze(1).to_broadcast([T, G, T]), ALU.mult), "gam_i")
                after(pe, DV.at("conv1"))
                for j in range(G):
                    c = slice(j * T, (j + 1) * T)
                    last = pe.matmul(ps[0:T, 5, c], kT[:, c], kT[:, c], start=True, stop=True)
                PE.do(last, "kk")
                after(pe, DV.at("conv0"))
                for j in range(G):
                    c = slice(j * T, (j + 1) * T)
                    last = pe.matmul(ps[0:T, 6, c], kT[:, c], qT[:, c], start=True, stop=True)
                PE.do(last, "kq")
                after(pe, DV.at("conv2"))
                for j in range(G):
                    last = pe.transpose(ps[0:T, 7, j * DK:(j + 1) * DK], vT[:, j * T:(j + 1) * T], ident[:, :])
                PE.do(last, "vtok")
                after(act, PE.at("vtok"))
                AC.do(act.activation(W, ps[0:T, 7, 0:G * DK], ACT.Copy), "W0")
                after(dve, PE.at("kk"), PL.at("gam_s"))
                for j in range(G):
                    c = slice(j * T, (j + 1) * T)
                    DV.do(dve.scalar_tensor_tensor(NT[0][:, c], ps[0:T, 5, c], here[:, 0, j:j + 1], gam_s[:, j, :],
                                                   ALU.mult, ALU.mult), "N0")
                after(dve, PE.at("kq"), PL.at("gam_i"))
                for j in range(G):
                    c = slice(j * T, (j + 1) * T)
                    DV.do(dve.scalar_tensor_tensor(QG[:, c], ps[0:T, 6, c], here[:, 0, j:j + 1], gam_i[:, j, :],
                                                   ALU.mult, ALU.mult), "QG")
                for lev in range(LEVELS):
                    N = NT[lev % 2]
                    after(pe, DV.at(f"N{lev}"))
                    if lev < LEVELS - 1:
                        if lev == 0:
                            after(pe, DV.at("conv0"))
                        for j in range(G):
                            c = slice(j * T, (j + 1) * T)
                            last = pe.transpose(ps[0:T, 0, c], N[:, c], ident[0:T, 0:T])
                        PE.do(last, f"M{lev}T")
                        after(act, PE.at(f"M{lev}T"))
                        AC.do(act.activation(MM, ps[0:T, 0, 0:GT], ACT.Copy), f"M{lev}")
                    after(pe, AC.at("W0") if lev == 0 else DV.at(f"W{lev}"))
                    for j in range(G):
                        c = slice(j * T, (j + 1) * T)
                        last = pe.matmul(ps[0:T, 7, j * DK:(j + 1) * DK], N[:, c], W[:, j * DK:(j + 1) * DK],
                                         start=True, stop=True)
                    PE.do(last, f"PW{lev}")
                    if lev < LEVELS - 1:
                        after(pe, AC.at(f"M{lev}"))
                        for j in range(G):
                            c = slice(j * T, (j + 1) * T)
                            last = pe.matmul(ps[0:T, 5, c], MM[:, c], N[:, c], start=True, stop=True)
                        PE.do(last, f"N{lev + 1}ps")
                    after(dve, PE.at(f"PW{lev}"), *([AC.at("W0")] if lev == 0 else []))
                    DV.do(dve.tensor_tensor(W, W, ps[0:T, 7, 0:G * DK], ALU.add), f"W{lev + 1}")
                    if lev < LEVELS - 1:
                        after(dve, PE.at(f"N{lev + 1}ps"))
                        DV.do(dve.tensor_copy(NT[(lev + 1) % 2], ps[0:T, 5, 0:GT]), f"N{lev + 1}")
                after(pe, DV.at(f"W{LEVELS}"))
                for j in range(G):
                    last = pe.matmul(ps[0:T, 6, j * DK:(j + 1) * DK], QG[:, j * T:(j + 1) * T],
                                     W[:, j * DK:(j + 1) * DK], start=True, stop=True)
                PE.do(last, "O")
                after(act, PE.at("O"))
                for j in range(G):
                    AC.do(act.activation(On[:, j * DK:(j + 1) * DK], ps[0:T, 6, j * DK:(j + 1) * DK], ACT.Square,
                                         accum_out=var_eps[:, j:j + 1]), "squares")
                after(dve, AC.at("squares"))
                DV.do(dve.tensor_scalar(var_eps[:, :], var_eps[:, :], 1.0 / DK, 1e-6, ALU.mult, ALU.add), "o_var")
                after(pool, DV.at("o_var"))
                PL.do(pool.tensor_tensor(rstd[:, :], var_eps[:, :], minus_half[:, :], ALU.pow), "o_rstd")
                after(dve, PL.at("o_rstd"))
                DV.do(dve.tensor_tensor(On.rearrange("p (g d) -> p g d", g=G),
                                        ps[0:T, 6, 0:G * DK].rearrange("p (g d) -> p g d", g=G),
                                        rstd[:, :].unsqueeze(2).to_broadcast([T, G, DK]), ALU.mult), "On")
                after(pe, DV.at("On"))
                for j in range(G):
                    last = pe.transpose(ps[:, 1, j * T:(j + 1) * T], On[:, j * DK:(j + 1) * DK], ident[0:T, 0:T])
                PE.do(last, "oT")
                after(dve, PE.at("oT"))
                DV.do(dve.scalar_tensor_tensor(oT, ps[:, 1, 0:GT], norm_w[:, 0:1], sz, ALU.mult, ALU.mult), "gated")
                after(pe, DV.at("gated"))
                for j in range(G):
                    last = pe.matmul(ps[0:T, 2 + j // 2, (j % 2) * D:(j % 2 + 1) * D], oT[:, j * T:(j + 1) * T],
                                     gdn_out_w[:, h, :], start=True, stop=True)
                PE.do(last, "out")
                after(dve, PE.at("out"))
                for n in range(G // 2):
                    xs = x[:, bass.ds(g * G + 2 * n, 2), :]
                    DV.do(dve.tensor_tensor(xs, xs, ps[0:T, 2 + n, :].rearrange("p (g d) -> p g d", g=2), ALU.add), "x")

        def cross_attention(l):
            scale_col = 2 * l
            w, name = xw[l], f"x{l}"
            ctxT = big_a[:, 0:2, 0:S2]
            KT = big_a[:, 2:4, 0:S2]
            V = big_a[0:CK, 4:6, :].rearrange("p a b -> p (a b)")[:, 0:NC * D].rearrange("p (c n) -> p c n", c=NC)
            qm = big_a[:, 6, :].rearrange("p (m e t) -> p m e t", m=KD, e=2)
            P = [big_b[0:T, n, 0:S2] for n in range(3)]
            PT = [big_b[0:CK, 3 + n, 0:NC * T] for n in range(2)]
            mask = big_b[0:T, 5, 0:S2].bitcast(I32) if l == 0 else \
                big_b[0:T, 5, 0:96].bitcast(U8)[:, 0:S2]
            mask_neg = big_b[0:T, 6, 0:192].bitcast(BF16)[:, 0:S2]
            neg_max = small[:, 0, 0:XH]
            sums = small[:, 1, 0:XH]
            inv = small[:, 2, 0:XH]
            on = big_b[0:T, 7, 0:D]
            onT = big_a[:, 7, 0:2 * T]
            for eng in (pe, act, dve):
                after(eng, s_w[name])
            after(sp, PE.all(), AC.all(), DV.all(), PL.all())
            base_ctx = l * B
            with loop(name, B) as b:
                after(sp, PE.at("v_proj", 1), DV.at("mask_neg", 1))
                sp.dma_start(ctxT, a["ctxT"][b]).then_inc(s_ctx, 16)
                sp.dma_start(mask, a[f"mask{l}"][b]).then_inc(s_mask, 16)
                ctx_in = (s_ctx, (b + base_ctx + 1) * 16)
                layernorm(1, b, T)
                for m in range(KD):
                    for k in range(KD):
                        last = pe.matmul(ps[:, 2, m * T:(m + 1) * T], w["q"][:, k, m * 128:(m + 1) * 128], xT[:, k, 0:T],
                                         start=(k == 0), stop=(k == KD - 1))
                PE.do(last, "q_proj")
                after(pe, ctx_in)
                for m in range(KD):
                    for k in range(KD):
                        last = pe.matmul(ps[:, 3 + m, 0:S2], w["k"][:, k, m * 128:(m + 1) * 128], ctxT[:, k, :],
                                         start=(k == 0), stop=(k == KD - 1))
                    PE.do(last, f"k_proj{m}")
                for c in range(NC):
                    for k in range(KD):
                        last = pe.matmul(ps[0:CK, 5 + c // 2, (c % 2) * D:(c % 2 + 1) * D],
                                         ctxT[:, k, c * CK:(c + 1) * CK], w["v"][:, k, :],
                                         start=(k == 0), stop=(k == KD - 1))
                PE.do(last, "v_proj")
                after(dve, (s_mask, (b + base_ctx + 1) * 16))
                DV.do(dve.tensor_scalar(mask_neg, mask, 0.0, NEG, ALU.is_equal, ALU.mult), "mask_neg")
                after(dve, PE.at("q_proj"))
                for m in range(KD):
                    for e in range(2):
                        src = ps[:, 2, m * T:(m + 1) * T]
                        row = rows[:, scale_col + e:scale_col + e + 1]
                        if l == 0:
                            ins = dve.tensor_scalar(qm[:, m, e, :], src, row, None, ALU.mult)
                        else:
                            ins = dve.tensor_scalar(qm[:, m, e, :], src, xb_col[:, 0, m:m + 1], row, ALU.add, ALU.mult)
                        DV.do(ins, "qm")
                for m in range(KD):
                    after(act, PE.at(f"k_proj{m}"))
                    if l == 0:
                        ins = act.activation(KT[:, m, :], ps[:, 3 + m, 0:S2], ACT.Copy)
                    else:
                        ins = act.activation(KT[:, m, :], ps[:, 3 + m, 0:S2], ACT.Identity, bias=xb_col[:, 1, m:m + 1])
                    AC.do(ins, "KT")
                after(dve, PE.at("v_proj"))
                for c in range(NC):
                    src = ps[0:CK, 5 + c // 2, (c % 2) * D:(c % 2 + 1) * D]
                    if l == 0:
                        ins = dve.tensor_copy(V[:, c, :], src)
                    else:
                        ins = dve.tensor_tensor(V[:, c, :], src, xb_row[1]["v"][0:CK, :], ALU.add)
                    DV.do(ins, "V")
                after(pe, DV.at("V"), AC.at("KT"))
                for s in range(XH + 2):
                    if s < XH:
                        m, r, e = s // 8, 32 * (s % 8 // 2), s % 2
                        sc = ps[0:T, s % 4, 0:S2]
                        if s >= 4:
                            after(pe, AC.at(f"exp{s - 4}"))
                        pe.matmul(sc, qm[r:r + 32, m, e, :], KT[r:r + 32, m, :], start=True, stop=False)
                        PE.do(pe.matmul(sc, ident_bf[0:T, 0:T], mask_neg, start=False, stop=True), f"S{s}")
                        after(dve, PE.at(f"S{s}"))
                        DV.do(dve.tensor_reduce(neg_max[:, s:s + 1], sc, AXX, ALU.max, negate=True), f"max{s}")
                        after(act, DV.at(f"max{s}"))
                        if s >= 3:
                            after(act, PE.at(f"PT{s - 3}"))
                        AC.do(act.activation(P[s % 3], sc, ACT.Exp, bias=neg_max[:, s:s + 1],
                                             accum_out=sums[:, s:s + 1]), f"exp{s}")
                    if 1 <= s <= XH:
                        h = s - 1
                        after(pe, AC.at(f"exp{h}"))
                        if h >= 2:
                            after(pe, DV.at(f"PTsb{h - 2}"))
                        for c in range(NC):
                            last = pe.transpose(ps[0:CK, 4 + h % 2, c * T:(c + 1) * T], P[h % 3][:, c * CK:(c + 1) * CK],
                                                ident[0:T, 0:T])
                        PE.do(last, f"PT{h}")
                        after(dve, PE.at(f"PT{h}"))
                        if h >= 2:
                            after(dve, PE.at(f"PV{h - 2}"))
                        DV.do(dve.tensor_copy(PT[h % 2], ps[0:CK, 4 + h % 2, 0:NC * T]), f"PTsb{h}")
                    if s >= 2:
                        h = s - 2
                        after(pe, DV.at(f"PTsb{h}"))
                        for c in range(NC):
                            last = pe.matmul(ps[0:T, 6, h * XD:(h + 1) * XD], PT[h % 2][:, c * T:(c + 1) * T],
                                             V[:, c, h * XD:(h + 1) * XD], start=(c == 0), stop=(c == NC - 1))
                        PE.do(last, f"PV{h}")
                after(dve, AC.at(f"exp{XH - 1}"))
                DV.do(dve.reciprocal(inv, sums), "inv")
                after(dve, DV.at("inv"), PE.at(f"PV{XH - 1}"))
                DV.do(dve.tensor_tensor(on.rearrange("p (h d) -> p h d", h=XH),
                                        ps[0:T, 6, 0:D].rearrange("p (h d) -> p h d", h=XH),
                                        inv.unsqueeze(2).to_broadcast([T, XH, XD]), ALU.mult), "on")
                after(pe, DV.at("on"))
                for k in range(KD):
                    last = pe.transpose(ps[:, 7, k * T:(k + 1) * T], on[:, k * 128:(k + 1) * 128], ident[0:T, 0:T])
                PE.do(last, "onT_ps")
                after(dve, PE.at("onT_ps"))
                DV.do(dve.tensor_tensor(x[:, b, :], x[:, b, :], xb_row[l]["o"][0:T, :], ALU.add), "xb")
                after(act, PE.at("onT_ps"))
                AC.do(act.activation(onT, ps[:, 7, 0:2 * T], ACT.Copy), "onT")
                after(pe, AC.at("onT"))
                for k in range(KD):
                    last = pe.matmul(ps[0:T, 6, 0:D], onT[:, k * T:(k + 1) * T], w["o"][:, k, :],
                                     start=(k == 0), stop=(k == KD - 1))
                PE.do(last, "o_proj")
                after(dve, PE.at("o_proj"), DV.at("xb"))
                DV.do(dve.tensor_tensor(x[:, b, :], x[:, b, :], ps[0:T, 6, 0:D], ALU.add), "x")

        if STAGES > 1:
            cross_attention(0)

        def experts():
            for eng in (pe, dve):
                after(eng, s_w["moe"])
            gateT = big_a[0:EXPERTS, 0, :]

            def sm(n):
                return small[:, n, :].rearrange("p (g e) -> p g e", g=G)

            def one(n):
                return soft_max[:, n, :]

            def wide(ap):
                return ap.unsqueeze(2).to_broadcast([T, G, EXPERTS])

            with loop("moe", NG) as g:
                layernorm(G, g * G, GT)
                for j in range(G):
                    for k in range(KD):
                        last = pe.matmul(ps[0:T, 2, j * EXPERTS:(j + 1) * EXPERTS], xT[:, k, j * T:(j + 1) * T],
                                         gate_w[:, k, :], start=(k == 0), stop=(k == KD - 1))
                PE.do(last, "logits")
                after(dve, PE.at("logits"))
                logit, hit, cand, keep1, rest, keep2, ex, gate = (sm(n) for n in range(8))
                top, pick, total = one(0), one(1), one(2)
                rk = rank[:, :].rearrange("p (g e) -> p g e", g=G)

                def chain(ins, name=None):
                    DV.do(ins, name)
                    after(dve, DV.all())

                chain(dve.tensor_tensor(logit, ps[0:T, 2, 0:G * EXPERTS].rearrange("p (g e) -> p g e", g=G),
                                        gate_b[:, :].unsqueeze(1).to_broadcast([T, G, EXPERTS]), ALU.add))
                chain(dve.tensor_reduce(top, logit, AXX, ALU.max))
                chain(dve.tensor_tensor(ex, logit, wide(top), ALU.subtract), "shifted")
                src = logit
                for n, keep in ((0, keep1), (1, keep2)):
                    if n:
                        chain(dve.tensor_reduce(pick, src, AXX, ALU.max))
                    chain(dve.tensor_tensor(hit, src, wide(pick if n else top), ALU.is_equal))
                    chain(dve.tensor_tensor(cand, hit, rk, ALU.mult))
                    chain(dve.tensor_reduce(pick, cand, AXX, ALU.max))
                    chain(dve.tensor_tensor(keep, cand, wide(pick), ALU.is_equal))
                    if n == 0:
                        chain(dve.scalar_tensor_tensor(rest, keep1, -3.0e38, logit, ALU.mult, ALU.add))
                        src = rest
                chain(dve.tensor_tensor(keep1, keep1, keep2, ALU.add))
                after(act, DV.at("shifted"))
                AC.do(act.activation(ex, ex, ACT.Exp), "ex")
                after(dve, AC.at("ex"))
                chain(dve.tensor_tensor(ex, ex, keep1, ALU.mult))
                chain(dve.tensor_reduce(total, ex, AXX, ALU.add))
                chain(dve.reciprocal(total, total))
                chain(dve.tensor_tensor(gate, ex, wide(total), ALU.mult), "gate")
                after(pe, DV.at("gate"))
                for j in range(G):
                    last = pe.transpose(ps[0:EXPERTS, 3, j * T:(j + 1) * T], gate[:, j, :], ident[0:T, 0:T])
                PE.do(last, "gateT_ps")
                after(act, PE.at("gateT_ps"))
                AC.do(act.activation(gateT, ps[0:EXPERTS, 3, 0:GT], ACT.Copy), "gateT")
                after(pe, AC.at("gateT"))
                for j in range(G):
                    last = pe.matmul(ps[0:T, j // 2, (j % 2) * D:(j % 2 + 1) * D], gateT[:, j * T:(j + 1) * T],
                                     expert_b[:, :], start=True, stop=True)
                PE.do(last, "bias")
                after(dve, PE.at("bias"))
                for n in range(G // 2):
                    xs = x[:, bass.ds(g * G + 2 * n, 2), :]
                    DV.do(dve.tensor_tensor(xs, xs, ps[0:T, n, :].rearrange("p (g d) -> p g d", g=2), ALU.add), "x_bias")
                after(dve, DV.at("x_bias"))
                n = 0
                for j in range(G):
                    for e in range(0, EXPERTS, 2):
                        bank = 4 + n % 4
                        if n >= 4:
                            after(pe, DV.at(f"x{n - 4}"))
                        for k in range(KD):
                            last = pe.matmul(ps[0:T, bank, :], xT[:, k, j * T:(j + 1) * T],
                                             expert_w[:, k, e * D:(e + 2) * D], start=(k == 0), stop=(k == KD - 1))
                        PE.do(last, f"e{n}")
                        after(dve, PE.at(f"e{n}"))
                        for q in range(2):
                            xs = x[:, g * G + j, :]
                            DV.do(dve.scalar_tensor_tensor(xs, ps[0:T, bank, q * D:(q + 1) * D],
                                                           gate[:, j, e + q:e + q + 1], xs, ALU.mult, ALU.add), f"x{n}")
                            after(dve, DV.at(f"x{n}"))
                        n += 1

        if STAGES > 2:
            experts()

        def self_attention():
            for eng in (pe,):
                after(eng, s_w["attn"])
            qk = big_b
            v = big_a[0:T, 0:3, :].rearrange("p a b -> p (a b)")[:, 0:G * D].rearrange("p (g d) -> p g d", g=G)
            PTs = big_a[0:T, 4, :]
            with loop("attn", NG) as g:
                layernorm(G, g * G, GT)
                for n in range(2 * KD):
                    for k in range(KD):
                        last = pe.matmul(ps[:, 2 + n, 0:GT], attn_w[:, k, n * 128:(n + 1) * 128], xT[:, k, :],
                                         start=(k == 0), stop=(k == KD - 1))
                    PE.do(last, f"qk{n}")
                for n in range(2 * KD):
                    if n < KD:
                        after(act, PE.at(f"qk{n}"))
                        AC.do(act.activation(qk[:, n, :], ps[:, 2 + n, 0:GT], ACT.Copy, scale=1.0 / 16), "q")
                    else:
                        after(dve, PE.at(f"qk{n}"))
                        DV.do(dve.tensor_copy(qk[:, n, :], ps[:, 2 + n, 0:GT]), "k")
                for j in range(G):
                    for k in range(KD):
                        last = pe.matmul(ps[0:T, 6 + j // 2, (j % 2) * D:(j % 2 + 1) * D], xT[:, k, j * T:(j + 1) * T],
                                         attn_w[:, k, 2 * D:3 * D], start=(k == 0), stop=(k == KD - 1))
                PE.do(last, "v_ps")
                after(act, PE.at("v_ps"))
                for n in range(G // 2):
                    AC.do(act.activation(v[:, 2 * n:2 * n + 2, :], ps[0:T, 6 + n, :].rearrange("p (g d) -> p g d", g=2),
                                         ACT.Copy), "v")
                after(pe, AC.at("q"), DV.at("k"))
                for j in range(G):
                    c = slice(j * T, (j + 1) * T)
                    for k in range(KD):
                        last = pe.matmul(ps[0:T, 0, c], qk[:, k, c], qk[:, KD + k, c], start=(k == 0), stop=(k == KD - 1))
                PE.do(last, "S")
                after(dve, PE.at("S"))
                mx, tot = soft_max[:, 0, :], soft_max[:, 1, :]
                DV.do(dve.tensor_tensor(soft[:, :, :], p3(ps[0:T, 0, 0:GT]),
                                        causal_neg[:, :].unsqueeze(1).to_broadcast([T, G, T]), ALU.add), "masked")
                after(dve, DV.at("masked"))
                DV.do(dve.tensor_reduce(mx, soft[:, :, :], AXX, ALU.max), "max")
                after(dve, DV.at("max"))
                DV.do(dve.tensor_tensor(soft[:, :, :], soft[:, :, :], mx.unsqueeze(2).to_broadcast([T, G, T]),
                                        ALU.subtract), "shifted")
                after(act, DV.at("shifted"))
                AC.do(act.activation(soft[:, :, :], soft[:, :, :], ACT.Exp), "P")
                after(dve, AC.at("P"))
                DV.do(dve.tensor_reduce(tot, soft[:, :, :], AXX, ALU.add), "tot")
                after(dve, DV.at("tot"))
                DV.do(dve.reciprocal(tot, tot), "inv")
                after(pe, AC.at("P"))
                for j in range(G):
                    last = pe.transpose(ps[0:T, 1, j * T:(j + 1) * T], soft[:, j, :], ident[0:T, 0:T])
                PE.do(last, "PT_ps")
                after(act, PE.at("PT_ps"))
                AC.do(act.activation(PTs, ps[0:T, 1, 0:GT], ACT.Copy), "PT")
                after(pe, AC.at("PT"))
                for j in range(G):
                    last = pe.matmul(ps[0:T, 6 + j // 2, (j % 2) * D:(j % 2 + 1) * D], PTs[:, j * T:(j + 1) * T],
                                     v[:, j, :], start=True, stop=True)
                PE.do(last, "PV")
                after(dve, PE.at("PV"), DV.at("inv"))
                for j in range(G):
                    xs = x[:, g * G + j, :]
                    DV.do(dve.scalar_tensor_tensor(xs, ps[0:T, 6 + j // 2, (j % 2) * D:(j % 2 + 1) * D],
                                                   tot[:, j:j + 1], xs, ALU.mult, ALU.add), "x")

        if STAGES > 3:
            self_attention()
        if STAGES > 4:
            cross_attention(1)

        def feed_forward():
            for eng in (pe, act, dve):
                after(eng, s_w["ffn"])
            with loop("ffn", NG) as g:
                layernorm(G, g * G, GT)
                for m in range(HT):
                    for n in range(2):
                        if m >= 2:
                            after(pe, DV.at(f"h0_{m - 2}"))
                        for k in range(KD):
                            last = pe.matmul(ps[:, 2 + 2 * n + m % 2, 0:GT], w12[:, n, k, m * 128:(m + 1) * 128], xT[:, k, :],
                                             start=(k == 0), stop=(k == KD - 1))
                        PE.do(last, f"w{n}_{m}")
                    after(act, PE.at(f"w0_{m}"))
                    if m >= 2:
                        after(act, DV.at(f"h0_{m - 2}"))
                    AC.do(act.activation(silu[:, m % 2, :], ps[:, 2 + m % 2, 0:GT], ACT.Silu, scale=hid_s[:, 0, m:m + 1]),
                          f"silu{m}")
                    after(dve, AC.at(f"silu{m}"), PE.at(f"w1_{m}"))
                    DV.do(dve.scalar_tensor_tensor(big_a[:, m, :], ps[:, 4 + m % 2, 0:GT], hid_s[:, 1, m:m + 1],
                                                   silu[:, m % 2, :], ALU.mult, ALU.mult), f"h0_{m}")
                for n, (src, dst) in enumerate(((big_a, big_b), (big_b, big_a))):
                    for m in range(HT):
                        if n == 0 and m in (0, 2):
                            after(pe, DV.at(f"h0_{HT - 1}"))
                        if m >= 4:
                            after(pe, AC.at(f"g{n}_{m - 4}"))
                        elif n == 1:
                            after(pe, AC.at(f"g0_{HT - 1}"))
                        for k in range(HT):
                            last = pe.matmul(ps[:, m % 4, 0:GT], hw[n][:, k, m * 128:(m + 1) * 128], src[:, k, :],
                                             start=(k == 0), stop=(k == HT - 1))
                        PE.do(last, f"h{n + 1}_{m}")
                        after(act, PE.at(f"h{n + 1}_{m}"))
                        if n == 0 and m == 0:
                            pass
                        AC.do(act.activation(dst[:, m, :], ps[:, m % 4, 0:GT], ACT.Gelu, scale=hid_s[:, 2 + n, m:m + 1]),
                              f"g{n}_{m}")
                after(pe, AC.at(f"g1_{HT - 1}"))
                for j in range(G):
                    for k in range(HT):
                        last = pe.matmul(ps[0:T, 4 + j // 2, (j % 2) * D:(j % 2 + 1) * D], big_a[:, k, j * T:(j + 1) * T],
                                         w3[:, k, :], start=(k == 0), stop=(k == HT - 1))
                PE.do(last, "y_ps")
                y = xn
                after(dve, PE.at("y_ps"))
                for n in range(G // 2):
                    DV.do(dve.tensor_tensor(y[:, 2 * n:2 * n + 2, :], ps[0:T, 4 + n, :].rearrange("p (g d) -> p g d", g=2),
                                            w3_s[:, :].unsqueeze(1).to_broadcast([T, 2, D]), ALU.mult), "y")
                after(dve, DV.at("y"))
                xs = x[:, bass.ds(g * G, G), :]
                DV.do(dve.tensor_tensor(xs, xs, y[:, :, :], ALU.add), "x")
                after(sp, DV.at("x"))
                sp.dma_start(out[g].rearrange("b t d -> t b d"), xs).then_inc(s_out, 16)

        if STAGES > 5:
            feed_forward()
        else:
            after(sp, DV.all())
            for g in range(NG):
                sp.dma_start(out[g].rearrange("b t d -> t b d"), x[:, g * G:(g + 1) * G, :]).then_inc(s_out, 16)
        after(sp, *s_w.values(), (s_out, 16 * NG))


def lay_out(i):
    def c(v):
        return np.ascontiguousarray(v)

    def rows_of(w):
        return c(w.reshape(-1, 128, w.shape[-1]).transpose(1, 0, 2))

    def wide(v, n):
        return c(np.broadcast_to(v, (n, v.shape[-1])))

    def cols_of(v):
        return c(v.reshape(-1, 128).T)

    f = np.float32
    one = np.arange(128)
    t = np.arange(T)
    a = {"x": i["x"]}
    a["ctxT"] = c(i["ctx_1024"].transpose(0, 2, 1).reshape(B, KD, 128, S2).transpose(0, 2, 1, 3))
    a["mask0"] = c(i["mask_Bx1xSxS2_if1"][:, 0])
    a["mask1"] = c(i["mask_Bx1xSxS2_bk0"][:, 0])
    a["ident"] = np.eye(128, dtype=f)
    a["before"] = (t[None, :] < t[:, None]).astype(f)
    a["upto"] = (t[:, None] <= t[None, :]).astype(f)
    a["minus_strict"] = np.where(t[:, None] < t[None, :], f(-1), f(0))
    a["causal_neg"] = np.where(t[None, :] > t[:, None], f(NEG), f(0))
    even = (one // XD % 2 == 0).astype(f)
    a["rows"] = np.stack([even / 16, (1 - even) / 16, even / 4, (1 - even) / 4], axis=1).astype(f)
    a["rank"] = wide(np.tile(EXPERTS - np.arange(EXPERTS), G).astype(f), T)
    qkvz = np.concatenate([i["L0_attn_qkv_w"], i["L0_attn_z_w"]], 0)
    w = qkvz.reshape(4, HEADS, 128, KD, 128).transpose(1, 4, 0, 3, 2).reshape(HEADS, 128, HWID)
    taps = i["L0_attn_conv_w"].reshape(3, HEADS, 128, TAPS).transpose(1, 2, 0, 3).reshape(HEADS, 128, 3 * TAPS)
    a["head_w"] = c(np.concatenate([w, taps], -1))
    a["ba_w"] = rows_of(c(np.concatenate([i["L0_attn_b_w"], i["L0_attn_a_w"]], 0).T))
    a["dt_bias"] = wide(i["L0_attn_dt_bias"], T)
    a["A_log"] = wide(i["L0_attn_A_log"], T)
    a["norm_w"] = c(i["L0_attn_norm_w"].reshape(128, 1))
    a["gdn_out_w"] = rows_of(c(i["L0_attn_out_w"].T))
    for n in "qkvo":
        a[f"x0_W{n}"] = rows_of(c(i[f"L0_xattn_W{n}"].T))
        a[f"x1_W{n}"] = rows_of(i[f"L1_xattn_W{n}"])
    a["x0_bo"] = wide(i["L0_xattn_bo"], 128)
    a["x1_bo"] = wide(i["L1_xattn_bo"], 128)
    a["x1_bv"] = wide(i["L1_xattn_bv"], 128)
    a["x1_bqk"] = c(np.stack([cols_of(i["L1_xattn_bq"]), cols_of(i["L1_xattn_bk"])], 1))
    a["gate_w"] = rows_of(c(i["L0_ffn_gate_w"].T))
    a["gate_b"] = wide(i["L0_ffn_gate_b"], T)
    a["expert_w"] = rows_of(c(i["L0_ffn_expert_w"].transpose(1, 0, 2).reshape(D, EXPERTS * D)))
    a["expert_b"] = i["L0_ffn_expert_b"]
    a["attn_w"] = rows_of(np.concatenate([i["L1_attn_Wq"], i["L1_attn_Wk"], i["L1_attn_Wv"]], 1))
    a["w12"] = c(np.stack([rows_of(c(i["L1_ffn_w1_w"].T)), rows_of(c(i["L1_ffn_w2_w"].T))], 1))
    a["h1"] = rows_of(c(i["L1_ffn_h1_w"].T))
    a["h2"] = rows_of(c(i["L1_ffn_h2_w"].T))
    a["w3"] = rows_of(c(i["L1_ffn_w3_w"].T))
    a["hid_s"] = c(np.stack([cols_of(i[f"L1_ffn_{n}_s"]) for n in ("w1", "w2", "h1", "h2")], 1))
    a["w3_s"] = wide(i["L1_ffn_w3_s"], T)
    return {n: c(v) for n, v in a.items()}


def build(nc, shapes, plan):
    a = {n: nc.dram_tensor(f"in_{n}", s, mybir.dt.from_np(d), kind="ExternalInput").ap() for n, (s, d) in shapes.items()}
    out = nc.dram_tensor("out", (NG, G, T, D), F32, kind="ExternalOutput").ap()
    decoder(nc, a, out, plan)


def kernel(**inputs):
    import concourse.bacc as bacc
    from concourse.bass_utils import run_bass_kernel_spmd

    arrays = lay_out({n: np.asarray(v) for n, v in inputs.items()})
    shapes = {n: (v.shape, v.dtype) for n, v in arrays.items()}
    plan = {}
    build(bacc.Bacc("TRN2", target_bir_lowering=False, num_devices=1), shapes, plan)
    nc = bacc.Bacc("TRN2", target_bir_lowering=False, num_devices=1)
    build(nc, shapes, plan)
    r = run_bass_kernel_spmd(nc, [{f"in_{n}": v for n, v in arrays.items()}], core_ids=[0])
    return r.results[0]["out"].reshape(B, T, D)
```

```python
from contextlib import ExitStack

import numpy as np

import concourse.bass as bass
from concourse import mybir

F32 = mybir.dt.float32
BF16 = mybir.dt.bfloat16
I32 = mybir.dt.int32
U8 = mybir.dt.uint8
ACT = mybir.ActivationFunctionType
ALU = mybir.AluOpType
AXX = mybir.AxisListType.X

B, T, D = 16, 112, 256
S2 = 375
KD = D // 128
G = 4
GT = G * T
NG = B // G
HEADS, DK = 8, 128
TAPS = 4
HWID = 4 * KD * 128
XH, XD = 16, 16
CK = 125
NC = S2 // CK
EXPERTS = 8
HID = 1024
HT = HID // 128
NEG = -1.0e30
BUMP = 4096
LEVELS = 7
STAGES = 6
MAXIMA_FROM = 5


class Steps:

    def __init__(self, who, sem, plan):
        self.who, self.sem, self.plan = who, sem, plan
        self.frames = [{"name": who, "start": BUMP, "i": 0, "origin": BUMP, "n": 0, "pos": 0}]

    def open(self, name, i):
        top = self.frames[-1]
        n = self.plan.get((self.who, name), 0)
        start = top["origin"] + top["pos"]
        self.frames.append({"name": name, "start": start, "i": i, "origin": start + i * n, "n": n, "pos": 0})

    def close(self, trips):
        f = self.frames.pop()
        self.plan[(self.who, f["name"])] = f["pos"]
        self.frames[-1]["pos"] += trips * f["pos"]

    def do(self, ins, name=None):
        f = self.frames[-1]
        f["pos"] += 1
        if name:
            self.plan[(self.who, f["name"], name)] = f["pos"]
        ins.then_inc(self.sem, 1)
        return ins

    def at(self, name, ago=0):
        for f in reversed(self.frames):
            if (self.who, f["name"], name) in self.plan:
                on = self.plan[(self.who, f["name"], name)] - ago * f["n"]
                return self.sem, f["origin"] + on, f["i"], f["n"], f["start"] + on
        return self.sem, self.frames[0]["origin"]

    def all(self):
        f = self.frames[-1]
        return self.sem, f["origin"] + f["pos"]


def latest(points):
    kept = []
    for point in points:
        for n, other in enumerate(kept):
            if len(point) > 2 and len(other) > 2 and point[0] is other[0] and point[2] is other[2]:
                if point[4] > other[4]:
                    kept[n] = point
                break
        else:
            kept.append(point)
    return kept


def after(eng, *points):
    for point in latest(points):
        eng.wait_ge(point[0], point[1])


def decoder(nc, a, out, plan):
    pe, act, dve, pool, sp = nc.tensor, nc.scalar, nc.vector, nc.gpsimd, nc.sync
    with ExitStack() as ctx:
        def sb(name, shape, dt=F32):
            return ctx.enter_context(nc.sbuf_tensor(name, shape, dt))

        def sem(name):
            return ctx.enter_context(nc.semaphore(name))

        x = sb("x", [T, B, D])
        ident = sb("ident", [128, 128])
        ident_bf = sb("ident_bf", [128, 128], BF16)
        before = sb("before", [T, T])
        upto = sb("upto", [T, T])
        minus_strict = sb("minus_strict", [T, T])
        causal_neg = sb("causal_neg", [T, T])
        rank = sb("rank", [T, G * EXPERTS])
        minus_half = sb("minus_half", [T, G])

        head_w = sb("head_w", [128, HWID + 3 * TAPS])
        ba_w = sb("ba_w", [128, KD, 2 * HEADS])
        dt_bias = sb("dt_bias", [T, HEADS])
        decay = sb("decay", [T, HEADS])
        norm_w = sb("norm_w", [128, 1])
        gdn_out_w = sb("gdn_out_w", [128, HEADS + 1, D])
        xw = [{n: sb(f"x{n}{l}", [128, KD, D]) for n in ("q", "k", "v", "o")} for l in range(2)]
        xb_row = [{n: sb(f"x{n}_bias{l}", [128, D]) for n in (("o",), ("v", "o"))[l]} for l in range(2)]
        xb_col = sb("xb_col", [128, 2, KD])
        gate_w = sb("gate_w", [128, KD, EXPERTS])
        gate_b = sb("gate_b", [T, EXPERTS])
        expert_w = sb("expert_w", [128, KD, EXPERTS * D])
        expert_b = sb("expert_b", [EXPERTS, D])
        attn_w = sb("attn_w", [128, KD, 3 * D])
        w12 = sb("w12", [128, 2, KD, HID])
        hw = [sb(f"h{n}_w", [128, HT, HID]) for n in (1, 2)]
        w3 = sb("w3", [128, HT, D])
        hid_s = sb("hid_s", [128, 4, HT])
        w3_s = sb("w3_s", [T, D])

        stats = sb("stats", [T, G, 6])
        mean_var = sb("mean_var", [T, G, 2])
        var_eps = sb("var_eps", [T, G])
        rstd = sb("rstd", [T, G])
        carrier = sb("carrier", [T, 1])
        xn = sb("xn", [T, G, D])
        xT = sb("xT", [128, KD, GT])
        big_a = sb("big_a", [128, HT, GT])
        big_b = sb("big_b", [128, HT, GT])
        silu = sb("silu", [128, 2, GT])
        small = sb("small", [T, 16, G * EXPERTS])
        soft = sb("soft", [T, G, T])
        soft_max = sb("soft_max", [T, 4, G])

        ps = ctx.enter_context(nc.psum_tensor("ps", [128, 8, 512], F32))

        PE, AC, DV, PL = (Steps(n, sem(f"s_{n}"), plan) for n in ("pe", "act", "dve", "pool"))
        for eng, st in ((pe, PE), (act, AC), (dve, DV), (pool, PL)):
            eng.sem_inc(st.sem, BUMP)
        s_x, s_const, s_headw, s_ctx, s_out = (sem(n) for n in ("s_x", "s_const", "s_headw", "s_ctx", "s_out"))
        s_mask = sem("s_mask")
        s_hw = sem("s_hw")

        fresh = [0]

        def loop(name, n):
            class L:
                def __enter__(self):
                    self.c = nc.Fori(0, n)
                    self.i = self.c.__enter__()
                    for st in (PE, AC, DV, PL):
                        st.open(name, self.i)
                    return self.i

                def __exit__(self, *e):
                    for st in (PE, AC, DV, PL):
                        st.close(n)
                    return self.c.__exit__(*e)
            return L()

        def after_sp(*points):
            for sem, value, *parts in latest(points):
                if parts and not isinstance(parts[0], int) and isinstance(parts[2], int):
                    i, n, rest = parts
                    fresh[0] += 1
                    value = (i + fresh[0]) * n + (rest - fresh[0] * n)
                sp.wait_ge(sem, value)

        def load(dst, name, s, eng=sp):
            eng.dma_start(dst, a[name]).then_inc(s, 16)

        sp.dma_start(x[:, :, :], a["x"].rearrange("b t d -> t b d")).then_inc(s_x, 16)
        consts = [(ident[:, :], "ident"), (before[:, :], "before"), (upto[:, :], "upto"),
                  (minus_strict[:, :], "minus_strict"), (causal_neg[:, :], "causal_neg"),
                  (rank[:, :], "rank"), (ba_w[:, :, :], "ba_w"), (dt_bias[:, :], "dt_bias"), (decay[:, :], "A_log"),
                  (norm_w[:, :], "norm_w"), (gdn_out_w[:, :, :], "gdn_out_w")]
        for dst, name in consts:
            load(dst, name, s_const)
        weights = {}
        for l in range(2):
            weights[f"x{l}"] = [(xw[l][n][:, :, :], f"x{l}_W{n}") for n in "qkvo"] + \
                               [(t[:, :], f"x{l}_b{n}") for n, t in xb_row[l].items()]
        weights["x1"].append((xb_col[:, :, :], "x1_bqk"))
        weights["moe"] = [(gate_w[:, :, :], "gate_w"), (gate_b[:, :], "gate_b"), (expert_w[:, :, :], "expert_w"),
                          (expert_b[:, :], "expert_b")]
        weights["attn"] = [(attn_w[:, :, :], "attn_w")]
        weights["ffn"] = [(w12[:, :, :, :], "w12"), (w3[:, :, :], "w3"), (hid_s[:, :, :], "hid_s"), (w3_s[:, :], "w3_s")]
        s_w = {}
        for stage in ("x0", "moe", "attn", "x1", "ffn"):
            s_w[stage] = (sem(f"s_w_{stage}"), 16 * len(weights[stage]))
            for dst, name in weights[stage]:
                load(dst, name, s_w[stage][0], act)

        consts_in = (s_const, 16 * len(consts))
        for eng in (pe, act, dve, pool):
            after(eng, consts_in)
        after(dve, (s_x, 16))
        PL.do(pool.memset(minus_half[:, :], -0.5), "minus_half")
        DV.do(dve.tensor_copy(ident_bf[:, :], ident[:, :]))
        DV.do(dve.tensor_scalar(norm_w[:, :], norm_w[:, :], 0.5, None, ALU.mult))
        AC.do(act.activation(decay[:, :], decay[:, :], ACT.Exp), "decay")
        for eng in (pe, act, dve, pool):
            after(eng, PL.all(), DV.all(), AC.all())

        def layernorm(seqs, first, cols):
            after(dve, DV.all(), PE.all())
            for j in range(seqs):
                DV.do(dve.bn_stats(stats[:, j, :], x[:, first + j, :]))
            after(dve, DV.all())
            DV.do(dve.memset(carrier[:, :], 0.0))
            for j in range(seqs):
                DV.do(dve.bn_aggr(mean_var[:, j, :], stats[:, j, :]))
            after(dve, DV.all())
            DV.do(dve.tensor_scalar(var_eps[:, 0:seqs], mean_var[:, 0:seqs, 1], 1e-5, None, ALU.add), "ln_var")
            after(pool, DV.at("ln_var"))
            PL.do(pool.tensor_tensor(rstd[:, 0:seqs], var_eps[:, 0:seqs], minus_half[:, 0:seqs], ALU.pow), "ln_rstd")
            after(dve, PL.at("ln_rstd"))
            for j in range(seqs):
                DV.do(dve.tensor_scalar(xn[:, j, :], x[:, first + j, :], mean_var[:, j, 0:1], rstd[:, j:j + 1],
                                        ALU.subtract, ALU.mult), "ln_xn")
            after(pe, DV.at("ln_xn"), AC.all())
            for k in range(KD):
                for j in range(seqs):
                    last = pe.transpose(ps[:, k, j * T:(j + 1) * T], xn[:, j, k * 128:(k + 1) * 128], ident[0:T, 0:T])
                PE.do(last, f"ln_T{k}")
            after(act, PE.at("ln_T0"))
            AC.do(act.activation(xT[:, 0, 0:cols], ps[:, 0, 0:cols], ACT.Copy), "ln_done0")
            after(dve, PE.at("ln_T1"))
            DV.do(dve.tensor_copy(xT[:, 1, 0:cols], ps[:, 1, 0:cols]), "ln_done1")
            after(pe, AC.at("ln_done0"), DV.at("ln_done1"))

        def p3(ap):
            return ap.rearrange("p (g t) -> p g t", g=G)

        late = hw[1][:, :, :].rearrange("p a b -> p (a b)")
        gdn_xT = late[:, 0:NG * KD * GT].rearrange("p (g k t) -> p g k t", g=NG, k=KD)
        spare = late[0:T, NG * KD * GT:]
        W0, W = (spare[:, n * G * DK:(n + 1) * G * DK] for n in range(2))
        On = xn[:, 0:2, :].rearrange("p a b -> p (a b)")
        beta_decay = small[:, 0:9, :].rearrange("p a b -> p (a b)").rearrange("p (n h g j) -> p n h g j", n=2, g=NG, j=G)
        here = sb("here", [T, 2, G])
        cum_l = soft[:, :, :]
        gamma = big_a[0:T, 1, :]
        gam_s, gam_i = p3(big_a[0:T, 2, :]), p3(big_a[0:T, 3, :])
        qT, kT, vT, zT = (big_b[:, n, :] for n in range(4))
        oT = big_b[:, 4, :]
        sz_next, sz = big_b[:, 5, :], big_b[:, 6, :]
        N0 = big_b[0:T, 7, :]
        NT = [big_a[0:T, 4, :], big_a[0:T, 5, :]]
        MM = big_a[0:T, 6, :]
        QG_next, QG = big_a[0:T, 0, :], big_a[0:T, 7, :]

        DV.do(dve.memset(beta_decay[:, :, HEADS, :, :], 0.0))
        DV.do(dve.memset(sz, 0.0))
        DV.do(dve.memset(ps[:, 6, :], 0.0))
        with loop("gdn", NG) as g:
            layernorm(G, g * G, GT)
            after(act, AC.at("ln_done0"), DV.at("ln_done1"))
            AC.do(act.activation(gdn_xT[:, g, :, :], xT[:, :, :], ACT.Copy), "keep")
            for j in range(G):
                for k in range(KD):
                    last = pe.matmul(ps[0:T, 2, j * 16:(j + 1) * 16], xT[:, k, j * T:(j + 1) * T], ba_w[:, k, :],
                                     start=(k == 0), stop=(k == KD - 1))
            PE.do(last, "ba")
            ba = ps[0:T, 2, 0:G * 16].rearrange("p (g c) -> p g c", g=G)
            y, t1, t2, bb = (small[:, n, :].rearrange("p (g c) -> p g c", g=G) for n in (9, 10, 11, 12))
            after(dve, PE.at("ba"))
            DV.do(dve.tensor_tensor(y, ba[:, :, HEADS:], dt_bias[:, :].unsqueeze(1).to_broadcast([T, G, HEADS]), ALU.add))
            DV.do(dve.tensor_copy(bb, ba[:, :, 0:HEADS]), "ba_in")
            after(act, DV.at("ba_in"))
            AC.do(act.activation(t1, y, ACT.Abs), "sp1")
            after(act, AC.at("sp1"))
            AC.do(act.activation(t1, t1, ACT.Exp, scale=-1.0), "sp2")
            AC.do(act.activation(bb, bb, ACT.Exp, scale=-1.0), "sig")
            after(act, AC.at("sp2"))
            AC.do(act.activation(t1, t1, ACT.Ln, bias=1.0), "sp3")
            after(dve, AC.at("sp3"))
            DV.do(dve.scalar_tensor_tensor(t2, y, 0.0, t1, ALU.max, ALU.add))
            DV.do(dve.tensor_scalar(bb, bb, 1.0, None, ALU.add))
            after(dve, DV.all())
            DV.do(dve.reciprocal(t1, bb))
            after(dve, DV.all())
            DV.do(dve.tensor_copy(beta_decay[:, 0, 0:HEADS, g, :], t1.rearrange("p g c -> p c g")))
            DV.do(dve.scalar_tensor_tensor(beta_decay[:, 1, 0:HEADS, g, :], t2.rearrange("p g c -> p c g"), -1.0,
                                           decay[:, :].unsqueeze(2).to_broadcast([T, HEADS, G]), ALU.mult, ALU.mult),
                  "beta_decay")

        w4 = head_w[:, 0:HWID].rearrange("p (n k c) -> p n k c", n=4, k=KD)
        taps = head_w[:, HWID:].rearrange("p (n j) -> p n j", j=TAPS)
        per_unit = [slice(j * T, (j + 1) * T) for j in range(G)]

        def unit(g, h, run=True):
            last_g, back = (g - 1) % NG, 1 if g == 0 else 0
            gn, hn = (g + 1) % NG, h if g < NG - 1 else h + 1

            def was(st, n):
                return st.at(f"{n}_{last_g}", back)

            def now(st, n):
                return st.at(f"{n}_{g}")

            def other_taps(n, dst):
                for s in range(1, TAPS):
                    DV.do(dve.scalar_tensor_tensor(p3(dst)[:, :, s:], p3(ps[:, 1 + n, 0:GT])[:, :, 0:T - s],
                                                   taps[:, n, TAPS - 1 - s:TAPS - s], p3(dst)[:, :, s:],
                                                   ALU.mult, ALU.add), f"conv{n}_{g}")
                    after(dve, now(DV, f"conv{n}"))

            def proj(n):
                for k in range(KD):
                    last = pe.matmul(ps[:, 1 + n, 0:GT], w4[:, n, k, :], gdn_xT[:, gn, k, :], start=(k == 0), stop=(k == KD - 1))
                PE.do(last, f"proj{n}_{g}")

            def tap(n, dst):
                after(act, now(PE, f"proj{n}"))
                AC.do(act.activation(dst, ps[:, 1 + n, 0:GT], ACT.Copy, scale=taps[:, n, TAPS - 1:TAPS]), f"tap{n}_{g}")

            def front():
                after(pe, (s_headw, (hn + 1) * 16), was(DV, "N0"))
                proj(1)
                after(act, (s_headw, (hn + 1) * 16))
                tap(1, kT)
                yield
                after(dve, was(DV, "QG"))
                DV.do(dve.tensor_copy(here[:, :, :], beta_decay[:, :, hn, gn, :]), f"here_{g}")
                after(dve, now(DV, "here"), was(PE, "logG"))
                DV.do(dve.tensor_tensor(cum_l, before[:, :].unsqueeze(1).to_broadcast([T, G, T]),
                                        here[:, 1, :].unsqueeze(2).to_broadcast([T, G, T]), ALU.mult), f"cum_l_{g}")
                after(dve, now(AC, "tap1"))
                other_taps(1, kT)
                yield
                after(pe, was(DV, "QG"))
                proj(0)
                tap(0, qT)
                yield
                after(dve, now(AC, "tap0"))
                other_taps(0, qT)
                yield
                after(pe, now(DV, "conv1"))
                for c in per_unit:
                    last = pe.matmul(ps[0:T, 2, c], kT[:, c], kT[:, c], start=True, stop=True)
                PE.do(last, f"kk_{g}")
                yield
                yield
                after(pe, was(AC, "W0"))
                proj(2)
                tap(2, vT)
                yield
                after(dve, now(AC, "tap2"))
                other_taps(2, vT)
                yield
                after(pe, now(DV, "x"))
                proj(3)
                if g == NG - 2:
                    after_sp(now(PE, "proj3"), now(DV, "conv2"))
                    sp.dma_start(head_w[:, :], a["head_w"][h + 1]).then_inc(s_headw, 16)
                after(act, now(PE, "proj3"))
                AC.do(act.activation(zT, ps[:, 4, 0:GT], ACT.Tanh, scale=0.5), f"tanh_{g}")
                yield
                after(dve, now(AC, "tanh"), now(AC, "sz"))
                DV.do(dve.scalar_tensor_tensor(sz_next, zT, 1.0, ps[:, 4, 0:GT], ALU.add, ALU.mult), f"sz_next_{g}")
                yield
                after(pe, now(DV, "cum_l"))
                for j, c in enumerate(per_unit):
                    last = pe.matmul(ps[0:T, 6, c], cum_l[:, j, :], upto[:, :], start=True, stop=True)
                PE.do(last, f"logG_{g}")
                after(act, now(PE, "logG"))
                AC.do(act.activation(gamma, ps[0:T, 6, 0:GT], ACT.Exp), f"gamma_{g}")
                yield
                after(pool, now(AC, "gamma"))
                PL.do(pool.tensor_tensor(gam_s, p3(gamma), minus_strict[:, :].unsqueeze(1).to_broadcast([T, G, T]), ALU.mult),
                      f"gam_s_{g}")
                PL.do(pool.tensor_tensor(gam_i, p3(gamma), upto[:, :].unsqueeze(1).to_broadcast([T, G, T]), ALU.mult),
                      f"gam_i_{g}")
                yield
                after(pe, now(DV, "conv0"))
                for c in per_unit:
                    last = pe.matmul(ps[0:T, 1, c], kT[:, c], qT[:, c], start=True, stop=True)
                PE.do(last, f"kq_{g}")
                after(dve, now(PE, "kk"), now(PL, "gam_s"))
                for j, c in enumerate(per_unit):
                    DV.do(dve.scalar_tensor_tensor(N0[:, c], ps[0:T, 2, c], here[:, 0, j:j + 1], gam_s[:, j, :],
                                                   ALU.mult, ALU.mult), f"N0_{g}")
                yield
                after(pe, now(DV, "conv2"))
                for j, c in enumerate(per_unit):
                    last = pe.transpose(ps[0:T, 3, j * DK:(j + 1) * DK], vT[:, c], ident[:, :])
                PE.do(last, f"vtok_{g}")
                after(act, now(PE, "vtok"), now(DV, "W1"))
                AC.do(act.activation(W0, ps[0:T, 3, 0:G * DK], ACT.Copy), f"W0_{g}")
                after(dve, now(PE, "kq"), now(PL, "gam_i"), now(AC, "QG"))
                for j, c in enumerate(per_unit):
                    DV.do(dve.scalar_tensor_tensor(QG_next[:, c], ps[0:T, 1, c], here[:, 0, j:j + 1], gam_i[:, j, :],
                                                   ALU.mult, ALU.mult), f"QG_{g}")
                yield

            def levels():
                for lev in range(LEVELS):
                    N = NT[lev % 2] if lev else N0
                    Wsrc = W if lev else W0
                    if lev < LEVELS - 1:
                        after(pe, now(AC, f"N{lev}") if lev else was(DV, "N0"))
                        after(pe, now(AC, f"M{lev - 1}") if lev else was(AC, f"M{LEVELS - 2}"))
                        for c in per_unit:
                            last = pe.transpose(ps[0:T, 0, c], N[:, c], ident[0:T, 0:T])
                        PE.do(last, f"M{lev}T_{g}")
                        after(act, now(PE, f"M{lev}T"))
                        AC.do(act.activation(MM, ps[0:T, 0, 0:GT], ACT.Copy), f"M{lev}_{g}")
                    yield
                    if lev < LEVELS - 1:
                        after(pe, now(AC, f"M{lev}"))
                        for c in per_unit:
                            last = pe.matmul(ps[0:T, 5, c], MM[:, c], N[:, c], start=True, stop=True)
                        PE.do(last, f"N{lev + 1}ps_{g}")
                        after(act, now(PE, f"N{lev + 1}ps"))
                        AC.do(act.activation(NT[(lev + 1) % 2], ps[0:T, 5, 0:GT], ACT.Copy), f"N{lev + 1}_{g}")
                    if lev:
                        after(pe, now(DV, f"W{lev}"), now(AC, f"N{lev}"))
                    else:
                        after(pe, was(AC, "W0"), was(DV, f"W{LEVELS}"))
                    for j, c in enumerate(per_unit):
                        last = pe.matmul(ps[0:T, 7, j * DK:(j + 1) * DK], N[:, c], Wsrc[:, j * DK:(j + 1) * DK],
                                         start=True, stop=True)
                    PE.do(last, f"PW{lev}_{g}")
                    after(dve, now(PE, f"PW{lev}"))
                    DV.do(dve.tensor_tensor(W, Wsrc, ps[0:T, 7, 0:G * DK], ALU.add), f"W{lev + 1}_{g}")
                    if lev == 0:
                        after(act, was(DV, "QG"), was(PE, "O"))
                        AC.do(act.activation(QG, QG_next, ACT.Copy), f"QG_{g}")
                    yield
                after(pe, now(DV, f"W{LEVELS}"), now(AC, "QG"), now(AC, "gamma"))
                for j, c in enumerate(per_unit):
                    last = pe.matmul(ps[0:T, 6, j * DK:(j + 1) * DK], QG[:, c], W[:, j * DK:(j + 1) * DK],
                                     start=True, stop=True)
                PE.do(last, f"O_{g}")
                yield

            def tail():
                after(act, was(PE, "O"))
                for j in range(G):
                    AC.do(act.activation(On[:, j * DK:(j + 1) * DK], ps[0:T, 6, j * DK:(j + 1) * DK], ACT.Square,
                                         accum_out=var_eps[:, j:j + 1]), f"squares_{g}")
                yield
                after(dve, now(AC, "squares"))
                DV.do(dve.tensor_scalar(var_eps[:, :], var_eps[:, :], 1.0 / DK, 1e-6, ALU.mult, ALU.add), f"o_var_{g}")
                after(pool, now(DV, "o_var"))
                PL.do(pool.tensor_tensor(rstd[:, :], var_eps[:, :], minus_half[:, :], ALU.pow), f"o_rstd_{g}")
                after(dve, now(PL, "o_rstd"))
                DV.do(dve.tensor_tensor(On.rearrange("p (g d) -> p g d", g=G),
                                        ps[0:T, 6, 0:G * DK].rearrange("p (g d) -> p g d", g=G),
                                        rstd[:, :].unsqueeze(2).to_broadcast([T, G, DK]), ALU.mult), f"On_{g}")
                yield
                after(pe, now(DV, "On"), was(DV, "sz_next"))
                for j in range(G):
                    last = pe.transpose(ps[:, 4, j * T:(j + 1) * T], On[:, j * DK:(j + 1) * DK], ident[0:T, 0:T])
                PE.do(last, f"oT_{g}")
                after(dve, now(PE, "oT"))
                DV.do(dve.scalar_tensor_tensor(oT, ps[:, 4, 0:GT], norm_w[:, 0:1], sz, ALU.mult, ALU.mult), f"gated_{g}")
                yield
                yield
                after(pe, now(DV, "gated"))
                for j in range(G):
                    last = pe.matmul(ps[0:T, (6, 4)[j // 2], (j % 2) * D:(j % 2 + 1) * D], oT[:, j * T:(j + 1) * T],
                                     gdn_out_w[:, h + (1 if g else 0), :], start=True, stop=True)
                PE.do(last, f"out_{g}")
                yield
                after(act, now(DV, "gated"), was(DV, "sz_next"))
                AC.do(act.activation(sz, sz_next, ACT.Copy), f"sz_{g}")
                after(dve, now(PE, "out"))
                for n in range(G // 2):
                    xs = x[:, last_g * G + 2 * n:last_g * G + 2 * n + 2, :]
                    DV.do(dve.tensor_tensor(xs, xs, ps[0:T, (6, 4)[n], :].rearrange("p (g d) -> p g d", g=2), ALU.add), f"x_{g}")
                yield

            return front, levels, tail

        def run_unit(g, h, with_front=True, with_levels=True, with_tail=True):
            front, levels, tail = unit(g, h)
            parts = [f() if on else iter(()) for f, on in ((levels, with_levels), (front, with_front), (tail, with_tail))]
            if with_levels:
                for n in range(2 * LEVELS):
                    lev, fr, ta = parts
                    next(lev, None)
                    for part in (fr, ta) if n % 2 == 0 else (ta, fr):
                        next(part, None)
            for part in parts:
                for _ in part:
                    pass

        def everyone():
            points = [st.all() for st in (PE, AC, DV, PL)]
            for eng in (pe, act, dve, pool, sp):
                after(eng, *points)

        sp.dma_start(head_w[:, :], a["head_w"][0]).then_inc(s_headw, 16)
        everyone()
        for st in (PE, AC, DV, PL):
            st.open("gdn_first", 0)
        run_unit(NG - 1, -1, with_levels=False, with_tail=False)
        for st in (PE, AC, DV, PL):
            st.close(1)
        everyone()
        with loop("heads", HEADS) as h:
            for g in range(NG):
                run_unit(g, h)
        everyone()
        for st in (PE, AC, DV, PL):
            st.open("gdn_last", 0)
        run_unit(0, HEADS, with_front=False, with_levels=False)
        for st in (PE, AC, DV, PL):
            st.close(1)
        everyone()

        KEY_PART = (0, 0, 0, 1, 1, 1, 2, 2)
        QRY_PART = (0, 1, 2, 0, 1, 2, 0, 1)
        late1 = hw[0][:, :, :].rearrange("p a b -> p (a b)")
        taken = [0, 0]

        def room(n, where, dt=F32, parts=128):
            words = n if dt == F32 or dt == I32 else (n + 1) // 2
            words += words % 2
            at = taken[where]
            taken[where] += words
            assert taken[where] <= HT * HID
            t = (late, late1)[where][0:parts, at:at + words]
            return t if dt == F32 else t.bitcast(dt)[:, 0:n]

        def heads_of(ap, n):
            return ap.rearrange("p (h t) -> p h t", h=XH)

        Kst = [heads_of(room(XH * S2, 0, BF16), S2) for _ in range(2)]
        Qst = [heads_of(room(XH * T, 0, BF16), T) for _ in range(2)]
        Vx = [room(NC * XH * 32, 1, parts=CK).rearrange("p (c h d) -> p c h d", c=NC, h=XH) for _ in range(2)]
        ctxT = room(KD * S2, 1).rearrange("p (k t) -> p k t", k=KD)
        ctxV = room(KD * S2, 1).rearrange("p (k t) -> p k t", k=KD)
        k_rest = big_a[:, 0:2, :].rearrange("p a b -> p (a b)")[:, 0:KD * S2].rearrange("p (k t) -> p k t", k=KD)
        k_part = [room(KD * S2, 1, BF16).rearrange("p (k t) -> p k t", k=KD) for _ in range(3)]
        q_full = room(KD * T, 1)
        q_part = [room(KD * T, 1, BF16) for _ in range(3)]
        PTx = [big_a[0:CK, 5 + n, 0:NC * T] for n in range(3)]
        maskT_raw = room(NC * T, 1, I32, CK)
        mask_raw = room(S2, 1, I32, T)
        maskT_raw8, mask_raw8 = (m.bitcast(U8)[:, 0:m.shape[1]] for m in (maskT_raw, mask_raw))
        mask_add = [room(S2, 1, BF16, T) for _ in range(2)]
        maskT_add = [room(NC * T, 1, BF16, CK) for _ in range(2)]
        nm = room(XH, 1, parts=T)
        nm_rest = room(XH, 1, parts=T)
        nm_part = room(128, 1, BF16, T)
        nmT = [room(T, 1, BF16, 3 * XH) for _ in range(2)]
        oa = big_b[:, 0, :]
        on = big_b[0:T, 1, 0:D]
        onT = big_b[:, 2, 0:KD * T]
        inv = room(XH, 1, parts=T)
        sel_f = big_a[0:3 * XH, :, :].rearrange("p a b -> p (a b)")[:, 0:XH * CK]
        sel = big_b[0:3 * XH, 3:6, :].rearrange("p a b -> p (a b)")[:, 0:XH * CK // 2].bitcast(BF16).rearrange("p (h t) -> p h t", h=XH)
        k_dram = nc.dram_tensor("k_parts", (2, 3, KD, 128, S2), BF16).ap()
        q_dram = nc.dram_tensor("q_parts", (2, 3, KD, 128, T), BF16).ap()
        s_kw, s_kst, s_qw, s_qst, s_sel, s_ctxv = (sem(n) for n in ("s_kw", "s_kst", "s_qw", "s_qst", "s_sel", "s_ctxv"))
        DV.do(dve.memset(nm_part, 0.0), "nm_part")
        for p in range(2):
            DV.do(dve.memset(Vx[p][:, :, :, XD:], 1.0), "ones")

        def cross_attention(l):
            w, name, done = xw[l], f"x{l}", l * B
            for eng in (pe, act, dve):
                after(eng, s_w[name])
            raw = (mask_raw, maskT_raw) if l == 0 else (mask_raw8, maskT_raw8)

            def half(h, i, prev_at, c_at, nxt_at, nxt2_at):
                q, back = 1 - h, 1 - h
                prev, c, nxt, nxt2 = (None if at is None else 2 * i + at for at in (prev_at, c_at, nxt_at, nxt2_at))

                def loads(sem, at, each):
                    rest = (done + at + 1) * each
                    return sem, 2 * i * each + rest, i, 2 * each, rest

                def was(st, n):
                    return st.at(f"{n}_{1 - h}", back)

                def now(st, n):
                    return st.at(f"{n}_{h}")

                def fetch():
                    if nxt2 is not None:
                        after_sp(was(PE, "k_proj1"))
                        sp.dma_start(ctxT, a["ctxT"][nxt2]).then_inc(s_ctx, 16)
                    if nxt is not None:
                        after_sp(was(PE, "v_proj"), was(DV, "mask"))
                        sp.dma_start(ctxV, a["ctxT"][nxt]).then_inc(s_ctxv, 16)
                        sp.dma_start(raw[0], a[f"mask{l}"][nxt]).then_inc(s_mask, 16)
                        sp.dma_start(raw[1].rearrange("p (c t) -> p c t", c=NC), a[f"maskT{l}"][nxt]).then_inc(s_mask, 16)
                        after_sp(was(PE, "ST15"), loads(s_kw, nxt_at, 48), loads(s_qw, nxt_at, 48))
                        for r, n in enumerate(KEY_PART):
                            sp.dma_start(Kst[q][16 * r:16 * r + 16, :, :],
                                         k_dram[q, n].rearrange("m (h d) t -> d (m h) t", d=XD)).then_inc(s_kst, 16)
                        for r, n in enumerate(QRY_PART):
                            sp.dma_start(Qst[q][16 * r:16 * r + 16, :, :],
                                         q_dram[q, n].rearrange("m (h d) t -> d (m h) t", d=XD)).then_inc(s_qst, 16)

                def prepare():
                    DV.do(dve.bn_stats(stats[:, 0, :], x[:, nxt2, :]), f"st_{h}")
                    after(dve, now(DV, "st"))
                    DV.do(dve.memset(carrier[:, :], 0.0))
                    DV.do(dve.bn_aggr(mean_var[:, 0, :], stats[:, 0, :]), f"mv_{h}")
                    after(dve, now(DV, "mv"))
                    DV.do(dve.tensor_scalar(var_eps[:, 0:1], mean_var[:, 0, 1:2], 1e-5, None, ALU.add), f"var_{h}")
                    after(pool, now(DV, "var"))
                    PL.do(pool.tensor_tensor(rstd[:, 0:1], var_eps[:, 0:1], minus_half[:, 0:1], ALU.pow), f"rstd_{h}")
                    after(pe, loads(s_ctx, nxt2_at, 16), was(DV, "V2"), was(DV, "k_r1"))
                    for m in range(KD):
                        for k in range(KD):
                            last = pe.matmul(ps[:, 5 + m, 0:S2], w["k"][:, k, m * 128:(m + 1) * 128], ctxT[:, k, :],
                                             start=(k == 0), stop=(k == KD - 1))
                        PE.do(last, f"k_proj{m}_{h}")
                    yield
                    after(dve, now(PL, "rstd"), was(PE, "xnT"))
                    DV.do(dve.tensor_scalar(xn[:, 0, :], x[:, nxt2, :], mean_var[:, 0, 0:1], rstd[:, 0:1],
                                            ALU.subtract, ALU.mult), f"xn_{h}")
                    after(act, loads(s_kw, nxt2_at - 1, 48))
                    for m in range(KD):
                        after(act, now(PE, f"k_proj{m}"))
                        if l == 0:
                            ins = act.activation(k_part[0][:, m, :], ps[:, 5 + m, 0:S2], ACT.Copy)
                        else:
                            ins = act.activation(k_part[0][:, m, :], ps[:, 5 + m, 0:S2], ACT.Identity,
                                                 bias=xb_col[:, 1, m:m + 1])
                        AC.do(ins, f"k_hi{m}_{h}")
                    for m in range(KD):
                        after(dve, now(AC, f"k_hi{m}"), was(PL, "k_lo"))
                        if l == 0:
                            ins = dve.tensor_tensor(k_rest[:, m, :], ps[:, 5 + m, 0:S2], k_part[0][:, m, :], ALU.subtract)
                        else:
                            ins = dve.scalar_tensor_tensor(k_rest[:, m, :], ps[:, 5 + m, 0:S2], xb_col[:, 1, m:m + 1],
                                                           k_part[0][:, m, :], ALU.add, ALU.subtract)
                        DV.do(ins, f"k_r{m}_{h}")
                    yield
                    yield
                    after(pe, now(DV, "k_r1"))
                    for k in range(KD):
                        last = pe.transpose(ps[:, 5, k * T:(k + 1) * T], xn[:, 0, k * 128:(k + 1) * 128], ident[0:T, 0:T])
                    PE.do(last, f"xnT_{h}")
                    after(act, now(PE, "xnT"))
                    AC.do(act.activation(xT[:, :, 0:T], ps[:, 5, 0:KD * T].rearrange("p (k t) -> p k t", k=KD), ACT.Copy),
                          f"xT_{h}")
                    after(act, now(DV, "k_r1"))
                    AC.do(act.activation(k_part[1], k_rest, ACT.Copy), f"k_mid_{h}")
                    after(pool, now(AC, "k_mid"))
                    PL.do(pool.tensor_tensor(k_part[2], k_rest, k_part[1], ALU.subtract), f"k_lo_{h}")
                    yield
                    yield
                    after(pe, now(AC, "xT"))
                    for m in range(KD):
                        for k in range(KD):
                            last = pe.matmul(ps[:, 6, m * T:(m + 1) * T], w["q"][:, k, m * 128:(m + 1) * 128], xT[:, k, 0:T],
                                             start=(k == 0), stop=(k == KD - 1))
                    PE.do(last, f"q_proj_{h}")
                    scale = 1.0 / 16 if l == 0 else 0.25
                    after(dve, now(PE, "q_proj"))
                    for m in range(KD):
                        dst, src = q_full[:, m * T:(m + 1) * T], ps[:, 6, m * T:(m + 1) * T]
                        if l == 0:
                            ins = dve.tensor_scalar(dst, src, scale, None, ALU.mult)
                        else:
                            ins = dve.tensor_scalar(dst, src, xb_col[:, 0, m:m + 1], scale, ALU.add, ALU.mult)
                        DV.do(ins, f"q_{h}")
                    after(dve, now(DV, "q"), loads(s_qw, nxt2_at - 1, 48))
                    DV.do(dve.tensor_copy(q_part[0], q_full), f"q_hi_{h}")
                    after(dve, now(DV, "q_hi"))
                    DV.do(dve.tensor_tensor(q_full, q_full, q_part[0], ALU.subtract), f"q_r_{h}")
                    after(dve, now(DV, "q_r"))
                    DV.do(dve.tensor_copy(q_part[1], q_full), f"q_mid_{h}")
                    after(dve, now(DV, "q_mid"))
                    DV.do(dve.tensor_tensor(q_part[2], q_full, q_part[1], ALU.subtract), f"q_lo_{h}")
                    read = [] if nxt2_at < 2 else [loads(s_kst, nxt2_at - 2, 128), loads(s_qst, nxt2_at - 2, 128)]
                    after_sp(now(PL, "k_lo"), *read)
                    for n in range(3):
                        sp.dma_start(k_dram[h, n].rearrange("m p t -> p m t"), k_part[n]).then_inc(s_kw, 16)
                    after_sp(now(DV, "q_lo"))
                    for n in range(3):
                        sp.dma_start(q_dram[h, n].rearrange("m p t -> p m t"),
                                     q_part[n].rearrange("p (m t) -> p m t", m=KD)).then_inc(s_qw, 16)
                    yield

                def values():
                    after(pe, loads(s_ctxv, nxt_at, 16), now(DV, "q"), now(AC, "xT"), *([] if nxt2 is not None else [was(DV, "q")]))
                    for c in range(NC):
                        for k in range(KD):
                            last = pe.matmul(ps[0:CK, 5 + c // 2, (c % 2) * D:(c % 2 + 1) * D], ctxV[:, k, c * CK:(c + 1) * CK],
                                             w["v"][:, k, :], start=(k == 0), stop=(k == KD - 1))
                        PE.do(last, "v_proj_%d" % h if c == NC - 1 else f"v{c}_{h}")
                        if c == 1:
                            yield
                    for c in range(NC):
                        after(dve, now(PE, "v1" if c < 2 else "v_proj"))
                        src = ps[0:CK, 5 + c // 2, (c % 2) * D:(c % 2 + 1) * D].rearrange("p (h d) -> p h d", h=XH)
                        dst = Vx[q][:, c, :, 0:XD]
                        if l == 0:
                            ins = dve.tensor_copy(dst, src)
                        else:
                            ins = dve.tensor_tensor(dst, src, xb_row[1]["v"][0:CK, :].rearrange("p (h d) -> p h d", h=XH),
                                                    ALU.add)
                        DV.do(ins, f"V{c}_{h}")
                    yield

                def masks():
                    after(dve, loads(s_mask, nxt_at, 32))
                    DV.do(dve.tensor_scalar(mask_add[q], raw[0], 0.0, NEG, ALU.is_equal, ALU.mult))
                    DV.do(dve.tensor_scalar(maskT_add[q], raw[1], 0.0, NEG, ALU.is_equal, ALU.mult), f"mask_{h}")

                def maxima():
                    for s in range(XH):
                        bank = 2 + s % 2
                        if s == 0:
                            after(pe, loads(s_kst, nxt_at, 128), loads(s_qst, nxt_at, 128), now(DV, "mask"), was(DV, "max15"))
                        if s >= 2:
                            after(pe, now(DV, f"max{s - 2}"))
                        pe.matmul(ps[0:T, bank, 0:S2], Qst[q][:, s, :], Kst[q][:, s, :], start=True, stop=False)
                        PE.do(pe.matmul(ps[0:T, bank, 0:S2], ident_bf[0:T, 0:T], mask_add[q], start=False, stop=True),
                              f"S{s}_{h}")
                        after(dve, now(PE, f"S{s}"))
                        DV.do(dve.tensor_reduce(nm[:, s:s + 1], ps[0:T, bank, 0:S2], AXX, ALU.max, negate=True),
                              f"max{s}_{h}")
                        yield
                    after(dve, now(DV, "max15"), was(PE, "nmT"))
                    DV.do(dve.tensor_copy(nm_part[:, 0:XH], nm), f"nm1_{h}")
                    after(dve, now(DV, "nm1"))
                    DV.do(dve.tensor_tensor(nm_rest, nm, nm_part[:, 0:XH], ALU.subtract), f"nm2_{h}")
                    after(dve, now(DV, "nm2"))
                    DV.do(dve.tensor_copy(nm_part[:, XH:2 * XH], nm_rest), f"nm3_{h}")
                    after(dve, now(DV, "nm3"))
                    DV.do(dve.tensor_tensor(nm_part[:, 2 * XH:3 * XH], nm_rest, nm_part[:, XH:2 * XH], ALU.subtract), f"nm4_{h}")
                    yield
                    yield
                    yield
                    after(pe, now(DV, "nm4"))
                    nmT_ps = ps[:, 2, 0:T // 2].bitcast(BF16)
                    PE.do(pe.transpose(nmT_ps, nm_part, ident_bf[0:T, 0:T]), f"nmT_{h}")
                    after(dve, now(PE, "nmT"))
                    DV.do(dve.tensor_copy(nmT[q], nmT_ps[0:3 * XH, :]), f"nmTsb_{h}")
                    yield

                def attend():
                    p = h
                    for s in range(XH + 1):
                        if s < XH:
                            out_ps = ps[0:CK, s % 2, 0:NC * T]
                            if s == 0:
                                after(pe, was(DV, "nmTsb"), was(DV, "V2"))
                            after(pe, now(AC, f"exp{s - 2}") if s >= 2 else was(AC, f"exp{XH - 2 + s}"))
                            for k in range(NC):
                                pe.matmul(out_ps[:, k * T:(k + 1) * T], Kst[p][:, s, k * CK:(k + 1) * CK], Qst[p][:, s, :],
                                          start=(k == 0), stop=False, skip_group_check=True)
                            pe.matmul(out_ps, ident_bf[0:CK, 0:CK], maskT_add[p], start=False, stop=False,
                                      skip_group_check=True)
                            PE.do(pe.matmul(out_ps.rearrange("p (c t) -> p c t", c=NC), sel[:, s, :],
                                            nmT[p].unsqueeze(1).to_broadcast([3 * XH, NC, T]), start=False, stop=True,
                                            skip_group_check=True), f"ST{s}_{h}")
                            after(act, now(PE, f"ST{s}"))
                            after(act, now(PE, f"PV{s - 3}") if s >= 3 else was(PE, f"PV{XH - 3 + s}"))
                            AC.do(act.activation(PTx[s % 3], out_ps, ACT.Exp), f"exp{s}_{h}")
                        if s >= 1:
                            e = s - 1
                            after(pe, now(AC, f"exp{e}"))
                            if e == 0:
                                after(pe, now(DV, "oa"))
                            for k in range(NC):
                                last = pe.matmul(ps[32 * (e % 4):32 * (e % 4) + 32, 4, e // 4 * T:(e // 4 + 1) * T],
                                                 Vx[p][:, k, e, :], PTx[e % 3][:, k * T:(k + 1) * T],
                                                 start=(k == 0), stop=(k == NC - 1))
                            PE.do(last, f"PV{e}_{h}")
                        yield

                def finish():
                    after(dve, was(PE, "PV15"), was(PE, "oT"))
                    DV.do(dve.tensor_copy(oa, ps[:, 4, 0:GT]), f"oa_{h}")
                    yield
                    after(pe, now(DV, "oa"), was(DV, "x"))
                    for n in range(4):
                        last = pe.transpose(ps[0:T, 7, n * 128:(n + 1) * 128], oa[:, n * T:(n + 1) * T], ident[:, :])
                    PE.do(last, f"oT_{h}")
                    yield
                    o_ps = ps[0:T, 7, :].rearrange("p (h d) -> p h d", h=XH)
                    after(dve, now(PE, "oT"))
                    DV.do(dve.reciprocal(inv, o_ps[:, :, XD]), f"inv_{h}")
                    after(dve, now(DV, "inv"), was(PE, "onT_ps"))
                    DV.do(dve.tensor_tensor(on.rearrange("p (h d) -> p h d", h=XH), o_ps[:, :, 0:XD],
                                            inv.unsqueeze(2).to_broadcast([T, XH, XD]), ALU.mult), f"on_{h}")
                    DV.do(dve.tensor_tensor(x[:, prev, :], x[:, prev, :], xb_row[l]["o"][0:T, :], ALU.add), f"xb_{h}")
                    after(pe, now(DV, "on"))
                    for k in range(KD):
                        last = pe.transpose(ps[:, 7, k * T:(k + 1) * T], on[:, k * 128:(k + 1) * 128], ident[0:T, 0:T])
                    PE.do(last, f"onT_ps_{h}")
                    after(act, now(PE, "onT_ps"), was(PE, "o_proj"))
                    AC.do(act.activation(onT, ps[:, 7, 0:KD * T], ACT.Copy), f"onT_{h}")
                    yield
                    after(pe, now(AC, "onT"))
                    for k in range(KD):
                        last = pe.matmul(ps[0:T, 7, 0:D], onT[:, k * T:(k + 1) * T], w["o"][:, k, :],
                                         start=(k == 0), stop=(k == KD - 1))
                    PE.do(last, f"o_proj_{h}")
                    after(dve, now(PE, "o_proj"), now(DV, "xb"))
                    DV.do(dve.tensor_tensor(x[:, prev, :], x[:, prev, :], ps[0:T, 7, 0:D], ALU.add), f"x_{h}")
                    yield

                fetch()
                prep = prepare() if nxt2 is not None else iter(())
                vals = values() if nxt is not None else iter(())
                maxs = maxima() if nxt is not None else iter(())
                main = attend() if c is not None else iter(())
                end = finish() if prev is not None else iter(())
                next(end, None)
                if nxt is not None:
                    masks()
                for step, _ in enumerate(main):
                    if next(prep, 0) == 0:
                        next(vals, None)
                    if step >= MAXIMA_FROM:
                        next(maxs, None)
                        next(maxs, None)
                    if step % 2:
                        next(end, None)
                for rest in (prep, vals, maxs, end):
                    for _ in rest:
                        pass

            everyone()
            sp.dma_start(sel_f, a["sel"]).then_inc(s_sel, 16)
            after(dve, (s_sel, (l + 1) * 16))
            DV.do(dve.tensor_copy(sel, sel_f.rearrange("p (h t) -> p h t", h=XH)), "sel")
            after(dve, DV.all())
            def once(which, *halves):
                for st in (PE, AC, DV, PL):
                    st.open(f"{name}_{which}", 0)
                for h, sequences in enumerate(halves):
                    half(h, 0, *sequences)
                for st in (PE, AC, DV, PL):
                    st.close(1)
                everyone()

            once("start", (None, None, None, 0), (None, None, 0, 1))
            once("first", (None, 0, 1, 2), (0, 1, 2, 3))
            with loop(name, B // 2 - 2) as i:
                half(0, i, 1, 2, 3, 4)
                half(1, i, 2, 3, 4, 5)
            everyone()
            once("last", (B - 3, B - 2, B - 1, None), (B - 2, B - 1, None, None))
            once("end", (B - 1, None, None, None))

        if STAGES > 1:
            cross_attention(0)

        def experts():
            for eng in (pe, dve):
                after(eng, s_w["moe"])
            gateT = big_a[0:EXPERTS, 0, :]

            def sm(n):
                return small[:, n, :].rearrange("p (g e) -> p g e", g=G)

            def one(n):
                return soft_max[:, n, :]

            def wide(ap):
                return ap.unsqueeze(2).to_broadcast([T, G, EXPERTS])

            with loop("moe", NG) as g:
                layernorm(G, g * G, GT)
                for j in range(G):
                    for k in range(KD):
                        last = pe.matmul(ps[0:T, 2, j * EXPERTS:(j + 1) * EXPERTS], xT[:, k, j * T:(j + 1) * T],
                                         gate_w[:, k, :], start=(k == 0), stop=(k == KD - 1))
                PE.do(last, "logits")
                after(dve, PE.at("logits"))
                logit, hit, cand, keep1, rest, keep2, ex, gate = (sm(n) for n in range(8))
                top, pick, total = one(0), one(1), one(2)
                rk = rank[:, :].rearrange("p (g e) -> p g e", g=G)

                def chain(ins, name=None):
                    DV.do(ins, name)
                    after(dve, DV.all())

                chain(dve.tensor_tensor(logit, ps[0:T, 2, 0:G * EXPERTS].rearrange("p (g e) -> p g e", g=G),
                                        gate_b[:, :].unsqueeze(1).to_broadcast([T, G, EXPERTS]), ALU.add))
                chain(dve.tensor_reduce(top, logit, AXX, ALU.max))
                chain(dve.tensor_tensor(ex, logit, wide(top), ALU.subtract), "shifted")
                src = logit
                for n, keep in ((0, keep1), (1, keep2)):
                    if n:
                        chain(dve.tensor_reduce(pick, src, AXX, ALU.max))
                    chain(dve.tensor_tensor(hit, src, wide(pick if n else top), ALU.is_equal))
                    chain(dve.tensor_tensor(cand, hit, rk, ALU.mult))
                    chain(dve.tensor_reduce(pick, cand, AXX, ALU.max))
                    chain(dve.tensor_tensor(keep, cand, wide(pick), ALU.is_equal))
                    if n == 0:
                        chain(dve.scalar_tensor_tensor(rest, keep1, -3.0e38, logit, ALU.mult, ALU.add))
                        src = rest
                chain(dve.tensor_tensor(keep1, keep1, keep2, ALU.add))
                after(act, DV.at("shifted"))
                AC.do(act.activation(ex, ex, ACT.Exp), "ex")
                after(dve, AC.at("ex"))
                chain(dve.tensor_tensor(ex, ex, keep1, ALU.mult))
                chain(dve.tensor_reduce(total, ex, AXX, ALU.add))
                chain(dve.reciprocal(total, total))
                chain(dve.tensor_tensor(gate, ex, wide(total), ALU.mult), "gate")
                after(pe, DV.at("gate"))
                for j in range(G):
                    last = pe.transpose(ps[0:EXPERTS, 3, j * T:(j + 1) * T], gate[:, j, :], ident[0:T, 0:T])
                PE.do(last, "gateT_ps")
                after(act, PE.at("gateT_ps"))
                AC.do(act.activation(gateT, ps[0:EXPERTS, 3, 0:GT], ACT.Copy), "gateT")
                after(pe, AC.at("gateT"))
                for j in range(G):
                    last = pe.matmul(ps[0:T, j // 2, (j % 2) * D:(j % 2 + 1) * D], gateT[:, j * T:(j + 1) * T],
                                     expert_b[:, :], start=True, stop=True)
                PE.do(last, "bias")
                after(dve, PE.at("bias"))
                for n in range(G // 2):
                    xs = x[:, bass.ds(g * G + 2 * n, 2), :]
                    DV.do(dve.tensor_tensor(xs, xs, ps[0:T, n, :].rearrange("p (g d) -> p g d", g=2), ALU.add), "x_bias")
                after(dve, DV.at("x_bias"))
                n = 0
                for j in range(G):
                    for e in range(0, EXPERTS, 2):
                        bank = 4 + n % 4
                        if n >= 4:
                            after(pe, DV.at(f"x{n - 4}"))
                        for k in range(KD):
                            last = pe.matmul(ps[0:T, bank, :], xT[:, k, j * T:(j + 1) * T],
                                             expert_w[:, k, e * D:(e + 2) * D], start=(k == 0), stop=(k == KD - 1))
                        PE.do(last, f"e{n}")
                        after(dve, PE.at(f"e{n}"))
                        for q in range(2):
                            xs = x[:, g * G + j, :]
                            DV.do(dve.scalar_tensor_tensor(xs, ps[0:T, bank, q * D:(q + 1) * D],
                                                           gate[:, j, e + q:e + q + 1], xs, ALU.mult, ALU.add), f"x{n}")
                            after(dve, DV.at(f"x{n}"))
                        n += 1

        if STAGES > 2:
            experts()

        def self_attention():
            for eng in (pe,):
                after(eng, s_w["attn"])
            qk = big_b
            v = big_a[0:T, 0:3, :].rearrange("p a b -> p (a b)")[:, 0:G * D].rearrange("p (g d) -> p g d", g=G)
            PTs = big_a[0:T, 4, :]
            with loop("attn", NG) as g:
                layernorm(G, g * G, GT)
                for n in range(2 * KD):
                    for k in range(KD):
                        last = pe.matmul(ps[:, 2 + n, 0:GT], attn_w[:, k, n * 128:(n + 1) * 128], xT[:, k, :],
                                         start=(k == 0), stop=(k == KD - 1))
                    PE.do(last, f"qk{n}")
                for n in range(2 * KD):
                    if n < KD:
                        after(act, PE.at(f"qk{n}"))
                        AC.do(act.activation(qk[:, n, :], ps[:, 2 + n, 0:GT], ACT.Copy, scale=1.0 / 16), "q")
                    else:
                        after(dve, PE.at(f"qk{n}"))
                        DV.do(dve.tensor_copy(qk[:, n, :], ps[:, 2 + n, 0:GT]), "k")
                for j in range(G):
                    for k in range(KD):
                        last = pe.matmul(ps[0:T, 6 + j // 2, (j % 2) * D:(j % 2 + 1) * D], xT[:, k, j * T:(j + 1) * T],
                                         attn_w[:, k, 2 * D:3 * D], start=(k == 0), stop=(k == KD - 1))
                PE.do(last, "v_ps")
                after(act, PE.at("v_ps"))
                for n in range(G // 2):
                    AC.do(act.activation(v[:, 2 * n:2 * n + 2, :], ps[0:T, 6 + n, :].rearrange("p (g d) -> p g d", g=2),
                                         ACT.Copy), "v")
                after(pe, AC.at("q"), DV.at("k"))
                for j in range(G):
                    c = slice(j * T, (j + 1) * T)
                    for k in range(KD):
                        last = pe.matmul(ps[0:T, 0, c], qk[:, k, c], qk[:, KD + k, c], start=(k == 0), stop=(k == KD - 1))
                PE.do(last, "S")
                after(dve, PE.at("S"))
                mx, tot = soft_max[:, 0, :], soft_max[:, 1, :]
                DV.do(dve.tensor_tensor(soft[:, :, :], p3(ps[0:T, 0, 0:GT]),
                                        causal_neg[:, :].unsqueeze(1).to_broadcast([T, G, T]), ALU.add), "masked")
                after(dve, DV.at("masked"))
                DV.do(dve.tensor_reduce(mx, soft[:, :, :], AXX, ALU.max), "max")
                after(dve, DV.at("max"))
                DV.do(dve.tensor_tensor(soft[:, :, :], soft[:, :, :], mx.unsqueeze(2).to_broadcast([T, G, T]),
                                        ALU.subtract), "shifted")
                after(act, DV.at("shifted"))
                AC.do(act.activation(soft[:, :, :], soft[:, :, :], ACT.Exp), "P")
                after(dve, AC.at("P"))
                DV.do(dve.tensor_reduce(tot, soft[:, :, :], AXX, ALU.add), "tot")
                after(dve, DV.at("tot"))
                DV.do(dve.reciprocal(tot, tot), "inv")
                after(pe, AC.at("P"))
                for j in range(G):
                    last = pe.transpose(ps[0:T, 1, j * T:(j + 1) * T], soft[:, j, :], ident[0:T, 0:T])
                PE.do(last, "PT_ps")
                after(act, PE.at("PT_ps"))
                AC.do(act.activation(PTs, ps[0:T, 1, 0:GT], ACT.Copy), "PT")
                after(pe, AC.at("PT"))
                for j in range(G):
                    last = pe.matmul(ps[0:T, 6 + j // 2, (j % 2) * D:(j % 2 + 1) * D], PTs[:, j * T:(j + 1) * T],
                                     v[:, j, :], start=True, stop=True)
                PE.do(last, "PV")
                after(dve, PE.at("PV"), DV.at("inv"))
                for j in range(G):
                    xs = x[:, g * G + j, :]
                    DV.do(dve.scalar_tensor_tensor(xs, ps[0:T, 6 + j // 2, (j % 2) * D:(j % 2 + 1) * D],
                                                   tot[:, j:j + 1], xs, ALU.mult, ALU.add), "x")

        if STAGES > 3:
            self_attention()
        if STAGES > 4:
            cross_attention(1)

        def feed_forward():
            for n in range(2):
                sp.dma_start(hw[n][:, :, :], a[f"h{n + 1}"]).then_inc(s_hw, 16)
            for eng in (pe, act, dve):
                after(eng, s_w["ffn"])
            with loop("ffn", NG) as g:
                layernorm(G, g * G, GT)
                for m in range(HT):
                    for n in range(2):
                        if m >= 2:
                            after(pe, DV.at(f"h0_{m - 2}"))
                        for k in range(KD):
                            last = pe.matmul(ps[:, 2 + 2 * n + m % 2, 0:GT], w12[:, n, k, m * 128:(m + 1) * 128], xT[:, k, :],
                                             start=(k == 0), stop=(k == KD - 1))
                        PE.do(last, f"w{n}_{m}")
                    after(act, PE.at(f"w0_{m}"))
                    if m >= 2:
                        after(act, DV.at(f"h0_{m - 2}"))
                    AC.do(act.activation(silu[:, m % 2, :], ps[:, 2 + m % 2, 0:GT], ACT.Silu, scale=hid_s[:, 0, m:m + 1]),
                          f"silu{m}")
                    after(dve, AC.at(f"silu{m}"), PE.at(f"w1_{m}"))
                    DV.do(dve.scalar_tensor_tensor(big_a[:, m, :], ps[:, 4 + m % 2, 0:GT], hid_s[:, 1, m:m + 1],
                                                   silu[:, m % 2, :], ALU.mult, ALU.mult), f"h0_{m}")
                for n, (src, dst) in enumerate(((big_a, big_b), (big_b, big_a))):
                    for m in range(HT):
                        if n == 0 and m in (0, 2):
                            after(pe, DV.at(f"h0_{HT - 1}"))
                        if m == 0:
                            after(pe, (s_hw, 32))
                        if m >= 4:
                            after(pe, AC.at(f"g{n}_{m - 4}"))
                        elif n == 1:
                            after(pe, AC.at(f"g0_{HT - 1}"))
                        for k in range(HT):
                            last = pe.matmul(ps[:, m % 4, 0:GT], hw[n][:, k, m * 128:(m + 1) * 128], src[:, k, :],
                                             start=(k == 0), stop=(k == HT - 1))
                        PE.do(last, f"h{n + 1}_{m}")
                        after(act, PE.at(f"h{n + 1}_{m}"))
                        if n == 0 and m == 0:
                            pass
                        AC.do(act.activation(dst[:, m, :], ps[:, m % 4, 0:GT], ACT.Gelu, scale=hid_s[:, 2 + n, m:m + 1]),
                              f"g{n}_{m}")
                after(pe, AC.at(f"g1_{HT - 1}"))
                for j in range(G):
                    for k in range(HT):
                        last = pe.matmul(ps[0:T, 4 + j // 2, (j % 2) * D:(j % 2 + 1) * D], big_a[:, k, j * T:(j + 1) * T],
                                         w3[:, k, :], start=(k == 0), stop=(k == HT - 1))
                PE.do(last, "y_ps")
                y = xn
                after(dve, PE.at("y_ps"))
                for n in range(G // 2):
                    DV.do(dve.tensor_tensor(y[:, 2 * n:2 * n + 2, :], ps[0:T, 4 + n, :].rearrange("p (g d) -> p g d", g=2),
                                            w3_s[:, :].unsqueeze(1).to_broadcast([T, 2, D]), ALU.mult), "y")
                after(dve, DV.at("y"))
                xs = x[:, bass.ds(g * G, G), :]
                DV.do(dve.tensor_tensor(xs, xs, y[:, :, :], ALU.add), "x")
                after_sp(DV.at("x"))
                sp.dma_start(out[g].rearrange("b t d -> t b d"), xs).then_inc(s_out, 16)

        if STAGES > 5:
            feed_forward()
        else:
            after_sp(DV.all())
            for g in range(NG):
                sp.dma_start(out[g].rearrange("b t d -> t b d"), x[:, g * G:(g + 1) * G, :]).then_inc(s_out, 16)
        after_sp(*s_w.values(), (s_out, 16 * NG))


def lay_out(i):
    def c(v):
        return np.ascontiguousarray(v)

    def rows_of(w):
        return c(w.reshape(-1, 128, w.shape[-1]).transpose(1, 0, 2))

    def wide(v, n):
        return c(np.broadcast_to(v, (n, v.shape[-1])))

    def cols_of(v):
        return c(v.reshape(-1, 128).T)

    f = np.float32
    t = np.arange(T)
    a = {"x": i["x"]}
    a["ctxT"] = c(i["ctx_1024"].transpose(0, 2, 1).reshape(B, KD, 128, S2).transpose(0, 2, 1, 3))
    a["mask0"] = c(i["mask_Bx1xSxS2_if1"][:, 0])
    a["maskT0"] = c(i["mask_Bx1xSxS2_if1"][:, 0].transpose(0, 2, 1).reshape(B, NC, CK, T).transpose(0, 2, 1, 3))
    a["maskT1"] = c(i["mask_Bx1xSxS2_bk0"][:, 0].transpose(0, 2, 1).reshape(B, NC, CK, T).transpose(0, 2, 1, 3))
    sel = np.zeros((3, XH, XH, CK), f)
    sel[:, np.arange(XH), np.arange(XH)] = 1
    a["sel"] = sel.reshape(3 * XH, XH * CK)
    a["mask1"] = c(i["mask_Bx1xSxS2_bk0"][:, 0])
    a["ident"] = np.eye(128, dtype=f)
    a["before"] = (t[None, :] < t[:, None]).astype(f)
    a["upto"] = (t[:, None] <= t[None, :]).astype(f)
    a["minus_strict"] = np.where(t[:, None] < t[None, :], f(-1), f(0))
    a["causal_neg"] = np.where(t[None, :] > t[:, None], f(NEG), f(0))
    a["rank"] = wide(np.tile(EXPERTS - np.arange(EXPERTS), G).astype(f), T)
    qkvz = np.concatenate([i["L0_attn_qkv_w"], i["L0_attn_z_w"]], 0)
    w = qkvz.reshape(4, HEADS, 128, KD, 128).transpose(1, 4, 0, 3, 2).reshape(HEADS, 128, HWID)
    taps = i["L0_attn_conv_w"].reshape(3, HEADS, 128, TAPS).transpose(1, 2, 0, 3).reshape(HEADS, 128, 3 * TAPS)
    a["head_w"] = c(np.concatenate([w, taps], -1)[[*range(HEADS), 0]])
    a["ba_w"] = rows_of(c(np.concatenate([i["L0_attn_b_w"], i["L0_attn_a_w"]], 0).T))
    a["dt_bias"] = wide(i["L0_attn_dt_bias"], T)
    a["A_log"] = wide(i["L0_attn_A_log"], T)
    a["norm_w"] = c(i["L0_attn_norm_w"].reshape(128, 1))
    a["gdn_out_w"] = c(rows_of(c(i["L0_attn_out_w"].T))[:, [0, *range(HEADS)]])
    for n in "qkvo":
        a[f"x0_W{n}"] = rows_of(c(i[f"L0_xattn_W{n}"].T))
        a[f"x1_W{n}"] = rows_of(i[f"L1_xattn_W{n}"])
    a["x0_bo"] = wide(i["L0_xattn_bo"], 128)
    a["x1_bo"] = wide(i["L1_xattn_bo"], 128)
    a["x1_bv"] = wide(i["L1_xattn_bv"], 128)
    a["x1_bqk"] = c(np.stack([cols_of(i["L1_xattn_bq"]), cols_of(i["L1_xattn_bk"])], 1))
    a["gate_w"] = rows_of(c(i["L0_ffn_gate_w"].T))
    a["gate_b"] = wide(i["L0_ffn_gate_b"], T)
    a["expert_w"] = rows_of(c(i["L0_ffn_expert_w"].transpose(1, 0, 2).reshape(D, EXPERTS * D)))
    a["expert_b"] = i["L0_ffn_expert_b"]
    a["attn_w"] = rows_of(np.concatenate([i["L1_attn_Wq"], i["L1_attn_Wk"], i["L1_attn_Wv"]], 1))
    a["w12"] = c(np.stack([rows_of(c(i["L1_ffn_w1_w"].T)), rows_of(c(i["L1_ffn_w2_w"].T))], 1))
    a["h1"] = rows_of(c(i["L1_ffn_h1_w"].T))
    a["h2"] = rows_of(c(i["L1_ffn_h2_w"].T))
    a["w3"] = rows_of(c(i["L1_ffn_w3_w"].T))
    a["hid_s"] = c(np.stack([cols_of(i[f"L1_ffn_{n}_s"]) for n in ("w1", "w2", "h1", "h2")], 1))
    a["w3_s"] = wide(i["L1_ffn_w3_s"], T)
    return {n: c(v) for n, v in a.items()}


def build(nc, shapes, plan):
    a = {n: nc.dram_tensor(f"in_{n}", s, mybir.dt.from_np(d), kind="ExternalInput").ap() for n, (s, d) in shapes.items()}
    out = nc.dram_tensor("out", (NG, G, T, D), F32, kind="ExternalOutput").ap()
    decoder(nc, a, out, plan)


def kernel(**inputs):
    import concourse.bacc as bacc
    from concourse.bass_utils import run_bass_kernel_spmd

    arrays = lay_out({n: np.asarray(v) for n, v in inputs.items()})
    shapes = {n: (v.shape, v.dtype) for n, v in arrays.items()}
    plan = {}
    build(bacc.Bacc("TRN2", target_bir_lowering=False, num_devices=1), shapes, plan)
    nc = bacc.Bacc("TRN2", target_bir_lowering=False, num_devices=1)
    build(nc, shapes, plan)
    r = run_bass_kernel_spmd(nc, [{f"in_{n}": v for n, v in arrays.items()}], core_ids=[0])
    return r.results[0]["out"].reshape(B, T, D)
```

```python
from contextlib import ExitStack

import numpy as np

import concourse.bass as bass
from concourse import mybir

F32 = mybir.dt.float32
BF16 = mybir.dt.bfloat16
I32 = mybir.dt.int32
U8 = mybir.dt.uint8
ACT = mybir.ActivationFunctionType
ALU = mybir.AluOpType
AXX = mybir.AxisListType.X

B, T, D = 16, 112, 256
S2 = 375
KD = D // 128
G = 4
GT = G * T
NG = B // G
HEADS, DK = 8, 128
TAPS = 4
HWID = 4 * KD * 128
XH, XD = 16, 16
CK = 125
NC = S2 // CK
EXPERTS = 8
HID = 1024
HT = HID // 128
NEG = -1.0e30
BUMP = 4096
LEVELS = 7
LAG = 2
MAXIMA_FROM = 5


class Steps:

    def __init__(self, who, sem, plan):
        self.who, self.sem, self.plan = who, sem, plan
        self.frames = [{"name": who, "start": BUMP, "i": 0, "origin": BUMP, "n": 0, "pos": 0}]

    def open(self, name, i):
        top = self.frames[-1]
        n = self.plan.get((self.who, name), 0)
        start = top["origin"] + top["pos"]
        self.frames.append({"name": name, "start": start, "i": i, "origin": start + i * n, "n": n, "pos": 0})

    def close(self, trips):
        f = self.frames.pop()
        self.plan[(self.who, f["name"])] = f["pos"]
        self.frames[-1]["pos"] += trips * f["pos"]

    def do(self, ins, name=None):
        f = self.frames[-1]
        f["pos"] += 1
        if name:
            self.plan[(self.who, f["name"], name)] = f["pos"]
        ins.then_inc(self.sem, 1)
        return ins

    def at(self, name, ago=0):
        for f in reversed(self.frames):
            if (self.who, f["name"], name) in self.plan:
                on = self.plan[(self.who, f["name"], name)] - ago * f["n"]
                return self.sem, f["origin"] + on, f["i"], f["n"], f["start"] + on
        return self.sem, self.frames[0]["origin"]

    def all(self):
        f = self.frames[-1]
        return self.sem, f["origin"] + f["pos"]


def latest(points):
    kept = []
    for point in points:
        for n, other in enumerate(kept):
            if len(point) > 2 and len(other) > 2 and point[0] is other[0] and point[2] is other[2]:
                if point[4] > other[4]:
                    kept[n] = point
                break
        else:
            kept.append(point)
    return kept


def after(eng, *points):
    for point in latest(points):
        eng.wait_ge(point[0], point[1])


def decoder(nc, a, out, plan):
    pe, act, dve, pool, sp = nc.tensor, nc.scalar, nc.vector, nc.gpsimd, nc.sync
    with ExitStack() as ctx:
        def sb(name, shape, dt=F32):
            return ctx.enter_context(nc.sbuf_tensor(name, shape, dt))

        def sem(name):
            return ctx.enter_context(nc.semaphore(name))

        x = sb("x", [T, B, D])
        ident = sb("ident", [128, 128])
        ident_bf = sb("ident_bf", [128, 128], BF16)
        before = sb("before", [T, T])
        upto = sb("upto", [T, T])
        minus_strict = sb("minus_strict", [T, T])
        causal_neg = sb("causal_neg", [T, T])
        rank = sb("rank", [T, G * EXPERTS])
        minus_half = sb("minus_half", [T, G])

        head_w = sb("head_w", [128, HWID + 3 * TAPS])
        ba_w = sb("ba_w", [128, KD, 2 * HEADS])
        dt_bias = sb("dt_bias", [T, HEADS])
        decay = sb("decay", [T, HEADS])
        norm_w = sb("norm_w", [128, 1])
        gdn_out_w = sb("gdn_out_w", [128, HEADS + 1, D])
        xw = [{n: sb(f"x{n}{l}", [128, KD, D]) for n in ("q", "k", "v", "o")} for l in range(2)]
        xb_row = [{n: sb(f"x{n}_bias{l}", [128, D]) for n in (("o",), ("v", "o"))[l]} for l in range(2)]
        xb_col = sb("xb_col", [128, 2, KD])
        gate_w = sb("gate_w", [128, KD, EXPERTS])
        gate_b = sb("gate_b", [T, EXPERTS])
        expert_w = sb("expert_w", [128, KD, EXPERTS * D])
        expert_b = sb("expert_b", [EXPERTS, D])
        attn_w = sb("attn_w", [128, KD, 3 * D])
        w12 = sb("w12", [128, 2, KD, HID])
        hw = [sb(f"h{n}_w", [128, HT, HID]) for n in (1, 2)]
        w3 = sb("w3", [128, HT, D])
        hid_s = sb("hid_s", [128, 4, HT])
        w3_s = sb("w3_s", [T, D])

        stats = sb("stats", [T, G, 6])
        mean_var = sb("mean_var", [T, G, 2])
        var_eps = sb("var_eps", [T, G])
        rstd = sb("rstd", [T, G])
        carrier = sb("carrier", [T, 1])
        xn = sb("xn", [T, G, D])
        xT = sb("xT", [128, KD, GT])
        big_a = sb("big_a", [128, HT, GT])
        big_b = sb("big_b", [128, HT, GT])
        silu = sb("silu", [128, 2, GT])
        small = sb("small", [T, 16, G * EXPERTS])
        soft = sb("soft", [T, G, T])
        soft_max = sb("soft_max", [T, 4, G])

        ps = ctx.enter_context(nc.psum_tensor("ps", [128, 8, 512], F32))

        PE, AC, DV, PL = (Steps(n, sem(f"s_{n}"), plan) for n in ("pe", "act", "dve", "pool"))
        for eng, st in ((pe, PE), (act, AC), (dve, DV), (pool, PL)):
            eng.sem_inc(st.sem, BUMP)
        s_x, s_const, s_headw, s_ctx, s_out = (sem(n) for n in ("s_x", "s_const", "s_headw", "s_ctx", "s_out"))
        s_mask = sem("s_mask")
        s_hw = sem("s_hw")

        fresh = [0]

        def loop(name, n):
            class L:
                def __enter__(self):
                    self.c = nc.Fori(0, n)
                    self.i = self.c.__enter__()
                    for st in (PE, AC, DV, PL):
                        st.open(name, self.i)
                    return self.i

                def __exit__(self, *e):
                    for st in (PE, AC, DV, PL):
                        st.close(n)
                    return self.c.__exit__(*e)
            return L()

        def after_sp(*points):
            for sem, value, *parts in latest(points):
                if parts and not isinstance(parts[0], int) and isinstance(parts[2], int):
                    i, n, rest = parts
                    fresh[0] += 1
                    value = (i + fresh[0]) * n + (rest - fresh[0] * n)
                sp.wait_ge(sem, value)

        def load(dst, name, s):
            sp.dma_start(dst, a[name]).then_inc(s, 16)

        sp.dma_start(x[:, :, :], a["x"].rearrange("b t d -> t b d")).then_inc(s_x, 16)
        consts = [(ident[:, :], "ident"), (before[:, :], "before"), (upto[:, :], "upto"),
                  (minus_strict[:, :], "minus_strict"), (causal_neg[:, :], "causal_neg"),
                  (rank[:, :], "rank"), (ba_w[:, :, :], "ba_w"), (dt_bias[:, :], "dt_bias"), (decay[:, :], "A_log"),
                  (norm_w[:, :], "norm_w")]
        for dst, name in consts:
            load(dst, name, s_const)
        weights = {"gdn": [(gdn_out_w[:, :, :], "gdn_out_w")]}
        for l in range(2):
            weights[f"x{l}"] = [(xw[l][n][:, :, :], f"x{l}_W{n}") for n in "qkvo"] + \
                               [(t[:, :], f"x{l}_b{n}") for n, t in xb_row[l].items()]
        weights["x1"].append((xb_col[:, :, :], "x1_bqk"))
        weights["moe"] = [(gate_w[:, :, :], "gate_w"), (gate_b[:, :], "gate_b"), (expert_w[:, :, :], "expert_w"),
                          (expert_b[:, :], "expert_b")]
        weights["attn"] = [(attn_w[:, :, :], "attn_w")]
        weights["ffn"] = [(w12[:, :, :, :], "w12"), (w3[:, :, :], "w3"), (hid_s[:, :, :], "hid_s"), (w3_s[:, :], "w3_s")]
        s_w = {}
        sp.dma_start(head_w[:, :], a["head_w"][0]).then_inc(s_headw, 16)
        for stage in ("gdn", "x0", "moe", "attn", "x1", "ffn"):
            s_w[stage] = (sem(f"s_w_{stage}"), 16 * len(weights[stage]))
            for dst, name in weights[stage]:
                load(dst, name, s_w[stage][0])

        consts_in = (s_const, 16 * len(consts))
        for eng in (pe, act, dve, pool):
            after(eng, consts_in)
        after(dve, (s_x, 16))
        PL.do(pool.memset(minus_half[:, :], -0.5), "minus_half")
        DV.do(dve.tensor_copy(ident_bf[:, :], ident[:, :]))
        DV.do(dve.tensor_scalar(norm_w[:, :], norm_w[:, :], 0.5, None, ALU.mult))
        AC.do(act.activation(decay[:, :], decay[:, :], ACT.Exp), "decay")
        for eng in (pe, act, dve, pool):
            after(eng, PL.all(), DV.all(), AC.all())

        def normalise(first, *free):
            after(dve, DV.all(), *free)
            for j in range(G):
                DV.do(dve.bn_stats(stats[:, j, :], x[:, first + j, :]))
            after(dve, DV.all())
            DV.do(dve.memset(carrier[:, :], 0.0))
            for j in range(G):
                DV.do(dve.bn_aggr(mean_var[:, j, :], stats[:, j, :]))
            after(dve, DV.all())
            DV.do(dve.tensor_scalar(var_eps[:, :], mean_var[:, :, 1], 1e-5, None, ALU.add), "ln_var")
            after(pool, DV.at("ln_var"))
            PL.do(pool.tensor_tensor(rstd[:, :], var_eps[:, :], minus_half[:, :], ALU.pow), "ln_rstd")
            after(dve, PL.at("ln_rstd"))
            for j in range(G):
                DV.do(dve.tensor_scalar(xn[:, j, :], x[:, first + j, :], mean_var[:, j, 0:1], rstd[:, j:j + 1],
                                        ALU.subtract, ALU.mult), "ln_xn")

        def transpose_xn(dst, bank, copiers="ad", ago=0):
            after(pe, DV.at("ln_xn", ago), AC.all())
            for k in range(KD):
                for j in range(G):
                    last = pe.transpose(ps[:, bank + k, j * T:(j + 1) * T], xn[:, j, k * 128:(k + 1) * 128], ident[0:T, 0:T])
                PE.do(last, f"ln_T{k}")
            for k, who in enumerate(copiers):
                if who == "a":
                    after(act, PE.at(f"ln_T{k}"))
                    AC.do(act.activation(dst[:, k, :], ps[:, bank + k, 0:GT], ACT.Copy), f"ln_done{k}")
                else:
                    after(dve, PE.at(f"ln_T{k}"))
                    DV.do(dve.tensor_copy(dst[:, k, :], ps[:, bank + k, 0:GT]), f"ln_done{k}")

        def xn_transposed(eng, copiers="ad"):
            after(eng, *((AC if who == "a" else DV).at(f"ln_done{k}") for k, who in enumerate(copiers)))

        def once(name, *parts):
            for st in (PE, AC, DV, PL):
                st.open(name, 0)
            for part in parts:
                part()
            for st in (PE, AC, DV, PL):
                st.close(1)
            everyone()

        def everyone():
            points = [st.all() for st in (PE, AC, DV, PL)]
            for eng in (pe, act, dve, pool, sp):
                after(eng, *points)

        def p3(ap):
            return ap.rearrange("p (g t) -> p g t", g=G)

        late = hw[1][:, :, :].rearrange("p a b -> p (a b)")
        gdn_xT = late[:, 0:NG * KD * GT].rearrange("p (g k t) -> p g k t", g=NG, k=KD)
        spare = late[0:T, NG * KD * GT:]
        W0, W = (spare[:, n * G * DK:(n + 1) * G * DK] for n in range(2))
        On = xn[:, 0:2, :].rearrange("p a b -> p (a b)")
        beta_decay = small[:, 0:9, :].rearrange("p a b -> p (a b)").rearrange("p (n h g j) -> p n h g j", n=2, g=NG, j=G)
        here = sb("here", [T, 2, G])
        cum_l = soft[:, :, :]
        gamma = big_a[0:T, 1, :]
        gam_s, gam_i = p3(big_a[0:T, 2, :]), p3(big_a[0:T, 3, :])
        qT, kT, vT, zT = (big_b[:, n, :] for n in range(4))
        oT = big_b[:, 4, :]
        sz_next, sz = big_b[:, 5, :], big_b[:, 6, :]
        N0 = big_b[0:T, 7, :]
        NT = [big_a[0:T, 4, :], big_a[0:T, 5, :]]
        MM = big_a[0:T, 6, :]
        QG_next, QG = big_a[0:T, 0, :], big_a[0:T, 7, :]

        DV.do(dve.memset(beta_decay[:, :, HEADS, :, :], 0.0))
        DV.do(dve.memset(sz, 0.0))
        DV.do(dve.memset(ps[:, 6, :], 0.0))

        def decays(g, more=True):
            transpose_xn(xT, 0, ago=1)
            xn_transposed(pe)
            xn_transposed(act)
            AC.do(act.activation(gdn_xT[:, g, :, :], xT[:, :, :], ACT.Copy), "keep")
            for j in range(G):
                for k in range(KD):
                    last = pe.matmul(ps[0:T, 2, j * 16:(j + 1) * 16], xT[:, k, j * T:(j + 1) * T], ba_w[:, k, :],
                                     start=(k == 0), stop=(k == KD - 1))
            PE.do(last, "ba")
            if more:
                normalise(g * G + G, PE.at("ln_T1"))
            ba = ps[0:T, 2, 0:G * 16].rearrange("p (g c) -> p g c", g=G)
            y, t1, t2, bb = (small[:, n, :].rearrange("p (g c) -> p g c", g=G) for n in (9, 10, 11, 12))
            after(dve, PE.at("ba"))
            DV.do(dve.tensor_tensor(y, ba[:, :, HEADS:], dt_bias[:, :].unsqueeze(1).to_broadcast([T, G, HEADS]), ALU.add))
            DV.do(dve.tensor_copy(bb, ba[:, :, 0:HEADS]), "ba_in")
            after(act, DV.at("ba_in"))
            AC.do(act.activation(t1, y, ACT.Abs), "sp1")
            after(act, AC.at("sp1"))
            AC.do(act.activation(t1, t1, ACT.Exp, scale=-1.0), "sp2")
            AC.do(act.activation(bb, bb, ACT.Exp, scale=-1.0), "sig")
            after(act, AC.at("sp2"))
            AC.do(act.activation(t1, t1, ACT.Ln, bias=1.0), "sp3")
            after(dve, AC.at("sp3"))
            DV.do(dve.scalar_tensor_tensor(t2, y, 0.0, t1, ALU.max, ALU.add))
            DV.do(dve.tensor_scalar(bb, bb, 1.0, None, ALU.add))
            after(dve, DV.all())
            DV.do(dve.reciprocal(t1, bb))
            after(dve, DV.all())
            DV.do(dve.tensor_copy(beta_decay[:, 0, 0:HEADS, g, :], t1.rearrange("p g c -> p c g")))
            DV.do(dve.scalar_tensor_tensor(beta_decay[:, 1, 0:HEADS, g, :], t2.rearrange("p g c -> p c g"), -1.0,
                                           decay[:, :].unsqueeze(2).to_broadcast([T, HEADS, G]), ALU.mult, ALU.mult),
                  "beta_decay")

        once("gdn_norm", lambda: normalise(0))
        with loop("gdn", NG - 1) as g:
            decays(g)
        everyone()
        once("gdn_gates", lambda: decays(NG - 1, more=False))

        w4 = head_w[:, 0:HWID].rearrange("p (n k c) -> p n k c", n=4, k=KD)
        taps = head_w[:, HWID:].rearrange("p (n j) -> p n j", j=TAPS)
        per_unit = [slice(j * T, (j + 1) * T) for j in range(G)]

        def unit(g, h):
            last_g, back = (g - 1) % NG, 1 if g == 0 else 0
            gn, hn = (g + 1) % NG, h if g < NG - 1 else h + 1

            def was(st, n):
                return st.at(f"{n}_{last_g}", back)

            def now(st, n):
                return st.at(f"{n}_{g}")

            def other_taps(n, dst):
                for s in range(1, TAPS):
                    DV.do(dve.scalar_tensor_tensor(p3(dst)[:, :, s:], p3(ps[:, 1 + n, 0:GT])[:, :, 0:T - s],
                                                   taps[:, n, TAPS - 1 - s:TAPS - s], p3(dst)[:, :, s:],
                                                   ALU.mult, ALU.add), f"conv{n}_{g}")
                    after(dve, now(DV, f"conv{n}"))

            def proj(n):
                for k in range(KD):
                    last = pe.matmul(ps[:, 1 + n, 0:GT], w4[:, n, k, :], gdn_xT[:, gn, k, :], start=(k == 0), stop=(k == KD - 1))
                PE.do(last, f"proj{n}_{g}")

            def tap(n, dst):
                after(act, now(PE, f"proj{n}"))
                AC.do(act.activation(dst, ps[:, 1 + n, 0:GT], ACT.Copy, scale=taps[:, n, TAPS - 1:TAPS]), f"tap{n}_{g}")

            def front():
                after(pe, (s_headw, (hn + 1) * 16), was(DV, "N0"))
                proj(1)
                after(act, (s_headw, (hn + 1) * 16))
                tap(1, kT)
                yield
                after(dve, was(DV, "QG"))
                DV.do(dve.tensor_copy(here[:, :, :], beta_decay[:, :, hn, gn, :]), f"here_{g}")
                after(dve, now(DV, "here"), was(PE, "logG"))
                DV.do(dve.tensor_tensor(cum_l, before[:, :].unsqueeze(1).to_broadcast([T, G, T]),
                                        here[:, 1, :].unsqueeze(2).to_broadcast([T, G, T]), ALU.mult), f"cum_l_{g}")
                after(dve, now(AC, "tap1"))
                other_taps(1, kT)
                yield
                after(pe, was(DV, "QG"))
                proj(0)
                tap(0, qT)
                yield
                after(dve, now(AC, "tap0"))
                other_taps(0, qT)
                yield
                after(pe, now(DV, "conv1"))
                for c in per_unit:
                    last = pe.matmul(ps[0:T, 2, c], kT[:, c], kT[:, c], start=True, stop=True)
                PE.do(last, f"kk_{g}")
                yield
                yield
                after(pe, was(AC, "W0"))
                proj(2)
                tap(2, vT)
                yield
                after(dve, now(AC, "tap2"))
                other_taps(2, vT)
                yield
                after(pe, now(DV, "x"))
                proj(3)
                if g == NG - 2:
                    after_sp(now(PE, "proj3"), now(DV, "conv2"))
                    sp.dma_start(head_w[:, :], a["head_w"][h + 1]).then_inc(s_headw, 16)
                after(act, now(PE, "proj3"))
                AC.do(act.activation(zT, ps[:, 4, 0:GT], ACT.Tanh, scale=0.5), f"tanh_{g}")
                yield
                after(dve, now(AC, "tanh"), now(AC, "sz"))
                DV.do(dve.scalar_tensor_tensor(sz_next, zT, 1.0, ps[:, 4, 0:GT], ALU.add, ALU.mult), f"sz_next_{g}")
                yield
                after(pe, now(DV, "cum_l"))
                for j, c in enumerate(per_unit):
                    last = pe.matmul(ps[0:T, 6, c], cum_l[:, j, :], upto[:, :], start=True, stop=True)
                PE.do(last, f"logG_{g}")
                after(act, now(PE, "logG"))
                AC.do(act.activation(gamma, ps[0:T, 6, 0:GT], ACT.Exp), f"gamma_{g}")
                yield
                after(pool, now(AC, "gamma"))
                PL.do(pool.tensor_tensor(gam_s, p3(gamma), minus_strict[:, :].unsqueeze(1).to_broadcast([T, G, T]), ALU.mult),
                      f"gam_s_{g}")
                PL.do(pool.tensor_tensor(gam_i, p3(gamma), upto[:, :].unsqueeze(1).to_broadcast([T, G, T]), ALU.mult),
                      f"gam_i_{g}")
                yield
                after(pe, now(DV, "conv0"))
                for c in per_unit:
                    last = pe.matmul(ps[0:T, 1, c], kT[:, c], qT[:, c], start=True, stop=True)
                PE.do(last, f"kq_{g}")
                after(dve, now(PE, "kk"), now(PL, "gam_s"))
                for j, c in enumerate(per_unit):
                    DV.do(dve.scalar_tensor_tensor(N0[:, c], ps[0:T, 2, c], here[:, 0, j:j + 1], gam_s[:, j, :],
                                                   ALU.mult, ALU.mult), f"N0_{g}")
                yield
                after(pe, now(DV, "conv2"))
                for j, c in enumerate(per_unit):
                    last = pe.transpose(ps[0:T, 3, j * DK:(j + 1) * DK], vT[:, c], ident[:, :])
                PE.do(last, f"vtok_{g}")
                after(act, now(PE, "vtok"), now(DV, "W1"))
                AC.do(act.activation(W0, ps[0:T, 3, 0:G * DK], ACT.Copy), f"W0_{g}")
                after(dve, now(PE, "kq"), now(PL, "gam_i"), now(AC, "QG"))
                for j, c in enumerate(per_unit):
                    DV.do(dve.scalar_tensor_tensor(QG_next[:, c], ps[0:T, 1, c], here[:, 0, j:j + 1], gam_i[:, j, :],
                                                   ALU.mult, ALU.mult), f"QG_{g}")
                yield

            def levels():
                for lev in range(LEVELS):
                    N = NT[lev % 2] if lev else N0
                    Wsrc = W if lev else W0
                    if lev < LEVELS - 1:
                        after(pe, now(AC, f"N{lev}") if lev else was(DV, "N0"))
                        after(pe, now(AC, f"M{lev - 1}") if lev else was(AC, f"M{LEVELS - 2}"))
                        for c in per_unit:
                            last = pe.transpose(ps[0:T, 0, c], N[:, c], ident[0:T, 0:T])
                        PE.do(last, f"M{lev}T_{g}")
                        after(act, now(PE, f"M{lev}T"))
                        AC.do(act.activation(MM, ps[0:T, 0, 0:GT], ACT.Copy), f"M{lev}_{g}")
                    yield
                    if lev < LEVELS - 1:
                        after(pe, now(AC, f"M{lev}"))
                        for c in per_unit:
                            last = pe.matmul(ps[0:T, 5, c], MM[:, c], N[:, c], start=True, stop=True)
                        PE.do(last, f"N{lev + 1}ps_{g}")
                        after(act, now(PE, f"N{lev + 1}ps"))
                        AC.do(act.activation(NT[(lev + 1) % 2], ps[0:T, 5, 0:GT], ACT.Copy), f"N{lev + 1}_{g}")
                    if lev:
                        after(pe, now(DV, f"W{lev}"), now(AC, f"N{lev}"))
                    else:
                        after(pe, was(AC, "W0"), was(DV, f"W{LEVELS}"))
                    for j, c in enumerate(per_unit):
                        last = pe.matmul(ps[0:T, 7, j * DK:(j + 1) * DK], N[:, c], Wsrc[:, j * DK:(j + 1) * DK],
                                         start=True, stop=True)
                    PE.do(last, f"PW{lev}_{g}")
                    after(dve, now(PE, f"PW{lev}"))
                    DV.do(dve.tensor_tensor(W, Wsrc, ps[0:T, 7, 0:G * DK], ALU.add), f"W{lev + 1}_{g}")
                    if lev == 0:
                        after(act, was(DV, "QG"), was(PE, "O"))
                        AC.do(act.activation(QG, QG_next, ACT.Copy), f"QG_{g}")
                    yield
                after(pe, now(DV, f"W{LEVELS}"), now(AC, "QG"), now(AC, "gamma"))
                for j, c in enumerate(per_unit):
                    last = pe.matmul(ps[0:T, 6, j * DK:(j + 1) * DK], QG[:, c], W[:, j * DK:(j + 1) * DK],
                                     start=True, stop=True)
                PE.do(last, f"O_{g}")
                yield

            def tail():
                after(act, was(PE, "O"))
                for j in range(G):
                    AC.do(act.activation(On[:, j * DK:(j + 1) * DK], ps[0:T, 6, j * DK:(j + 1) * DK], ACT.Square,
                                         accum_out=var_eps[:, j:j + 1]), f"squares_{g}")
                yield
                after(dve, now(AC, "squares"))
                DV.do(dve.tensor_scalar(var_eps[:, :], var_eps[:, :], 1.0 / DK, 1e-6, ALU.mult, ALU.add), f"o_var_{g}")
                after(pool, now(DV, "o_var"))
                PL.do(pool.tensor_tensor(rstd[:, :], var_eps[:, :], minus_half[:, :], ALU.pow), f"o_rstd_{g}")
                after(dve, now(PL, "o_rstd"))
                DV.do(dve.tensor_tensor(On.rearrange("p (g d) -> p g d", g=G),
                                        ps[0:T, 6, 0:G * DK].rearrange("p (g d) -> p g d", g=G),
                                        rstd[:, :].unsqueeze(2).to_broadcast([T, G, DK]), ALU.mult), f"On_{g}")
                yield
                after(pe, now(DV, "On"), was(DV, "sz_next"))
                for j in range(G):
                    last = pe.transpose(ps[:, 4, j * T:(j + 1) * T], On[:, j * DK:(j + 1) * DK], ident[0:T, 0:T])
                PE.do(last, f"oT_{g}")
                after(dve, now(PE, "oT"))
                DV.do(dve.scalar_tensor_tensor(oT, ps[:, 4, 0:GT], norm_w[:, 0:1], sz, ALU.mult, ALU.mult), f"gated_{g}")
                yield
                yield
                after(pe, now(DV, "gated"))
                for j in range(G):
                    last = pe.matmul(ps[0:T, (6, 4)[j // 2], (j % 2) * D:(j % 2 + 1) * D], oT[:, j * T:(j + 1) * T],
                                     gdn_out_w[:, h + (1 if g else 0), :], start=True, stop=True)
                PE.do(last, f"out_{g}")
                yield
                after(act, now(DV, "gated"), was(DV, "sz_next"))
                AC.do(act.activation(sz, sz_next, ACT.Copy), f"sz_{g}")
                after(dve, now(PE, "out"))
                for n in range(G // 2):
                    xs = x[:, last_g * G + 2 * n:last_g * G + 2 * n + 2, :]
                    DV.do(dve.tensor_tensor(xs, xs, ps[0:T, (6, 4)[n], :].rearrange("p (g d) -> p g d", g=2), ALU.add), f"x_{g}")
                yield

            return front, levels, tail

        def run_unit(g, h, with_front=True, with_levels=True, with_tail=True):
            front, levels, tail = unit(g, h)
            parts = [f() if on else iter(()) for f, on in ((levels, with_levels), (front, with_front), (tail, with_tail))]
            if with_levels:
                for n in range(2 * LEVELS):
                    lev, fr, ta = parts
                    next(lev, None)
                    for part in (fr, ta) if n % 2 == 0 else (ta, fr):
                        next(part, None)
            for part in parts:
                for _ in part:
                    pass

        everyone()
        once("gdn_first", lambda: run_unit(NG - 1, -1, with_levels=False, with_tail=False))
        after(pe, s_w["gdn"])
        with loop("heads", HEADS) as h:
            for g in range(NG):
                run_unit(g, h)
        everyone()

        KEY_PART = (0, 0, 0, 1, 1, 1, 2, 2)
        QRY_PART = (0, 1, 2, 0, 1, 2, 0, 1)
        late1 = hw[0][:, :, :].rearrange("p a b -> p (a b)")
        taken = [0, 0]

        def room(n, where, dt=F32, parts=128):
            words = n if dt == F32 or dt == I32 else (n + 1) // 2
            words += words % 2
            at = taken[where]
            taken[where] += words
            assert taken[where] <= HT * HID
            t = (late, late1)[where][0:parts, at:at + words]
            return t if dt == F32 else t.bitcast(dt)[:, 0:n]

        def heads_of(ap, n):
            return ap.rearrange("p (h t) -> p h t", h=XH)

        Kst = [heads_of(room(XH * S2, 0, BF16), S2) for _ in range(2)]
        Qst = [heads_of(room(XH * T, 0, BF16), T) for _ in range(2)]
        Vx = [room(NC * XH * 32, 1, parts=CK).rearrange("p (c h d) -> p c h d", c=NC, h=XH) for _ in range(2)]
        ctxT = room(KD * S2, 1).rearrange("p (k t) -> p k t", k=KD)
        ctxV = room(KD * S2, 1).rearrange("p (k t) -> p k t", k=KD)
        k_rest = big_a[:, 0:2, :].rearrange("p a b -> p (a b)")[:, 0:KD * S2].rearrange("p (k t) -> p k t", k=KD)
        k_part = [room(KD * S2, 1, BF16).rearrange("p (k t) -> p k t", k=KD) for _ in range(3)]
        q_full = room(KD * T, 1)
        q_part = [room(KD * T, 1, BF16) for _ in range(3)]
        PTx = [big_a[0:CK, 5 + n, 0:NC * T] for n in range(3)]
        maskT_raw = room(NC * T, 1, I32, CK)
        mask_raw = room(S2, 1, I32, T)
        maskT_raw8, mask_raw8 = (m.bitcast(U8)[:, 0:m.shape[1]] for m in (maskT_raw, mask_raw))
        mask_add = [room(S2, 1, BF16, T) for _ in range(2)]
        maskT_add = [room(NC * T, 1, BF16, CK) for _ in range(2)]
        nm = room(XH, 1, parts=T)
        nm_rest = room(XH, 1, parts=T)
        nm_part = room(128, 1, BF16, T)
        nmT = [room(T, 1, BF16, 3 * XH) for _ in range(2)]
        oa = big_b[:, 0, :]
        on = big_b[0:T, 1, 0:D]
        onT = big_b[:, 2, 0:KD * T]
        inv = room(XH, 1, parts=T)
        sel_f = big_a[0:3 * XH, :, :].rearrange("p a b -> p (a b)")[:, 0:XH * CK]
        sel = big_b[0:3 * XH, 3:6, :].rearrange("p a b -> p (a b)")[:, 0:XH * CK // 2].bitcast(BF16).rearrange("p (h t) -> p h t", h=XH)
        k_dram = nc.dram_tensor("k_parts", (2, 3, KD, 128, S2), BF16).ap()
        q_dram = nc.dram_tensor("q_parts", (2, 3, KD, 128, T), BF16).ap()
        s_kw, s_kst, s_qw, s_qst, s_sel, s_ctxv = (sem(n) for n in ("s_kw", "s_kst", "s_qw", "s_qst", "s_sel", "s_ctxv"))
        DV.do(dve.memset(nm_part, 0.0), "nm_part")
        for p in range(2):
            DV.do(dve.memset(Vx[p][:, :, :, XD:], 1.0), "ones")

        def first_loads():
            sp.dma_start(sel_f, a["sel"]).then_inc(s_sel, 16)
            sp.dma_start(ctxT, a["ctxT"][0]).then_inc(s_ctx, 16)

        first_loads()
        once("gdn_last", lambda: run_unit(0, HEADS, with_front=False, with_levels=False))

        def cross_attention(l):
            w, name, done = xw[l], f"x{l}", l * B
            for eng in (pe, act, dve):
                after(eng, s_w[name])
            raw = (mask_raw, maskT_raw) if l == 0 else (mask_raw8, maskT_raw8)

            def half(h, i, prev_at, c_at, nxt_at, nxt2_at):
                q, back = 1 - h, 1 - h
                prev, c, nxt, nxt2 = (None if at is None else 2 * i + at for at in (prev_at, c_at, nxt_at, nxt2_at))

                def loads(sem, at, each):
                    rest = (done + at + 1) * each
                    return sem, 2 * i * each + rest, i, 2 * each, rest

                def was(st, n):
                    return st.at(f"{n}_{1 - h}", back)

                def now(st, n):
                    return st.at(f"{n}_{h}")

                def fetch():
                    if c is not None and nxt2 is not None:
                        after_sp(was(PE, "k_proj1"))
                        sp.dma_start(ctxT, a["ctxT"][nxt2]).then_inc(s_ctx, 16)
                    if nxt is not None:
                        after_sp(was(PE, "v_proj"), was(DV, "mask"))
                        sp.dma_start(ctxV, a["ctxT"][nxt]).then_inc(s_ctxv, 16)
                        sp.dma_start(raw[0], a[f"mask{l}"][nxt]).then_inc(s_mask, 16)
                        sp.dma_start(raw[1].rearrange("p (c t) -> p c t", c=NC), a[f"maskT{l}"][nxt]).then_inc(s_mask, 16)
                        after_sp(was(PE, "ST15"), loads(s_kw, nxt_at, 48), loads(s_qw, nxt_at, 48))
                        for r, n in enumerate(KEY_PART):
                            sp.dma_start(Kst[q][16 * r:16 * r + 16, :, :],
                                         k_dram[q, n].rearrange("m (h d) t -> d (m h) t", d=XD)).then_inc(s_kst, 16)
                        for r, n in enumerate(QRY_PART):
                            sp.dma_start(Qst[q][16 * r:16 * r + 16, :, :],
                                         q_dram[q, n].rearrange("m (h d) t -> d (m h) t", d=XD)).then_inc(s_qst, 16)

                def prepare():
                    DV.do(dve.bn_stats(stats[:, 0, :], x[:, nxt2, :]), f"st_{h}")
                    after(dve, now(DV, "st"))
                    DV.do(dve.memset(carrier[:, :], 0.0))
                    DV.do(dve.bn_aggr(mean_var[:, 0, :], stats[:, 0, :]), f"mv_{h}")
                    after(dve, now(DV, "mv"))
                    DV.do(dve.tensor_scalar(var_eps[:, 0:1], mean_var[:, 0, 1:2], 1e-5, None, ALU.add), f"var_{h}")
                    after(pool, now(DV, "var"))
                    PL.do(pool.tensor_tensor(rstd[:, 0:1], var_eps[:, 0:1], minus_half[:, 0:1], ALU.pow), f"rstd_{h}")
                    after(pe, loads(s_ctx, nxt2_at, 16), was(DV, "V2"), was(DV, "q"))
                    for m in range(KD):
                        for k in range(KD):
                            last = pe.matmul(ps[:, 5 + m, 0:S2], w["k"][:, k, m * 128:(m + 1) * 128], ctxT[:, k, :],
                                             start=(k == 0), stop=(k == KD - 1))
                        PE.do(last, f"k_proj{m}_{h}")
                    if nxt is None:
                        after_sp(now(PE, "k_proj1"))
                        sp.dma_start(ctxT, a["ctxT"][nxt2 + 1]).then_inc(s_ctx, 16)
                    yield
                    after(dve, now(PL, "rstd"), was(PE, "xnT"))
                    DV.do(dve.tensor_scalar(xn[:, 0, :], x[:, nxt2, :], mean_var[:, 0, 0:1], rstd[:, 0:1],
                                            ALU.subtract, ALU.mult), f"xn_{h}")
                    after(act, loads(s_kw, nxt2_at - 1, 48))
                    for m in range(KD):
                        after(act, now(PE, f"k_proj{m}"))
                        if l == 0:
                            ins = act.activation(k_part[0][:, m, :], ps[:, 5 + m, 0:S2], ACT.Copy)
                        else:
                            ins = act.activation(k_part[0][:, m, :], ps[:, 5 + m, 0:S2], ACT.Identity,
                                                 bias=xb_col[:, 1, m:m + 1])
                        AC.do(ins, f"k_hi{m}_{h}")
                    for m in range(KD):
                        after(dve, now(AC, f"k_hi{m}"), was(PL, "k_lo"))
                        if l == 0:
                            ins = dve.tensor_tensor(k_rest[:, m, :], ps[:, 5 + m, 0:S2], k_part[0][:, m, :], ALU.subtract)
                        else:
                            ins = dve.scalar_tensor_tensor(k_rest[:, m, :], ps[:, 5 + m, 0:S2], xb_col[:, 1, m:m + 1],
                                                           k_part[0][:, m, :], ALU.add, ALU.subtract)
                        DV.do(ins, f"k_r{m}_{h}")
                    yield
                    yield
                    after(pe, now(DV, "k_r1"))
                    for k in range(KD):
                        last = pe.transpose(ps[:, 5, k * T:(k + 1) * T], xn[:, 0, k * 128:(k + 1) * 128], ident[0:T, 0:T])
                    PE.do(last, f"xnT_{h}")
                    after(act, now(PE, "xnT"))
                    AC.do(act.activation(xT[:, :, 0:T], ps[:, 5, 0:KD * T].rearrange("p (k t) -> p k t", k=KD), ACT.Copy),
                          f"xT_{h}")
                    after(act, now(DV, "k_r1"))
                    AC.do(act.activation(k_part[1], k_rest, ACT.Copy), f"k_mid_{h}")
                    after(pool, now(AC, "k_mid"))
                    PL.do(pool.tensor_tensor(k_part[2], k_rest, k_part[1], ALU.subtract), f"k_lo_{h}")
                    yield
                    yield
                    after(pe, now(AC, "xT"))
                    for m in range(KD):
                        for k in range(KD):
                            last = pe.matmul(ps[:, 6, m * T:(m + 1) * T], w["q"][:, k, m * 128:(m + 1) * 128], xT[:, k, 0:T],
                                             start=(k == 0), stop=(k == KD - 1))
                    PE.do(last, f"q_proj_{h}")
                    scale = 1.0 / 16 if l == 0 else 0.25
                    after(dve, now(PE, "q_proj"))
                    for m in range(KD):
                        dst, src = q_full[:, m * T:(m + 1) * T], ps[:, 6, m * T:(m + 1) * T]
                        if l == 0:
                            ins = dve.tensor_scalar(dst, src, scale, None, ALU.mult)
                        else:
                            ins = dve.tensor_scalar(dst, src, xb_col[:, 0, m:m + 1], scale, ALU.add, ALU.mult)
                        DV.do(ins, f"q_{h}")
                    after(dve, now(DV, "q"), loads(s_qw, nxt2_at - 1, 48))
                    DV.do(dve.tensor_copy(q_part[0], q_full), f"q_hi_{h}")
                    after(dve, now(DV, "q_hi"))
                    DV.do(dve.tensor_tensor(q_full, q_full, q_part[0], ALU.subtract), f"q_r_{h}")
                    after(dve, now(DV, "q_r"))
                    DV.do(dve.tensor_copy(q_part[1], q_full), f"q_mid_{h}")
                    after(dve, now(DV, "q_mid"))
                    DV.do(dve.tensor_tensor(q_part[2], q_full, q_part[1], ALU.subtract), f"q_lo_{h}")
                    read = [] if nxt2_at < 2 else [loads(s_kst, nxt2_at - 2, 128), loads(s_qst, nxt2_at - 2, 128)]
                    after_sp(now(PL, "k_lo"), *read)
                    for n in range(3):
                        sp.dma_start(k_dram[h, n].rearrange("m p t -> p m t"), k_part[n]).then_inc(s_kw, 16)
                    after_sp(now(DV, "q_lo"))
                    for n in range(3):
                        sp.dma_start(q_dram[h, n].rearrange("m p t -> p m t"),
                                     q_part[n].rearrange("p (m t) -> p m t", m=KD)).then_inc(s_qw, 16)
                    yield

                def values():
                    after(pe, loads(s_ctxv, nxt_at, 16), now(DV, "q"), now(AC, "xT"), *([] if nxt2 is not None else [was(DV, "q")]))
                    for c in range(NC):
                        for k in range(KD):
                            last = pe.matmul(ps[0:CK, 5 + c // 2, (c % 2) * D:(c % 2 + 1) * D], ctxV[:, k, c * CK:(c + 1) * CK],
                                             w["v"][:, k, :], start=(k == 0), stop=(k == KD - 1))
                        PE.do(last, "v_proj_%d" % h if c == NC - 1 else f"v{c}_{h}")
                        if c == 1:
                            yield
                    for c in range(NC):
                        after(dve, now(PE, "v1" if c < 2 else "v_proj"))
                        src = ps[0:CK, 5 + c // 2, (c % 2) * D:(c % 2 + 1) * D].rearrange("p (h d) -> p h d", h=XH)
                        dst = Vx[q][:, c, :, 0:XD]
                        if l == 0:
                            ins = dve.tensor_copy(dst, src)
                        else:
                            ins = dve.tensor_tensor(dst, src, xb_row[1]["v"][0:CK, :].rearrange("p (h d) -> p h d", h=XH),
                                                    ALU.add)
                        DV.do(ins, f"V{c}_{h}")
                    yield

                def masks():
                    after(dve, loads(s_mask, nxt_at, 32))
                    DV.do(dve.tensor_scalar(mask_add[q], raw[0], 0.0, NEG, ALU.is_equal, ALU.mult))
                    DV.do(dve.tensor_scalar(maskT_add[q], raw[1], 0.0, NEG, ALU.is_equal, ALU.mult), f"mask_{h}")

                def maxima():
                    for s in range(XH):
                        bank = 2 + s % 2
                        if s == 0:
                            after(pe, loads(s_kst, nxt_at, 128), loads(s_qst, nxt_at, 128), now(DV, "mask"), was(DV, "max15"))
                        if s >= 2:
                            after(pe, now(DV, f"max{s - 2}"))
                        pe.matmul(ps[0:T, bank, 0:S2], Qst[q][:, s, :], Kst[q][:, s, :], start=True, stop=False)
                        PE.do(pe.matmul(ps[0:T, bank, 0:S2], ident_bf[0:T, 0:T], mask_add[q], start=False, stop=True),
                              f"S{s}_{h}")
                        after(dve, now(PE, f"S{s}"))
                        DV.do(dve.tensor_reduce(nm[:, s:s + 1], ps[0:T, bank, 0:S2], AXX, ALU.max, negate=True),
                              f"max{s}_{h}")
                        yield
                    after(dve, now(DV, "max15"), was(PE, "nmT"))
                    DV.do(dve.tensor_copy(nm_part[:, 0:XH], nm), f"nm1_{h}")
                    after(dve, now(DV, "nm1"))
                    DV.do(dve.tensor_tensor(nm_rest, nm, nm_part[:, 0:XH], ALU.subtract), f"nm2_{h}")
                    after(dve, now(DV, "nm2"))
                    DV.do(dve.tensor_copy(nm_part[:, XH:2 * XH], nm_rest), f"nm3_{h}")
                    after(dve, now(DV, "nm3"))
                    DV.do(dve.tensor_tensor(nm_part[:, 2 * XH:3 * XH], nm_rest, nm_part[:, XH:2 * XH], ALU.subtract), f"nm4_{h}")
                    yield
                    yield
                    yield
                    after(pe, now(DV, "nm4"))
                    nmT_ps = ps[:, 2, 0:T // 2].bitcast(BF16)
                    PE.do(pe.transpose(nmT_ps, nm_part, ident_bf[0:T, 0:T]), f"nmT_{h}")
                    after(dve, now(PE, "nmT"))
                    DV.do(dve.tensor_copy(nmT[q], nmT_ps[0:3 * XH, :]), f"nmTsb_{h}")
                    yield

                def attend():
                    p = h
                    for s in range(XH + LAG):
                        if s < XH:
                            out_ps = ps[0:CK, s % 2, 0:NC * T]
                            if s == 0:
                                after(pe, was(DV, "nmTsb"), was(DV, "V2"))
                            after(pe, now(AC, f"exp{s - 2}") if s >= 2 else was(AC, f"exp{XH - 2 + s}"))
                            for k in range(NC):
                                pe.matmul(out_ps[:, k * T:(k + 1) * T], Kst[p][:, s, k * CK:(k + 1) * CK], Qst[p][:, s, :],
                                          start=(k == 0), stop=False, skip_group_check=True)
                            pe.matmul(out_ps, ident_bf[0:CK, 0:CK], maskT_add[p], start=False, stop=False,
                                      skip_group_check=True)
                            PE.do(pe.matmul(out_ps.rearrange("p (c t) -> p c t", c=NC), sel[:, s, :],
                                            nmT[p].unsqueeze(1).to_broadcast([3 * XH, NC, T]), start=False, stop=True,
                                            skip_group_check=True), f"ST{s}_{h}")
                            after(act, now(PE, f"ST{s}"))
                            after(act, now(PE, f"PV{s - 3}") if s >= 3 else was(PE, f"PV{XH - 3 + s}"))
                            AC.do(act.activation(PTx[s % 3], out_ps, ACT.Exp), f"exp{s}_{h}")
                        if s >= LAG:
                            e = s - LAG
                            after(pe, now(AC, f"exp{e}"))
                            if e == 0:
                                after(pe, now(DV, "oa"))
                            for k in range(NC):
                                last = pe.matmul(ps[32 * (e % 4):32 * (e % 4) + 32, 4, e // 4 * T:(e // 4 + 1) * T],
                                                 Vx[p][:, k, e, :], PTx[e % 3][:, k * T:(k + 1) * T],
                                                 start=(k == 0), stop=(k == NC - 1))
                            PE.do(last, f"PV{e}_{h}")
                        yield

                def finish():
                    after(dve, was(PE, "PV15"), was(PE, "oT"))
                    DV.do(dve.tensor_copy(oa, ps[:, 4, 0:GT]), f"oa_{h}")
                    yield
                    after(pe, now(DV, "oa"), was(DV, "x"))
                    for n in range(4):
                        last = pe.transpose(ps[0:T, 7, n * 128:(n + 1) * 128], oa[:, n * T:(n + 1) * T], ident[:, :])
                    PE.do(last, f"oT_{h}")
                    yield
                    o_ps = ps[0:T, 7, :].rearrange("p (h d) -> p h d", h=XH)
                    after(dve, now(PE, "oT"))
                    DV.do(dve.reciprocal(inv, o_ps[:, :, XD]), f"inv_{h}")
                    after(dve, now(DV, "inv"), was(PE, "onT_ps"))
                    DV.do(dve.tensor_tensor(on.rearrange("p (h d) -> p h d", h=XH), o_ps[:, :, 0:XD],
                                            inv.unsqueeze(2).to_broadcast([T, XH, XD]), ALU.mult), f"on_{h}")
                    DV.do(dve.tensor_tensor(x[:, prev, :], x[:, prev, :], xb_row[l]["o"][0:T, :], ALU.add), f"xb_{h}")
                    after(pe, now(DV, "on"))
                    for k in range(KD):
                        last = pe.transpose(ps[:, 7, k * T:(k + 1) * T], on[:, k * 128:(k + 1) * 128], ident[0:T, 0:T])
                    PE.do(last, f"onT_ps_{h}")
                    after(act, now(PE, "onT_ps"), was(PE, "o_proj"))
                    AC.do(act.activation(onT, ps[:, 7, 0:KD * T], ACT.Copy), f"onT_{h}")
                    yield
                    after(pe, now(AC, "onT"))
                    for k in range(KD):
                        last = pe.matmul(ps[0:T, 7, 0:D], onT[:, k * T:(k + 1) * T], w["o"][:, k, :],
                                         start=(k == 0), stop=(k == KD - 1))
                    PE.do(last, f"o_proj_{h}")
                    after(dve, now(PE, "o_proj"), now(DV, "xb"))
                    DV.do(dve.tensor_tensor(x[:, prev, :], x[:, prev, :], ps[0:T, 7, 0:D], ALU.add), f"x_{h}")
                    yield

                fetch()
                prep = prepare() if nxt2 is not None else iter(())
                vals = values() if nxt is not None else iter(())
                maxs = maxima() if nxt is not None else iter(())
                main = attend() if c is not None else iter(())
                end = finish() if prev is not None else iter(())
                next(end, None)
                if nxt is not None:
                    masks()
                for step, _ in enumerate(main):
                    if next(prep, 0) == 0:
                        next(vals, None)
                    if step >= MAXIMA_FROM:
                        next(maxs, None)
                        next(maxs, None)
                    if step % 3 == 1:
                        next(end, None)
                for rest in (prep, vals, maxs, end):
                    for _ in rest:
                        pass

            everyone()
            if l:
                first_loads()
            after(dve, (s_sel, (l + 1) * 16))
            DV.do(dve.tensor_copy(sel, sel_f.rearrange("p (h t) -> p h t", h=XH)), "sel")
            after(dve, DV.all())
            def halves(which, *of):
                once(f"{name}_{which}", *(lambda h=h, sequences=sequences: half(h, 0, *sequences)
                                          for h, sequences in enumerate(of)))

            halves("start", (None, None, None, 0), (None, None, 0, 1))
            halves("first", (None, 0, 1, 2), (0, 1, 2, 3))
            with loop(name, B // 2 - 2) as i:
                half(0, i, 1, 2, 3, 4)
                half(1, i, 2, 3, 4, 5)
            everyone()
            halves("last", (B - 3, B - 2, B - 1, None), (B - 2, B - 1, None, None))
            halves("end", (B - 1, None, None, None))

        cross_attention(0)

        def experts():
            for eng in (pe, dve):
                after(eng, s_w["moe"])
            gateT = big_a[0:EXPERTS, 0, :]

            def sm(n):
                return small[:, n, :].rearrange("p (g e) -> p g e", g=G)

            def one(n):
                return soft_max[:, n, :]

            def wide(ap):
                return ap.unsqueeze(2).to_broadcast([T, G, EXPERTS])

            xT_next, gate, gate_next = big_b[:, 0:KD, :], sm(7), sm(8)

            def gating(g):
                normalise(g * G, PE.at("ln_T1", 1))
                yield
                yield
                yield
                after(dve, AC.at("taken", 1))
                transpose_xn(xT_next, 0)
                yield
                xn_transposed(pe)
                for j in range(G):
                    for k in range(KD):
                        last = pe.matmul(ps[0:T, 2, j * EXPERTS:(j + 1) * EXPERTS], xT_next[:, k, j * T:(j + 1) * T],
                                         gate_w[:, k, :], start=(k == 0), stop=(k == KD - 1))
                PE.do(last, "logits")
                yield
                after(dve, PE.at("logits"))
                logit, hit, cand, keep1, rest, keep2, ex = (sm(n) for n in range(7))
                top, pick, total = one(0), one(1), one(2)
                rk = rank[:, :].rearrange("p (g e) -> p g e", g=G)

                def chain(ins, name=None):
                    DV.do(ins, name)
                    after(dve, DV.all())

                chain(dve.tensor_tensor(logit, ps[0:T, 2, 0:G * EXPERTS].rearrange("p (g e) -> p g e", g=G),
                                        gate_b[:, :].unsqueeze(1).to_broadcast([T, G, EXPERTS]), ALU.add))
                chain(dve.tensor_reduce(top, logit, AXX, ALU.max))
                chain(dve.tensor_tensor(ex, logit, wide(top), ALU.subtract), "shifted")
                src = logit
                for n, keep in ((0, keep1), (1, keep2)):
                    if n:
                        chain(dve.tensor_reduce(pick, src, AXX, ALU.max))
                    yield
                    chain(dve.tensor_tensor(hit, src, wide(pick if n else top), ALU.is_equal))
                    chain(dve.tensor_tensor(cand, hit, rk, ALU.mult))
                    chain(dve.tensor_reduce(pick, cand, AXX, ALU.max))
                    yield
                    chain(dve.tensor_tensor(keep, cand, wide(pick), ALU.is_equal))
                    if n == 0:
                        chain(dve.scalar_tensor_tensor(rest, keep1, -3.0e38, logit, ALU.mult, ALU.add))
                        src = rest
                chain(dve.tensor_tensor(keep1, keep1, keep2, ALU.add))
                after(act, DV.at("shifted"))
                AC.do(act.activation(ex, ex, ACT.Exp), "ex")
                yield
                after(dve, AC.at("ex"))
                chain(dve.tensor_tensor(ex, ex, keep1, ALU.mult))
                chain(dve.tensor_reduce(total, ex, AXX, ALU.add))
                chain(dve.reciprocal(total, total))
                chain(dve.tensor_tensor(gate_next, ex, wide(total), ALU.mult), "gate")
                yield
                after(pe, DV.at("gate"))
                for j in range(G):
                    last = pe.transpose(ps[0:EXPERTS, 3, j * T:(j + 1) * T], gate_next[:, j, :], ident[0:T, 0:T])
                PE.do(last, "gateT_ps")
                after(act, PE.at("gateT_ps"))
                AC.do(act.activation(gateT, ps[0:EXPERTS, 3, 0:GT], ACT.Copy), "gateT")
                yield
                after(pe, AC.at("gateT"))
                for j in range(G):
                    last = pe.matmul(ps[0:T, j // 2, (j % 2) * D:(j % 2 + 1) * D], gateT[:, j * T:(j + 1) * T],
                                     expert_b[:, :], start=True, stop=True)
                PE.do(last, "bias")
                yield
                after(dve, PE.at("bias"))
                for n in range(G // 2):
                    xs = x[:, bass.ds(g * G + 2 * n, 2), :]
                    DV.do(dve.tensor_tensor(xs, xs, ps[0:T, n, :].rearrange("p (g d) -> p g d", g=2), ALU.add), "x_bias")
                yield

            def take():
                after(act, PE.all(), DV.at("ln_done1"))
                AC.do(act.activation(xT[:, :, :], xT_next, ACT.Copy), "taken")
                after(dve, DV.all())
                DV.do(dve.tensor_copy(gate, gate_next), "gate_taken")

            def mixture(g, gates):
                after(pe, AC.at("taken", 1))
                after(dve, DV.at("gate_taken", 1))
                n = 0
                for j in range(G):
                    for e in range(0, EXPERTS, 2):
                        bank = 4 + n % 4
                        after(pe, DV.at(f"x{n - 4}") if n >= 4 else DV.at(f"x{4 * G - 4 + n}", 1))
                        for k in range(KD):
                            last = pe.matmul(ps[0:T, bank, :], xT[:, k, j * T:(j + 1) * T],
                                             expert_w[:, k, e * D:(e + 2) * D], start=(k == 0), stop=(k == KD - 1))
                        PE.do(last, f"e{n}")
                        after(dve, PE.at(f"e{n}"))
                        for q in range(2):
                            xs = x[:, g * G + j, :]
                            after(dve, DV.all())
                            DV.do(dve.scalar_tensor_tensor(xs, ps[0:T, bank, q * D:(q + 1) * D],
                                                           gate[:, j, e + q:e + q + 1], xs, ALU.mult, ALU.add), f"x{n}")
                        next(gates, None)
                        n += 1
                for _ in gates:
                    pass

            def first():
                for _ in gating(0):
                    pass
                take()

            once("moe_first", first)
            with loop("moe", NG - 1) as g:
                mixture(g, gating(g + 1))
                take()
            everyone()
            once("moe_last", lambda: mixture(NG - 1, iter(())))

        experts()

        def self_attention():
            after(pe, s_w["attn"])
            qk = big_b
            v = big_a[0:T, 0:3, :].rearrange("p a b -> p (a b)")[:, 0:G * D].rearrange("p (g d) -> p g d", g=G)
            PTs = big_a[0:T, 4, :]

            def projections(g, more=True):
                transpose_xn(xT, 6, ago=1)
                yield
                xn_transposed(pe)
                for n in range(2 * KD):
                    for k in range(KD):
                        last = pe.matmul(ps[:, 2 + n, 0:GT], attn_w[:, k, n * 128:(n + 1) * 128], xT[:, k, :],
                                         start=(k == 0), stop=(k == KD - 1))
                    PE.do(last, f"qk{n}")
                yield
                if more:
                    normalise(g * G + G, PE.at("ln_T1"))
                for n in range(2 * KD):
                    if n < KD:
                        after(act, PE.at(f"qk{n}"))
                        AC.do(act.activation(qk[:, n, :], ps[:, 2 + n, 0:GT], ACT.Copy, scale=1.0 / 16), "q")
                    else:
                        after(dve, PE.at(f"qk{n}"))
                        DV.do(dve.tensor_copy(qk[:, n, :], ps[:, 2 + n, 0:GT]), "k")
                yield
                for j in range(G):
                    for k in range(KD):
                        last = pe.matmul(ps[0:T, 6 + j // 2, (j % 2) * D:(j % 2 + 1) * D], xT[:, k, j * T:(j + 1) * T],
                                         attn_w[:, k, 2 * D:3 * D], start=(k == 0), stop=(k == KD - 1))
                PE.do(last, "v_ps")
                yield
                after(act, PE.all())
                for n in range(G // 2):
                    AC.do(act.activation(v[:, 2 * n:2 * n + 2, :], ps[0:T, 6 + n, :].rearrange("p (g d) -> p g d", g=2),
                                         ACT.Copy), "v")

            def attention(g, nxt):
                next(nxt, None)
                after(pe, AC.at("q", 1), DV.at("k", 1), DV.at("x", 1))
                for j in range(G):
                    c = slice(j * T, (j + 1) * T)
                    for k in range(KD):
                        last = pe.matmul(ps[0:T, 0, c], qk[:, k, c], qk[:, KD + k, c], start=(k == 0), stop=(k == KD - 1))
                PE.do(last, "S")
                after(dve, PE.at("S"), DV.at("x", 1))
                mx, tot = soft_max[:, 0, :], soft_max[:, 1, :]
                DV.do(dve.tensor_tensor(soft[:, :, :], p3(ps[0:T, 0, 0:GT]),
                                        causal_neg[:, :].unsqueeze(1).to_broadcast([T, G, T]), ALU.add), "masked")
                after(dve, DV.at("masked"))
                DV.do(dve.tensor_reduce(mx, soft[:, :, :], AXX, ALU.max), "max")
                after(dve, DV.at("max"))
                DV.do(dve.tensor_tensor(soft[:, :, :], soft[:, :, :], mx.unsqueeze(2).to_broadcast([T, G, T]),
                                        ALU.subtract), "shifted")
                after(act, DV.at("shifted"))
                AC.do(act.activation(soft[:, :, :], soft[:, :, :], ACT.Exp), "P")
                next(nxt, None)
                after(dve, AC.at("P"))
                DV.do(dve.tensor_reduce(tot, soft[:, :, :], AXX, ALU.add), "tot")
                after(dve, DV.at("tot"))
                DV.do(dve.reciprocal(tot, tot), "inv")
                next(nxt, None)
                after(pe, AC.at("P"), DV.at("x", 1))
                for j in range(G):
                    last = pe.transpose(ps[0:T, 1, j * T:(j + 1) * T], soft[:, j, :], ident[0:T, 0:T])
                PE.do(last, "PT_ps")
                after(act, PE.at("PT_ps"))
                AC.do(act.activation(PTs, ps[0:T, 1, 0:GT], ACT.Copy), "PT")
                next(nxt, None)
                after(pe, AC.at("PT"), AC.at("v", 1), DV.at("masked"))
                for j in range(G):
                    last = pe.matmul(ps[0:T, j // 2, (j % 2) * D:(j % 2 + 1) * D], PTs[:, j * T:(j + 1) * T],
                                     v[:, j, :], start=True, stop=True)
                PE.do(last, "PV")
                for _ in nxt:
                    pass
                after(dve, PE.at("PV"), DV.at("inv"))
                for j in range(G):
                    xs = x[:, g * G + j, :]
                    DV.do(dve.scalar_tensor_tensor(xs, ps[0:T, j // 2, (j % 2) * D:(j % 2 + 1) * D],
                                                   tot[:, j:j + 1], xs, ALU.mult, ALU.add), "x")

            def first():
                for _ in projections(0):
                    pass

            once("attn_norm", lambda: normalise(0))
            once("attn_first", first)
            with loop("attn", NG - 2) as g:
                attention(g, projections(g + 1))
            everyone()
            once("attn_last", lambda: attention(NG - 2, projections(NG - 1, more=False)))
            once("attn_end", lambda: attention(NG - 1, iter(())))

        self_attention()
        cross_attention(1)

        def feed_forward():
            for n in range(2):
                sp.dma_start(hw[n][:, :, :], a[f"h{n + 1}"]).then_inc(s_hw, 16)
            for eng in (pe, act, dve):
                after(eng, s_w["ffn"])

            def network(g, with_next):
                for m in range(HT):
                    for n in range(2):
                        if m >= 2:
                            after(pe, DV.at(f"h0_{m - 2}"))
                        elif n:
                            after(pe, DV.at("y", 1))
                        if m == n == 0:
                            after(pe, DV.at("ln_done1", 1))
                        for k in range(KD):
                            last = pe.matmul(ps[:, 2 + 2 * n + m % 2, 0:GT], w12[:, n, k, m * 128:(m + 1) * 128], xT[:, k, :],
                                             start=(k == 0), stop=(k == KD - 1))
                        PE.do(last, f"w{n}_{m}")
                    after(act, PE.at(f"w0_{m}"))
                    if m >= 2:
                        after(act, DV.at(f"h0_{m - 2}"))
                    AC.do(act.activation(silu[:, m % 2, :], ps[:, 2 + m % 2, 0:GT], ACT.Silu, scale=hid_s[:, 0, m:m + 1]),
                          f"silu{m}")
                    after(dve, AC.at(f"silu{m}"), PE.at(f"w1_{m}"))
                    DV.do(dve.scalar_tensor_tensor(big_a[:, m, :], ps[:, 4 + m % 2, 0:GT], hid_s[:, 1, m:m + 1],
                                                   silu[:, m % 2, :], ALU.mult, ALU.mult), f"h0_{m}")
                for n, (src, dst) in enumerate(((big_a, big_b), (big_b, big_a))):
                    for m in range(HT):
                        if n == 0 and m in (0, 2):
                            after(pe, DV.at(f"h0_{HT - 1}"))
                        if m == 0:
                            after(pe, (s_hw, 32))
                        if m >= 4:
                            after(pe, AC.at(f"g{n}_{m - 4}"))
                        elif n == 1:
                            after(pe, AC.at(f"g0_{HT - 1}"))
                        for k in range(HT):
                            last = pe.matmul(ps[:, m % 4, 0:GT], hw[n][:, k, m * 128:(m + 1) * 128], src[:, k, :],
                                             start=(k == 0), stop=(k == HT - 1))
                        PE.do(last, f"h{n + 1}_{m}")
                        after(act, PE.at(f"h{n + 1}_{m}"))
                        AC.do(act.activation(dst[:, m, :], ps[:, m % 4, 0:GT], ACT.Gelu, scale=hid_s[:, 2 + n, m:m + 1]),
                              f"g{n}_{m}")
                        if with_next and n == 0 and m == 1:
                            normalise(g * G + G)
                        if with_next and n == 0 and m == HT - 1:
                            transpose_xn(xT, 6, "dd")
                after(pe, AC.at(f"g1_{HT - 1}"))
                for j in range(G):
                    for k in range(HT):
                        last = pe.matmul(ps[0:T, 4 + j // 2, (j % 2) * D:(j % 2 + 1) * D], big_a[:, k, j * T:(j + 1) * T],
                                         w3[:, k, :], start=(k == 0), stop=(k == HT - 1))
                PE.do(last, "y_ps")
                y = xn
                after(dve, PE.at("y_ps"))
                for n in range(G // 2):
                    DV.do(dve.tensor_tensor(y[:, 2 * n:2 * n + 2, :], ps[0:T, 4 + n, :].rearrange("p (g d) -> p g d", g=2),
                                            w3_s[:, :].unsqueeze(1).to_broadcast([T, 2, D]), ALU.mult), "y")
                after(dve, DV.at("y"))
                xs = x[:, bass.ds(g * G, G), :]
                DV.do(dve.tensor_tensor(xs, xs, y[:, :, :], ALU.add), "x")
                after_sp(DV.at("x"))
                sp.dma_start(out[g].rearrange("b t d -> t b d"), xs).then_inc(s_out, 16)

            def first():
                normalise(0)
                transpose_xn(xT, 6, "dd")

            once("ffn_first", first)
            with loop("ffn", NG - 1) as g:
                network(g, True)
            everyone()
            once("ffn_last", lambda: network(NG - 1, False))

        feed_forward()
        after_sp(*s_w.values(), (s_out, 16 * NG))


def lay_out(i):
    def c(v):
        return np.ascontiguousarray(v)

    def rows_of(w):
        return c(w.reshape(-1, 128, w.shape[-1]).transpose(1, 0, 2))

    def wide(v, n):
        return c(np.broadcast_to(v, (n, v.shape[-1])))

    def cols_of(v):
        return c(v.reshape(-1, 128).T)

    f = np.float32
    t = np.arange(T)
    a = {"x": i["x"]}
    a["ctxT"] = c(i["ctx_1024"].transpose(0, 2, 1).reshape(B, KD, 128, S2).transpose(0, 2, 1, 3))
    a["mask0"] = c(i["mask_Bx1xSxS2_if1"][:, 0])
    a["maskT0"] = c(i["mask_Bx1xSxS2_if1"][:, 0].transpose(0, 2, 1).reshape(B, NC, CK, T).transpose(0, 2, 1, 3))
    a["maskT1"] = c(i["mask_Bx1xSxS2_bk0"][:, 0].transpose(0, 2, 1).reshape(B, NC, CK, T).transpose(0, 2, 1, 3))
    sel = np.zeros((3, XH, XH, CK), f)
    sel[:, np.arange(XH), np.arange(XH)] = 1
    a["sel"] = sel.reshape(3 * XH, XH * CK)
    a["mask1"] = c(i["mask_Bx1xSxS2_bk0"][:, 0])
    a["ident"] = np.eye(128, dtype=f)
    a["before"] = (t[None, :] < t[:, None]).astype(f)
    a["upto"] = (t[:, None] <= t[None, :]).astype(f)
    a["minus_strict"] = np.where(t[:, None] < t[None, :], f(-1), f(0))
    a["causal_neg"] = np.where(t[None, :] > t[:, None], f(NEG), f(0))
    a["rank"] = wide(np.tile(EXPERTS - np.arange(EXPERTS), G).astype(f), T)
    qkvz = np.concatenate([i["L0_attn_qkv_w"], i["L0_attn_z_w"]], 0)
    w = qkvz.reshape(4, HEADS, 128, KD, 128).transpose(1, 4, 0, 3, 2).reshape(HEADS, 128, HWID)
    taps = i["L0_attn_conv_w"].reshape(3, HEADS, 128, TAPS).transpose(1, 2, 0, 3).reshape(HEADS, 128, 3 * TAPS)
    a["head_w"] = c(np.concatenate([w, taps], -1)[[*range(HEADS), 0]])
    a["ba_w"] = rows_of(c(np.concatenate([i["L0_attn_b_w"], i["L0_attn_a_w"]], 0).T))
    a["dt_bias"] = wide(i["L0_attn_dt_bias"], T)
    a["A_log"] = wide(i["L0_attn_A_log"], T)
    a["norm_w"] = c(i["L0_attn_norm_w"].reshape(128, 1))
    a["gdn_out_w"] = c(rows_of(c(i["L0_attn_out_w"].T))[:, [0, *range(HEADS)]])
    for n in "qkvo":
        a[f"x0_W{n}"] = rows_of(c(i[f"L0_xattn_W{n}"].T))
        a[f"x1_W{n}"] = rows_of(i[f"L1_xattn_W{n}"])
    a["x0_bo"] = wide(i["L0_xattn_bo"], 128)
    a["x1_bo"] = wide(i["L1_xattn_bo"], 128)
    a["x1_bv"] = wide(i["L1_xattn_bv"], 128)
    a["x1_bqk"] = c(np.stack([cols_of(i["L1_xattn_bq"]), cols_of(i["L1_xattn_bk"])], 1))
    a["gate_w"] = rows_of(c(i["L0_ffn_gate_w"].T))
    a["gate_b"] = wide(i["L0_ffn_gate_b"], T)
    a["expert_w"] = rows_of(c(i["L0_ffn_expert_w"].transpose(1, 0, 2).reshape(D, EXPERTS * D)))
    a["expert_b"] = i["L0_ffn_expert_b"]
    a["attn_w"] = rows_of(np.concatenate([i["L1_attn_Wq"], i["L1_attn_Wk"], i["L1_attn_Wv"]], 1))
    a["w12"] = c(np.stack([rows_of(c(i["L1_ffn_w1_w"].T)), rows_of(c(i["L1_ffn_w2_w"].T))], 1))
    a["h1"] = rows_of(c(i["L1_ffn_h1_w"].T))
    a["h2"] = rows_of(c(i["L1_ffn_h2_w"].T))
    a["w3"] = rows_of(c(i["L1_ffn_w3_w"].T))
    a["hid_s"] = c(np.stack([cols_of(i[f"L1_ffn_{n}_s"]) for n in ("w1", "w2", "h1", "h2")], 1))
    a["w3_s"] = wide(i["L1_ffn_w3_s"], T)
    return {n: c(v) for n, v in a.items()}


def build(nc, shapes, plan):
    a = {n: nc.dram_tensor(f"in_{n}", s, mybir.dt.from_np(d), kind="ExternalInput").ap() for n, (s, d) in shapes.items()}
    out = nc.dram_tensor("out", (NG, G, T, D), F32, kind="ExternalOutput").ap()
    decoder(nc, a, out, plan)


def kernel(**inputs):
    import concourse.bacc as bacc
    from concourse.bass_utils import run_bass_kernel_spmd

    arrays = lay_out({n: np.asarray(v) for n, v in inputs.items()})
    shapes = {n: (v.shape, v.dtype) for n, v in arrays.items()}
    plan = {}
    build(bacc.Bacc("TRN2", target_bir_lowering=False, num_devices=1), shapes, plan)
    nc = bacc.Bacc("TRN2", target_bir_lowering=False, num_devices=1)
    build(nc, shapes, plan)
    r = run_bass_kernel_spmd(nc, [{f"in_{n}": v for n, v in arrays.items()}], core_ids=[0])
    return r.results[0]["out"].reshape(B, T, D)
```
